# Optimizing a Trainium2 kernel written in Bass

```python
import numpy as np
import jax
import jax.numpy as jnp

def _softmax(x, axis=-1):
    return jax.nn.softmax(x, axis=axis)

def _gelu(x):
    return jax.nn.gelu(x, approximate=True)

def _silu(x):
    return jax.nn.silu(x)

def _sigmoid(x):
    return jax.nn.sigmoid(x)

def _layernorm(x, axis=-1, eps=1e-05):
    m = jnp.mean(x, axis=axis, keepdims=True)
    v = jnp.var(x, axis=axis, keepdims=True)
    return (x - m) / jnp.sqrt(v + eps)

def _scatter_add(tgt, idx, src, axis=0):
    return tgt.at[idx].add(src)

def _segment_sum(src, seg, n):
    return jax.ops.segment_sum(src, seg, n)
kernel_name = 'mk_gnn_ffn_d1_gnn_r8_c5cccf'

def setup_inputs(seed: int=0):
    np.random.seed(seed)
    _w = jnp.asarray

    def _rec_inputs():
        import jax
        import jax.numpy as jnp
        _gk = jax.random.key(seed)
        x = 0.0002542 + 0.9999 * jax.random.normal(jax.random.fold_in(_gk, 1), (6250, 256), jnp.float32)
        src = jax.random.randint(jax.random.fold_in(_gk, 2), (100000,), 0, 6250, jnp.int32)
        dst = jnp.minimum((6250 * jax.random.uniform(jax.random.fold_in(_gk, 3), (100000,)) ** 2.0).astype(jnp.int32), 49999)
        _o = jnp.argsort(dst, stable=True)
        src = src[_o]
        dst = dst[_o]
        return (x, src, dst)
    x, src, dst = _rec_inputs()

    def _L0_gnn_setup():
        import jax, jax.numpy as jnp
        import numpy as np
        N_NODES = 6250

        def _gcn_layer(src, dst, h, W, b):
            ones = jnp.ones(src.shape[0], dtype=h.dtype)
            deg_out = jnp.clip(jax.ops.segment_sum(ones, src, num_segments=N_NODES), 1.0)
            deg_in = jnp.clip(jax.ops.segment_sum(ones, dst, num_segments=N_NODES), 1.0)
            h = h * (deg_out ** (-0.5))[:, None]
            msg = h[src]
            agg = jax.ops.segment_sum(msg, dst, num_segments=N_NODES)
            agg = agg * (deg_in ** (-0.5))[:, None]
            return agg @ W + b
        key = jax.random.key(seed)
        k = jax.random.split(key, 7)
        E = 200000
        in_dim, hid_dim, out_dim = (256, 256, 256)
        src = jax.random.randint(k[0], (E,), 0, N_NODES)
        dst = jax.random.randint(k[1], (E,), 0, N_NODES)
        emb = jax.random.normal(k[2], (N_NODES, in_dim), dtype=jnp.float32)
        W1 = jax.random.normal(k[3], (in_dim, hid_dim), dtype=jnp.float32) * (1.0 / np.sqrt(in_dim))
        b1 = jnp.zeros((hid_dim,), dtype=jnp.float32)
        W2 = jax.random.normal(k[4], (hid_dim, out_dim), dtype=jnp.float32) * (1.0 / np.sqrt(hid_dim))
        b2 = jnp.zeros((out_dim,), dtype=jnp.float32)
        return {'src': src, 'dst': dst, 'emb': emb, 'W1': W1, 'b1': b1, 'W2': W2, 'b2': b2}
    _L0_gnn_all = _L0_gnn_setup()
    _L0_gnn_in = {k: v for k, v in _L0_gnn_all.items() if k in ('W1', 'b1', 'W2', 'b2')}
    del _L0_gnn_all

    def _L0_ffn_setup():
        import jax, jax.numpy as jnp
        import numpy as np
        B, N, D = (16, 512, 256)
        NUM_EXPERTS, TOP_K, HEADS = (4, 2, 4)
        N_EDGES = 131072
        LN_EPS = 1e-05

        def _layernorm(x, g, b):
            mu = x.mean(-1, keepdims=True)
            var = ((x - mu) ** 2).mean(-1, keepdims=True)
            return (x - mu) * jax.lax.rsqrt(var + LN_EPS) * g + b

        def _forward(x, edge_index, W_gat, att_src, att_dst, b_gat, ln_gamma, ln_beta, W1, b1, W2, b2):
            Bc, Nc, Dc = x.shape
            M = Bc * Nc
            x_flat = x.reshape(M, Dc)
            h = (x_flat @ W_gat).reshape(M, HEADS, NUM_EXPERTS)
            loops = jnp.arange(M, dtype=edge_index.dtype)
            src = jnp.concatenate([edge_index[0], loops])
            dst = jnp.concatenate([edge_index[1], loops])
            a_src = (h * att_src).sum(-1)
            a_dst = (h * att_dst).sum(-1)
            e = jax.nn.leaky_relu(a_src[src] + a_dst[dst], negative_slope=0.2)
            e_max = jax.ops.segment_max(e, dst, num_segments=M)
            ee = jnp.exp(e - e_max[dst])
            denom = jax.ops.segment_sum(ee, dst, num_segments=M)
            alpha = ee / (denom[dst] + 1e-16)
            msg = h[src] * alpha[:, :, None]
            agg = jax.ops.segment_sum(msg, dst, num_segments=M).reshape(M, HEADS * NUM_EXPERTS) + b_gat
            scores = _layernorm(agg, ln_gamma, ln_beta).reshape(M, HEADS, NUM_EXPERTS).mean(1)
            scores = scores.reshape(Bc, Nc, NUM_EXPERTS)
            topk_s, topk_i = jax.lax.top_k(scores, TOP_K)
            w = jax.nn.softmax(topk_s, axis=-1)
            out = jnp.zeros_like(x)
            for ei in range(NUM_EXPERTS):
                g = jnp.where(topk_i == ei, w, 0.0).sum(-1)
                hh = jax.nn.gelu(x @ W1[ei] + b1[ei], approximate=False)
                out = out + g[..., None] * (hh @ W2[ei] + b2[ei])
            return out
        key = jax.random.key(seed)
        ks = jax.random.split(key, 8)
        s = 0.05
        return {'x': jax.random.normal(ks[0], (B, N, D), jnp.float32), 'W_gat': jax.random.normal(ks[1], (D, HEADS * NUM_EXPERTS), jnp.float32) * s, 'att_src': jax.random.normal(ks[2], (HEADS, NUM_EXPERTS), jnp.float32) * s, 'att_dst': jax.random.normal(ks[3], (HEADS, NUM_EXPERTS), jnp.float32) * s, 'b_gat': jnp.zeros((HEADS * NUM_EXPERTS,), jnp.float32), 'ln_gamma': jnp.ones((HEADS * NUM_EXPERTS,), jnp.float32), 'ln_beta': jnp.zeros((HEADS * NUM_EXPERTS,), jnp.float32), 'W1': jax.random.normal(ks[4], (NUM_EXPERTS, D, 2 * D), jnp.float32) * s, 'b1': jnp.zeros((NUM_EXPERTS, 2 * D), jnp.float32), 'W2': jax.random.normal(ks[5], (NUM_EXPERTS, 2 * D, D), jnp.float32) * s, 'b2': jnp.zeros((NUM_EXPERTS, D), jnp.float32), 'edge_index': jax.random.randint(ks[6], (2, N_EDGES), 0, B * N, jnp.int32)}
    _L0_ffn_all = _L0_ffn_setup()
    _L0_ffn_in = {k: v for k, v in _L0_ffn_all.items() if k in ('W_gat', 'att_src', 'att_dst', 'b_gat', 'ln_gamma', 'ln_beta', 'W1', 'b1', 'W2', 'b2', 'edge_index')}
    del _L0_ffn_all
    return {'x': x, 'src': src, 'dst': dst, 'L0_gnn_W1': _L0_gnn_in['W1'], 'L0_gnn_b1': _L0_gnn_in['b1'], 'L0_gnn_W2': _L0_gnn_in['W2'], 'L0_gnn_b2': _L0_gnn_in['b2'], 'L0_ffn_W_gat': _L0_ffn_in['W_gat'], 'L0_ffn_att_src': _L0_ffn_in['att_src'], 'L0_ffn_att_dst': _L0_ffn_in['att_dst'], 'L0_ffn_b_gat': _L0_ffn_in['b_gat'], 'L0_ffn_ln_gamma': _L0_ffn_in['ln_gamma'], 'L0_ffn_ln_beta': _L0_ffn_in['ln_beta'], 'L0_ffn_W1': _L0_ffn_in['W1'], 'L0_ffn_b1': _L0_ffn_in['b1'], 'L0_ffn_W2': _L0_ffn_in['W2'], 'L0_ffn_b2': _L0_ffn_in['b2'], 'L0_ffn_edge_index': _L0_ffn_in['edge_index']}

def reference(x, src, dst, L0_gnn_W1, L0_gnn_b1, L0_gnn_W2, L0_gnn_b2, L0_ffn_W_gat, L0_ffn_att_src, L0_ffn_att_dst, L0_ffn_b_gat, L0_ffn_ln_gamma, L0_ffn_ln_beta, L0_ffn_W1, L0_ffn_b1, L0_ffn_W2, L0_ffn_b2, L0_ffn_edge_index):
    import jax
    import jax.numpy as jnp

    def _L0_gnn_ref(src, dst, emb, W1, b1, W2, b2):
        import jax, jax.numpy as jnp
        import numpy as np
        N_NODES = 6250

        def _gcn_layer(src, dst, h, W, b):
            ones = jnp.ones(src.shape[0], dtype=h.dtype)
            deg_out = jnp.clip(jax.ops.segment_sum(ones, src, num_segments=N_NODES), 1.0)
            deg_in = jnp.clip(jax.ops.segment_sum(ones, dst, num_segments=N_NODES), 1.0)
            h = h * (deg_out ** (-0.5))[:, None]
            msg = h[src]
            agg = jax.ops.segment_sum(msg, dst, num_segments=N_NODES)
            agg = agg * (deg_in ** (-0.5))[:, None]
            return agg @ W + b
        h = _gcn_layer(src, dst, emb, W1, b1)
        h = jax.nn.relu(h)
        h = _gcn_layer(src, dst, h, W2, b2)
        return h

    def _L0_ffn_ref(x, W_gat, att_src, att_dst, b_gat, ln_gamma, ln_beta, W1, b1, W2, b2, edge_index):
        import jax, jax.numpy as jnp
        import numpy as np
        B, N, D = (16, 512, 256)
        NUM_EXPERTS, TOP_K, HEADS = (4, 2, 4)
        N_EDGES = 131072
        LN_EPS = 1e-05

        def _layernorm(x, g, b):
            mu = x.mean(-1, keepdims=True)
            var = ((x - mu) ** 2).mean(-1, keepdims=True)
            return (x - mu) * jax.lax.rsqrt(var + LN_EPS) * g + b

        def _forward(x, edge_index, W_gat, att_src, att_dst, b_gat, ln_gamma, ln_beta, W1, b1, W2, b2):
            Bc, Nc, Dc = x.shape
            M = Bc * Nc
            x_flat = x.reshape(M, Dc)
            h = (x_flat @ W_gat).reshape(M, HEADS, NUM_EXPERTS)
            loops = jnp.arange(M, dtype=edge_index.dtype)
            src = jnp.concatenate([edge_index[0], loops])
            dst = jnp.concatenate([edge_index[1], loops])
            a_src = (h * att_src).sum(-1)
            a_dst = (h * att_dst).sum(-1)
            e = jax.nn.leaky_relu(a_src[src] + a_dst[dst], negative_slope=0.2)
            e_max = jax.ops.segment_max(e, dst, num_segments=M)
            ee = jnp.exp(e - e_max[dst])
            denom = jax.ops.segment_sum(ee, dst, num_segments=M)
            alpha = ee / (denom[dst] + 1e-16)
            msg = h[src] * alpha[:, :, None]
            agg = jax.ops.segment_sum(msg, dst, num_segments=M).reshape(M, HEADS * NUM_EXPERTS) + b_gat
            scores = _layernorm(agg, ln_gamma, ln_beta).reshape(M, HEADS, NUM_EXPERTS).mean(1)
            scores = scores.reshape(Bc, Nc, NUM_EXPERTS)
            topk_s, topk_i = jax.lax.top_k(scores, TOP_K)
            w = jax.nn.softmax(topk_s, axis=-1)
            out = jnp.zeros_like(x)
            for ei in range(NUM_EXPERTS):
                g = jnp.where(topk_i == ei, w, 0.0).sum(-1)
                hh = jax.nn.gelu(x @ W1[ei] + b1[ei], approximate=False)
                out = out + g[..., None] * (hh @ W2[ei] + b2[ei])
            return out
        return _forward(x, edge_index, W_gat, att_src, att_dst, b_gat, ln_gamma, ln_beta, W1, b1, W2, b2)
    x = x + _L0_gnn_ref(src, dst, _layernorm(x, axis=-1), L0_gnn_W1, L0_gnn_b1, L0_gnn_W2, L0_gnn_b2)
    x = x + _L0_ffn_ref(_layernorm(x, axis=-1)[None], L0_ffn_W_gat, L0_ffn_att_src, L0_ffn_att_dst, L0_ffn_b_gat, L0_ffn_ln_gamma, L0_ffn_ln_beta, L0_ffn_W1, L0_ffn_b1, L0_ffn_W2, L0_ffn_b2, L0_ffn_edge_index)[0]
    return x

_drawn_inputs = setup_inputs


def setup_inputs(seed=0):
    import zlib

    import numpy as np

    out = dict(_drawn_inputs(seed))
    spreads = {'L0_gnn_b1': (0.0, 0.1),
     'L0_gnn_b2': (0.0, 0.1),
     'L0_ffn_b_gat': (0.0, 0.1),
     'L0_ffn_ln_gamma': (1.0, 0.2),
     'L0_ffn_ln_beta': (0.0, 0.1),
     'L0_ffn_b1': (0.0, 0.1),
     'L0_ffn_b2': (0.0, 0.1)}
    factors = {'L0_ffn_att_dst': 7.678}
    for name, (base, spread) in spreads.items():
        noise = np.random.default_rng([zlib.crc32(name.encode()), seed]).standard_normal(out[name].shape)
        drawn = base * np.exp(spread * noise) if base else spread * noise
        out[name] = jnp.asarray(drawn.astype(out[name].dtype))
    for name, factor in factors.items():
        out[name] = (out[name] * factor).astype(out[name].dtype)
    return out
```

```python
import concourse.bass as bass
from concourse import mybir
from contextlib import ExitStack

F32, BF16, I32 = mybir.dt.float32, mybir.dt.bfloat16, mybir.dt.int32
ALU = mybir.AluOpType
ACT = mybir.ActivationFunctionType
AX = mybir.AxisListType.X
RMAX = bass.bass_isa.ReduceOp.max

P = 128
N = 6250
D = 256
DC = D // P
NT = (N + P - 1) // P
NFULL = N // P
NREST = N - NFULL * P

E = 100000
ET = (E + P - 1) // P
EFULL = E // P
EREST = E - EFULL * P
GT = 4
SETS = 4
NG = -(-ET // GT)
NG += -NG % SETS
NGP = NG + 1
HT = 8
WIN = P
AGGC = N + WIN + (-(N + WIN)) % P

EF = 131072
FT = EF // P
HEADS, NE = 4, 4
HE = HEADS * NE
HID = 512
FC = HID // P
VAL = HE + HEADS
LO = 256
HI = -(-N // LO)
CV = 5
NC = VAL // CV
BT = 4
FIT = SETS * BT
EPS = 1e-5
NEG = -1.0e30


def program(nc, x, src, src_rest, dst, dst_rest, w1, b1, w2, b2, w_gat, att_src, att_dst, b_gat,
            ln_gamma, ln_beta, ew1, eb1, ew2, eb2, esrc, edst, out):
    table1 = nc.dram_tensor("table1", (NT * P, D), F32).ap()
    table2 = nc.dram_tensor("table2", (NT * P, D), F32).ap()
    node_tab = nc.dram_tensor("node_tab", (NT * P, VAL), F32).ap()
    dest_tab = nc.dram_tensor("dest_tab", (NT * P, 2 * HEADS), F32).ap()
    x1_dram = nc.dram_tensor("x1_dram", (NT, P, D), F32).ap()
    y_dram = nc.dram_tensor("y_dram", (NT, P, NE * D), F32).ap()

    with ExitStack() as top:
        def sb(name, shape, dt=F32, ctx=top):
            return ctx.enter_context(nc.sbuf_tensor(name, shape, dt))

        ident = sb("ident", [P, P])
        iota = sb("iota", [P, LO])
        erow_i = sb("erow_i", [P, 2, FT], I32)
        edst_hi = sb("edst_hi", [P, FT])
        edst_lo = sb("edst_lo", [P, FT])
        agg = sb("agg", [P, DC, AGGC])
        node = dict(as_=sb("as_", [P, NT, HEADS]), ad=sb("ad", [P, NT, 2, HEADS]),
                    h=sb("h", [P, NT, HE]), e_self=sb("e_self", [P, NT, HEADS]))
        with ExitStack() as nodes:
            x_sb = sb("x_sb", [P, NT, D], F32, nodes)
            with ExitStack() as gnn:
                def gb(name, shape, dt=F32):
                    return sb(name, shape, dt, gnn)
                g = dict(
                    nc=nc, x=x, x_sb=x_sb, ident=ident, iota=iota, table1=table1, table2=table2, agg=agg,
                    src_f=gb("src_f", [P, NG * GT]),
                    dst_i=gb("dst_i", [P, NG * GT], I32),
                    dst_left=gb("dst_left", [P, NG * GT]),
                    rel=gb("rel", [P, NGP * GT]),
                    dst_hi=gb("dst_hi", [P, NGP * GT]),
                    dst_lo=gb("dst_lo", [P, NGP * GT]),
                    iota_bf=gb("iota_bf", [P, P], BF16),
                    tile_base=gb("tile_base", [P, NT]),
                    left_i=gb("left_i", [P, 1], I32),
                    rs_out=gb("rs_out", [P, NT]),
                    rs_in=gb("rs_in", [P, NT]),
                    w=[gb("w_1", [P, DC, D]), gb("w_2", [P, DC, D])],
                    b=[gb("b_1", [P, D]), gb("b_2", [P, D])],
                    erow_i=erow_i, edst_hi=edst_hi, edst_lo=edst_lo,
                )
                prologue(g, src, src_rest, dst, dst_rest, (w1, w2), (b1, b2), esrc, edst)
                aggregate(g, 1)
                transform(g, 1)
                aggregate(g, 2)
                transform(g, 2)
            gat_nodes(nc, x_sb, agg, node, ident, node_tab, dest_tab, x1_dram, w_gat, att_src, att_dst)
        gat_edges(nc, agg, node, ident, iota, erow_i, edst_hi, edst_lo, node_tab, dest_tab, y_dram, x1_dram,
                  b_gat, ln_gamma, ln_beta, ew1, eb1, ew2, eb2, out)


class Chain:

    def __init__(self, eng, sem):
        self.eng, self.sem, self.n = eng, sem, 0

    def __call__(self, ins):
        self.n += 1
        ins.then_inc(self.sem, 1)
        self.eng.wait_ge(self.sem, self.n)


def prologue(g, src, src_rest, dst, dst_rest, ws, bs, esrc, edst):
    nc, x_sb, iota, ident = g["nc"], g["x_sb"], g["iota"], g["ident"]
    src_f, dst_i, rel, dst_left = g["src_f"], g["dst_i"], g["rel"], g["dst_left"]
    with ExitStack() as c:
        def sb(name, shape, dt=F32):
            return c.enter_context(nc.sbuf_tensor(name, shape, dt))
        def sem(name):
            return c.enter_context(nc.semaphore(name))
        src_i = sb("src_i", [P, NG * GT], I32)
        key_i = sb("key_i", [P, FT], I32)
        src_hi = sb("src_hi", [P, NG * GT])
        src_lo = sb("src_lo", [P, NG * GT])
        tmp = sb("tmp_f", [P, NG * GT])
        far = sb("far", [P, NG * GT])
        far_max = sb("far_max", [P, 2])
        ones = sb("ones", [1, P])
        row_f = sb("row_f", [1, NG])
        oh_lo = sb("oh_lo", [P, 2, HT, P], BF16)
        oh_hi = sb("oh_hi", [P, 2, HT, NT], BF16)
        zero = sb("zero", [P, P], BF16)
        stats = sb("stats", [P, NT, 6])
        mv = sb("mv", [P, NT, 2])
        scale = sb("scale", [P, NT])
        std = sb("std", [P, NT])
        xn = sb("xn", [P, 4, D])
        ps_deg = c.enter_context(nc.psum_tensor("ps_deg", [P, 512], F32))
        ps_win = c.enter_context(nc.psum_tensor("ps_win", [P, 512], F32))
        s_fill = sem("s_fill")
        s_edges = sem("s_edges")
        s_fedges = sem("s_fedges")
        s_x = sem("s_x")
        s_w = sem("s_w")
        s_iota = sem("s_iota")
        s_iota2 = sem("s_iota2")
        s_ch = sem("s_ch")
        s_keys = sem("s_keys")
        s_win = sem("s_win")
        s_oh = sem("s_oh")
        s_used = sem("s_used")
        s_var = sem("s_var")
        s_sd = sem("s_sd")
        s_deg = sem("s_deg")
        s_sdeg = sem("s_sdeg")
        s_xn = sem("s_xn")
        s_xst = [sem(f"s_xst{i}") for i in range(4)]
        s_far = sem("s_far")
        s_farall = sem("s_farall")
        b = c.enter_context(nc.Block())
        NH = NG * GT // HT

        @b.sync
        def _(sp):
            sp.wait_ge(s_fill, 1)
            sp.dma_start(src_i[:, 0:EFULL], src).then_inc(s_edges, 16)
            sp.dma_start(src_i[0:EREST, EFULL:ET], src_rest).then_inc(s_edges, 16)
            sp.dma_start(dst_i[:, 0:EFULL], dst).then_inc(s_edges, 16)
            sp.dma_start(dst_i[0:EREST, EFULL:ET], dst_rest).then_inc(s_edges, 16)
            sp.dma_start(x_sb[0:NREST, NFULL, :], g["x"][NFULL * P:N, :]).then_inc(s_x, 16)
            sp.dma_start(x_sb[:, 0:NFULL, :], g["x"][0:NFULL * P, :].rearrange("(t p) d -> p t d", p=P)).then_inc(s_x, 16)
            sp.dma_start(g["erow_i"][:, 0, :], esrc).then_inc(s_fedges, 16)
            sp.dma_start(g["erow_i"][:, 1, :], edst).then_inc(s_fedges, 16)
            for w_sb, w, b_sb, bias in zip(g["w"], ws, g["b"], bs):
                sp.dma_start(w_sb[:, :, :], w.rearrange("(c p) n -> p c n", p=P)).then_inc(s_w, 16)
                sp.dma_start(b_sb[:, :], bias.partition_broadcast(P)).then_inc(s_w, 16)
            for t in range(NT):
                sp.wait_ge(s_xn, t + 1)
                sp.dma_start(g["table1"][t * P:(t + 1) * P, :], xn[:, t % 4, :]).then_inc(s_xst[t % 4], 16)
            for q in range(4):
                sp.wait_ge(s_xst[q], 16 * len(range(q, NT, 4)))
            sp.wait_ge(s_w, 64)

        @b.gpsimd
        def _(pool):
            nc.gpsimd.iota(iota[:, :], pattern=[[1, LO]], base=0, channel_multiplier=0,
                           allow_small_or_imprecise_dtypes=True).then_inc(s_iota, 1)
            nc.gpsimd.iota(g["tile_base"][:, :], pattern=[[P, NT]], base=0, channel_multiplier=0,
                           allow_small_or_imprecise_dtypes=True).then_inc(s_iota2, 1)
            nc.gpsimd.memset(ident[:, :], 0.0).then_inc(s_iota2, 1)
            pool.wait_ge(s_iota2, 2)
            nc.gpsimd.affine_select(out=ident[:, :], in_=ident[:, :], compare_op=ALU.not_equal, fill=1.0,
                                    base=0, pattern=[[-1, P]], channel_multiplier=1).then_inc(s_iota2, 1)
            pool.wait_ge(s_iota2, 3)
            pool.wait_ge(s_far, 1)
            nc.gpsimd.partition_all_reduce(far_max[:, 1:2], far_max[:, 0:1], P, RMAX).then_inc(s_farall, 1)

        @b.vector
        def _(dve):
            v = nc.vector
            step = Chain(dve, s_ch)
            v.memset(x_sb[:, NFULL, :], 0.0)
            v.memset(src_i[:, EFULL:NG * GT], -1)
            v.memset(dst_i[:, EFULL:NG * GT], -1).then_inc(s_fill, 1)
            v.memset(zero[:, :], 0.0)
            v.memset(ones[:, :], 1.0)
            v.memset(rel[:, NG * GT:NGP * GT], -1.0)
            v.memset(g["dst_hi"][:, NG * GT:NGP * GT], -1.0)
            step(v.memset(g["dst_lo"][:, NG * GT:NGP * GT], -1.0))
            dve.wait_ge(s_iota, 1)
            v.tensor_copy(g["iota_bf"][:, :], iota[:, 0:P])
            dve.wait_ge(s_edges, 64)

            def keys(raw, hi, lo, n, shift):
                step(v.tensor_single_scalar(key_i[:, 0:n], raw[:, 0:n], shift, op=ALU.arith_shift_right))
                step(v.tensor_copy(hi[:, 0:n], key_i[:, 0:n]))
                step(v.tensor_single_scalar(key_i[:, 0:n], raw[:, 0:n], (1 << shift) - 1, op=ALU.bitwise_and))
                step(v.tensor_copy(lo[:, 0:n], key_i[:, 0:n]))

            keys(src_i, src_hi, src_lo, NG * GT, 7)

            def onehots(i, par):
                t0 = i * (2 * HT) + par * HT
                for t in range(HT):
                    v.tensor_scalar(oh_lo[:, par, t, :], g["iota_bf"][:, :], src_lo[:, bass.ds(t0 + t, 1)], None,
                                    ALU.is_equal)
                v.tensor_tensor(oh_hi[:, par, :, :], iota[:, 0:NT].unsqueeze(1).to_broadcast([P, HT, NT]),
                                src_hi[:, bass.ds(t0, HT)].unsqueeze(2).to_broadcast([P, HT, NT]),
                                ALU.is_equal).then_inc(s_oh, 1)

            with dve.Fori(0, NH // 2) as i:
                for par in range(2):
                    dve.wait_ge(s_used, i * 2 + par + 1)
                    onehots(i, par)

            dve.wait_ge(s_x, 32)
            for t in range(NT):
                last = v.bn_stats(stats[:, t, :], x_sb[:, t, :])
            step(last)
            for t in range(NT):
                last = v.bn_aggr(mv[:, t, :], stats[:, t, :])
            step(last)
            step(v.tensor_scalar(scale[:, :], mv[:, :, 1], EPS, None, ALU.add))
            dve.sem_inc(s_var, 1)

            keys(dst_i, g["dst_hi"], g["dst_lo"], NG * GT, 7)
            step(v.tensor_copy(dst_left[:, :], dst_i[:, :]))
            step(v.tensor_copy(row_f[:, :], dst_left[0:1, 0:NG * GT:GT]))
            dve.sem_inc(s_keys, 1)
            dve.wait_ge(s_win, 1)
            step(v.tensor_tensor(rel[:, 0:NG * GT].rearrange("p (g t) -> p g t", t=GT),
                                 dst_left[:, :].rearrange("p (g t) -> p g t", t=GT),
                                 ps_win[:, 0:NG].unsqueeze(2).to_broadcast([P, NG, GT]), ALU.subtract))
            step(v.tensor_scalar(tmp[:, :], rel[:, 0:NG * GT], 0.0, None, ALU.is_lt))
            step(v.scalar_tensor_tensor(far[:, :], rel[:, 0:NG * GT], float(WIN - 1), tmp[:, :], ALU.is_gt, ALU.max))
            step(v.tensor_scalar(tmp[:, :], dst_left[:, :], 0.0, None, ALU.is_ge))
            step(v.tensor_tensor(far[:, :], far[:, :], tmp[:, :], ALU.mult))
            step(v.scalar_tensor_tensor(tmp[:, :], dst_left[:, :], 1.0, far[:, :], ALU.add, ALU.mult))
            step(v.tensor_scalar(dst_left[:, :], tmp[:, :], -1.0, None, ALU.add))
            step(v.tensor_reduce(far_max[:, 0:1], far[:, :], AX, ALU.max))
            dve.sem_inc(s_far, 1)
            dve.wait_ge(s_farall, 1)
            step(v.tensor_copy(g["left_i"][:, :], far_max[:, 1:2]))
            step(v.tensor_copy(src_f[:, :], src_i[:, :]))
            step(v.tensor_scalar(src_f[:, :], src_f[:, :], 0.0, None, ALU.max))

            dve.wait_ge(s_used, NH + 2)
            step(v.tensor_scalar(g["rs_out"][:, :], ps_deg[:, 0:NT], 1.0, None, ALU.max))
            dve.sem_inc(s_deg, 1)
            dve.wait_ge(s_sd, 1)
            step(v.reciprocal(scale[:, :], std[:, :]))
            dve.wait_ge(s_sdeg, 1)
            step(v.reciprocal(g["rs_out"][:, :], src_hi[:, 0:NT]))
            step(v.tensor_tensor(scale[:, :], scale[:, :], g["rs_out"][:, :], ALU.mult))
            for t in range(NT):
                if t >= 4:
                    dve.wait_ge(s_xst[t % 4], 16 * (t // 4))
                v.tensor_scalar(xn[:, t % 4, :], x_sb[:, t, :], mv[:, t, 0:1], scale[:, t:t + 1],
                                ALU.subtract, ALU.mult).then_inc(s_xn, 1)

            dve.wait_ge(s_fedges, 32)
            keys(g["erow_i"][:, 1, :], g["edst_hi"], g["edst_lo"], FT, 8)
            step(v.tensor_scalar(g["erow_i"][:, :, :], g["erow_i"][:, :, :], float(N - 1), None, ALU.min))

        @b.scalar
        def _(act):
            act.wait_ge(s_var, 1)
            nc.scalar.activation(std[:, :], scale[:, :], ACT.Sqrt).then_inc(s_sd, 1)
            act.wait_ge(s_deg, 1)
            nc.scalar.activation(src_hi[:, 0:NT], g["rs_out"][:, :], ACT.Sqrt).then_inc(s_sdeg, 1)

        @b.tensor
        def _(pe):
            pe.wait_ge(s_ch, 1)
            nc.tensor.matmul(ps_deg[:, 0:NT], zero[:, :], zero[:, 0:NT], start=True, stop=False,
                             skip_group_check=True).then_inc(s_used, 2)
            with pe.Fori(0, NH // 2) as i:
                for par in range(2):
                    pe.wait_ge(s_oh, i * 2 + par + 1)
                    for t in range(HT):
                        last = nc.tensor.matmul(ps_deg[:, 0:NT], oh_lo[:, par, t, :], oh_hi[:, par, t, :],
                                                start=False, stop=False, skip_group_check=True)
                    last.then_inc(s_used, 1)
            pe.wait_ge(s_keys, 1)
            nc.tensor.matmul(ps_win[:, 0:NG], ones[:, :], row_f[:, :], start=True, stop=True).then_inc(s_win, 1)


def aggregate(g, layer):
    nc, agg, iota = g["nc"], g["agg"], g["iota"]
    table = g["table1"] if layer == 1 else g["table2"]
    rel, src_f, dst_i, dst_left = g["rel"], g["src_f"], g["dst_i"], g["dst_left"]
    hist = layer == 1
    with ExitStack() as c:
        def sb(name, shape, dt=F32):
            return c.enter_context(nc.sbuf_tensor(f"{name}_{layer}", shape, dt))
        def sem(name):
            return c.enter_context(nc.semaphore(f"{name}_{layer}"))
        idx = [sb(f"idx{s}", [P, GT], I32) for s in range(SETS)]
        msg = [sb(f"msg{s}", [P, GT, D]) for s in range(SETS)]
        oh = [sb(f"oh{s}", [P, GT, WIN]) for s in range(SETS)]
        oh_lo = [sb(f"ohlo{s}", [P, GT, P], BF16) for s in range(SETS)]
        oh_hi = [sb(f"ohhi{s}", [P, GT, NT], BF16) for s in range(SETS)]
        zero = sb("zero_a", [P, P], BF16)
        left_rel = sb("left_rel", [P, GT])
        ps = [c.enter_context(nc.psum_tensor(f"ps_agg{s}_{layer}", [P, 512], F32)) for s in range(SETS)]
        ps_deg = c.enter_context(nc.psum_tensor(f"ps_in_{layer}", [P, 512], F32))
        idx_ready = sem("idx_ready")
        gathered = [sem(f"gathered{s}") for s in range(SETS)]
        oh_ready = sem("oh_ready")
        summed = sem("summed")
        added = sem("added")
        zeroed = sem("zeroed")
        chain = sem("chain")
        l_idx, l_gath, l_oh, l_sum, l_add, l_ch = (sem(f"left_{n}") for n in ("idx", "gath", "oh", "sum", "add", "ch"))
        s_deg, s_sdeg = sem("s_deg"), sem("s_sdeg")
        b = c.enter_context(nc.Block())

        @b.scalar
        def _(act):
            with act.Fori(0, NG // SETS) as i:
                for s in range(SETS):
                    act.wait_ge(summed, i * SETS + s + 1)
                    nc.scalar.activation(idx[s][:, :], src_f[:, bass.ds(i * (SETS * GT) + s * GT, GT)],
                                         ACT.Copy).then_inc(idx_ready, 1)
            if hist:
                act.wait_ge(s_deg, 1)
                nc.scalar.activation(left_rel[:, 0:GT], zero[:, 0:GT], ACT.Sqrt)
                nc.scalar.activation(g["dst_hi"][:, 0:NT], g["rs_in"][:, :], ACT.Sqrt).then_inc(s_sdeg, 1)
            left = act.value_load(g["left_i"][0:1, 0:1], min_val=0, max_val=1)
            with act.If(left > 0):
                with act.Fori(0, NT) as t:
                    with act.Fori(0, NG) as k:
                        act.wait_ge(l_sum, t * NG + k + 1)
                        nc.scalar.activation(idx[0][:, :], src_f[:, bass.ds(k * GT, GT)], ACT.Copy).then_inc(l_idx, 1)
            act.sem_inc(l_ch, 1)

        @b.gpsimd
        def _(pool):
            def gathers(s, done):
                for t in range(GT):
                    nc.gpsimd.indirect_dma_start(msg[s][:, t, :], None, table,
                                                 bass.IndirectOffsetOnAxis(ap=idx[s][:, t:t + 1], axis=0)
                                                 ).then_inc(done, 16)
            with pool.Fori(0, NG // SETS) as i:
                for s in range(SETS):
                    pool.wait_ge(idx_ready, i * SETS + s + 1)
                    pool.nop(nofuse=True)
                    gathers(s, gathered[s])
            left = pool.value_load(g["left_i"][0:1, 0:1], min_val=0, max_val=1)
            with pool.If(left > 0):
                with pool.Fori(0, NT) as t:
                    with pool.Fori(0, NG) as k:
                        pool.wait_ge(l_idx, t * NG + k + 1)
                        pool.nop(nofuse=True)
                        gathers(0, l_gath)
            pool.sem_inc(l_ch, 1)

        @b.vector
        def _(dve):
            v = nc.vector
            v.memset(zero[:, :], 0.0).then_inc(zeroed, 1)
            v.memset(agg[:, :, :], 0.0).then_inc(chain, 1)

            def onehots(k, s):
                for t in range(GT):
                    last = v.tensor_scalar(oh[s][:, t, :], iota[:, 0:WIN], rel[:, bass.ds(k * GT + t, 1)], None, ALU.is_equal)
                if hist:
                    for t in range(GT):
                        v.tensor_scalar(oh_lo[s][:, t, :], g["iota_bf"][:, :], g["dst_lo"][:, bass.ds(k * GT + t, 1)],
                                        None, ALU.is_equal)
                    last = v.tensor_tensor(oh_hi[s][:, :, :], iota[:, 0:NT].unsqueeze(1).to_broadcast([P, GT, NT]),
                                           g["dst_hi"][:, bass.ds(k * GT, GT)].unsqueeze(2).to_broadcast([P, GT, NT]),
                                           ALU.is_equal)
                last.then_inc(oh_ready, 1)

            onehots(0, 0)
            with dve.Fori(0, NG // SETS) as i:
                for s in range(SETS):
                    k = i * SETS + s
                    dve.wait_ge(summed, k + 2)
                    onehots(k + 1, (s + 1) % SETS)
                    dve.wait_ge(summed, k + SETS + 1)
                    dve.wait_ge(chain, k + 1)
                    w = dve.value_load(dst_i[0:1, bass.ds(k * GT, 1)], min_val=0, max_val=N - 1)
                    win = agg[:, :, bass.ds(w, WIN)]
                    v.tensor_tensor(win, win, ps[s][:, 0:D].rearrange("p (c n) -> p c n", c=DC),
                                    ALU.add).then_inc(chain, 1)
            if hist:
                v.tensor_scalar(g["rs_in"][:, :], ps_deg[:, 0:NT], 1.0, None, ALU.max).then_inc(s_deg, 1)
                dve.wait_ge(s_sdeg, 1)
                v.reciprocal(g["rs_in"][:, :], g["dst_hi"][:, 0:NT]).then_inc(s_deg, 1)
            left = dve.value_load(g["left_i"][0:1, 0:1], min_val=0, max_val=1)
            with dve.If(left > 0):
                dve.wait_ge(chain, NG + 1)
                with dve.Fori(0, NT) as t:
                    with dve.Fori(0, NG) as k:
                        n = t * NG + k
                        dve.wait_ge(l_add, n + 1)
                        v.tensor_scalar(left_rel[:, :], dst_left[:, bass.ds(k * GT, GT)],
                                        g["tile_base"][:, bass.ds(t, 1)], None, ALU.subtract).then_inc(l_oh, 1)
                        dve.wait_ge(l_oh, n * 2 + 1)
                        for j in range(GT):
                            last = v.tensor_scalar(oh[0][:, j, :], iota[:, 0:P],
                                                   left_rel[:, j:j + 1], None, ALU.is_equal)
                        last.then_inc(l_oh, 1)
                        dve.wait_ge(l_sum, n + 2)
                        win = agg[:, :, bass.ds(t * P, P)]
                        v.tensor_tensor(win, win, ps[0][:, 0:D].rearrange("p (c n) -> p c n", c=DC),
                                        ALU.add).then_inc(l_add, 1)
            dve.sem_inc(l_ch, 1)

        @b.tensor
        def _(pe):
            t_ = nc.tensor
            pe.wait_ge(zeroed, 1)
            t_.matmul(ps_deg[:, 0:NT], zero[:, :], zero[:, 0:NT], start=True, stop=False,
                      skip_group_check=True).then_inc(summed, SETS)

            def sums(s):
                for h in range(DC):
                    for t in range(GT):
                        last = t_.matmul(ps[s][:, h * WIN:(h + 1) * WIN], msg[s][:, t, h * P:(h + 1) * P], oh[s][:, t, :],
                                         start=(t == 0), stop=(t == GT - 1), skip_group_check=True)
                return last

            with pe.Fori(0, NG // SETS) as i:
                for s in range(SETS):
                    k = i * SETS + s
                    pe.wait_ge(oh_ready, k + 1)
                    if hist:
                        for t in range(GT):
                            t_.matmul(ps_deg[:, 0:NT], oh_lo[s][:, t, :], oh_hi[s][:, t, :], start=False, stop=False,
                                      skip_group_check=True)
                    pe.wait_ge(gathered[s], (i + 1) * (16 * GT))
                    sums(s).then_inc(summed, 1)
            left = pe.value_load(g["left_i"][0:1, 0:1], min_val=0, max_val=1)
            pe.sem_inc(l_sum, 1)
            pe.sem_inc(l_add, 1)
            with pe.If(left > 0):
                with pe.Fori(0, NT) as t:
                    with pe.Fori(0, NG) as k:
                        n = t * NG + k
                        pe.wait_ge(l_oh, n * 2 + 2)
                        pe.wait_ge(l_gath, (n + 1) * (16 * GT))
                        sums(0).then_inc(l_sum, 1)
            pe.sem_inc(l_ch, 1)


def transform(g, layer):
    nc, agg, x_sb = g["nc"], g["agg"], g["x_sb"]
    w, bias = g["w"][layer - 1], g["b"][layer - 1]
    B = 4
    with ExitStack() as c:
        def sem(name):
            return c.enter_context(nc.semaphore(f"{name}_{layer}"))
        lin = c.enter_context(nc.sbuf_tensor(f"lin_{layer}", [P, B, D], F32))
        hid = c.enter_context(nc.sbuf_tensor(f"hid_{layer}", [P, B, D], F32))
        ps = [c.enter_context(nc.psum_tensor(f"ps_lin{s}_{layer}", [P, 512], F32)) for s in range(B)]
        t_mm, t_lin, t_hid, t_add = sem("t_mm"), sem("t_lin"), sem("t_hid"), sem("t_add")
        stored = [sem(f"t_st{s}") for s in range(B)]
        b = c.enter_context(nc.Block())

        @b.tensor
        def _(pe):
            for t in range(NT):
                if t >= B:
                    pe.wait_ge(t_lin, t - B + 1)
                for h in range(DC):
                    last = nc.tensor.matmul(ps[t % B][:, 0:D], agg[:, h, t * P:(t + 1) * P], w[:, h, :],
                                            start=(h == 0), stop=(h == DC - 1))
                last.then_inc(t_mm, 1)

        @b.vector
        def _(dve):
            for t in range(NT):
                dve.wait_ge(t_mm, t + 1)
                if layer == 1 and t >= B:
                    dve.wait_ge(t_hid, t - B + 1)
                if layer == 2 and t >= B:
                    dve.wait_ge(t_add, t - B + 1)
                nc.vector.scalar_tensor_tensor(lin[:, t % B, :], ps[t % B][:, 0:D], g["rs_in"][:, t:t + 1],
                                               bias[:, :], ALU.mult, ALU.add).then_inc(t_lin, 1)
                if layer == 2 and t >= 1:
                    dve.wait_ge(t_lin, t)
                    nc.vector.tensor_tensor(x_sb[:, t - 1, :], x_sb[:, t - 1, :], lin[:, (t - 1) % B, :],
                                            ALU.add).then_inc(t_add, 1)
            if layer == 2:
                dve.wait_ge(t_lin, NT)
                nc.vector.tensor_tensor(x_sb[:, NT - 1, :], x_sb[:, NT - 1, :], lin[:, (NT - 1) % B, :],
                                        ALU.add).then_inc(t_add, 1)

        if layer == 1:
            @b.scalar
            def _(act):
                for t in range(NT):
                    act.wait_ge(t_lin, t + 1)
                    if t >= B:
                        act.wait_ge(stored[t % B], 16 * (t // B))
                    nc.scalar.activation(hid[:, t % B, :], lin[:, t % B, :], ACT.Relu,
                                         scale=g["rs_out"][:, t:t + 1]).then_inc(t_hid, 1)

            @b.sync
            def _(sp):
                for t in range(NT):
                    sp.wait_ge(t_hid, t + 1)
                    sp.dma_start(g["table2"][t * P:(t + 1) * P, :], hid[:, t % B, :]).then_inc(stored[t % B], 16)
                for s in range(B):
                    sp.wait_ge(stored[s], 16 * len(range(s, NT, B)))


def gat_nodes(nc, x_sb, xt, node, ident, node_tab, dest_tab, x1_dram, w_gat, att_src, att_dst):
    as_, ad, h = node["as_"], node["ad"], node["h"]
    B = 2
    with ExitStack() as c:
        def sb(name, shape, dt=F32):
            return c.enter_context(nc.sbuf_tensor(name, shape, dt))
        def sem(name):
            return c.enter_context(nc.semaphore(name))
        wg = sb("wg", [P, DC, HE])
        att = sb("att", [P, 2, HE])
        stats = sb("stats_g", [P, NT, 6])
        mv = sb("mv_g", [P, NT, 2])
        dev = sb("dev_g", [P, NT])
        xn = sb("xn_g", [P, 4, D])
        prod = sb("prod_g", [P, NT, HE])
        row = sb("row_g", [P, NT, VAL])
        real = sb("real", [P, 2])
        top = sb("top_g", [P, 2, HEADS])
        z = sb("z_g", [P, NT, HEADS])
        ps_t = [c.enter_context(nc.psum_tensor(f"ps_t{s}", [P, 512], F32)) for s in range(B)]
        ps_h = [c.enter_context(nc.psum_tensor(f"ps_h{s}", [P, 512], F32)) for s in range(B)]
        n_w, n_x1, n_ch, n_var, n_dev = sem("n_w"), sem("n_x1"), sem("n_ch"), sem("n_var"), sem("n_dev")
        n_xn, n_tr, n_xt, n_h, n_hc = sem("n_xn"), sem("n_tr"), sem("n_xt"), sem("n_h"), sem("n_hc")
        n_top, n_all, n_z, n_e, n_tab, n_st, n_real = (sem(k) for k in ("n_top", "n_all", "n_z", "n_e", "n_tab", "n_st", "n_real"))
        b = c.enter_context(nc.Block())

        @b.sync
        def _(sp):
            sp.dma_start(wg[:, :, :], w_gat.rearrange("(c p) n -> p c n", p=P)).then_inc(n_w, 16)
            sp.dma_start(att[:, 0, :], att_src.rearrange("h e -> (h e)").partition_broadcast(P)).then_inc(n_w, 16)
            sp.dma_start(att[:, 1, :], att_dst.rearrange("h e -> (h e)").partition_broadcast(P)).then_inc(n_w, 16)
            sp.dma_start(x1_dram.rearrange("t p d -> p t d"), x_sb[:, :, :]).then_inc(n_x1, 16)
            sp.wait_ge(n_tab, 1)
            sp.dma_start(node_tab.rearrange("(t p) v -> p t v", p=P), row[:, :, :]).then_inc(n_st, 16)
            sp.wait_ge(n_tab, 2)
            sp.dma_start(dest_tab.rearrange("(t p) v -> p t v", p=P),
                         ad[:, :, :, :].rearrange("p t a h -> p t (a h)")).then_inc(n_st, 16)
            sp.wait_ge(n_x1, 16)
            sp.wait_ge(n_st, 32)

        @b.gpsimd
        def _(pool):
            nc.gpsimd.memset(real[:, 0:1], 1.0).then_inc(n_real, 1)
            pool.wait_ge(n_real, 1)
            nc.gpsimd.affine_select(out=real[:, 0:1], in_=real[:, 0:1], compare_op=ALU.is_ge, fill=0.0,
                                    base=NREST - 1, pattern=[[0, 1]], channel_multiplier=-1).then_inc(n_real, 1)
            pool.wait_ge(n_top, 1)
            nc.gpsimd.partition_all_reduce(top[:, 1, :], top[:, 0, :], P, RMAX).then_inc(n_all, 1)

        @b.vector
        def _(dve):
            v = nc.vector
            step = Chain(dve, n_ch)
            for t in range(NT):
                last = v.bn_stats(stats[:, t, :], x_sb[:, t, :])
            step(last)
            for t in range(NT):
                last = v.bn_aggr(mv[:, t, :], stats[:, t, :])
            step(last)
            step(v.tensor_scalar(dev[:, :], mv[:, :, 1], EPS, None, ALU.add))
            dve.sem_inc(n_var, 1)
            dve.wait_ge(n_dev, 1)
            step(v.reciprocal(dev[:, :], z[:, :, 0]))
            for t in range(NT + 1):
                if t < NT:
                    if t >= 4:
                        dve.wait_ge(n_tr, t - 3)
                    v.tensor_scalar(xn[:, t % 4, :], x_sb[:, t, :], mv[:, t, 0:1], dev[:, t:t + 1],
                                    ALU.subtract, ALU.mult).then_inc(n_xn, 1)
                if t >= 1:
                    dve.wait_ge(n_h, t)
                    v.tensor_copy(h[:, t - 1, :], ps_h[(t - 1) % B][:, 0:HE]).then_inc(n_hc, 1)
            dve.wait_ge(n_w, 48)
            dve.wait_ge(n_hc, NT)
            for a, o in ((0, as_[:, :, :]), (1, ad[:, :, 0, :])):
                step(v.tensor_tensor(prod[:, :, :], h[:, :, :], att[:, a, :].unsqueeze(1).to_broadcast([P, NT, HE]), ALU.mult))
                step(v.tensor_reduce(o, prod[:, :, :].rearrange("p t (h e) -> p t h e", h=HEADS), AX, ALU.add))
            v.tensor_copy(row[:, :, 0:HEADS], as_[:, :, :])
            v.tensor_copy(row[:, :, HEADS:VAL], h[:, :, :]).then_inc(n_tab, 1)
            dve.wait_ge(n_real, 2)
            v.tensor_copy(z[:, :, :], as_[:, :, :])
            step(v.tensor_scalar(real[:, 1:2], real[:, 0:1], 1.0, -NEG, ALU.subtract, ALU.mult))
            step(v.tensor_scalar(z[:, NT - 1, :], as_[:, NT - 1, :], real[:, 0:1], real[:, 1:2], ALU.mult, ALU.add))
            step(v.tensor_reduce(top[:, 0, :], z[:, :, :].rearrange("p t h -> p h t"), AX, ALU.max))
            dve.sem_inc(n_top, 1)
            dve.wait_ge(n_all, 1)
            guard = ad[:, :, 1, :]
            step(v.tensor_tensor(guard, ad[:, :, 0, :], top[:, 1, :].unsqueeze(1).to_broadcast([P, NT, HEADS]), ALU.add))
            step(v.scalar_tensor_tensor(guard, guard, 0.2, guard, ALU.mult, ALU.max))
            dve.sem_inc(n_tab, 1)
            step(v.tensor_tensor(z[:, :, :], as_[:, :, :], ad[:, :, 0, :], ALU.add))
            step(v.scalar_tensor_tensor(z[:, :, :], z[:, :, :], 0.2, z[:, :, :], ALU.mult, ALU.max))
            step(v.tensor_tensor(z[:, :, :], z[:, :, :], guard, ALU.subtract))
            dve.sem_inc(n_z, 1)

        @b.scalar
        def _(act):
            act.wait_ge(n_var, 1)
            nc.scalar.activation(z[:, :, 0], dev[:, :], ACT.Sqrt).then_inc(n_dev, 1)
            for t in range(NT):
                act.wait_ge(n_tr, t + 1)
                nc.scalar.activation(xt[:, :, t * P:(t + 1) * P],
                                     ps_t[t % B][:, 0:D].rearrange("p (c n) -> p c n", c=DC), ACT.Copy).then_inc(n_xt, 1)
            act.wait_ge(n_z, 1)
            nc.scalar.activation(node["e_self"][:, :, :], z[:, :, :], ACT.Exp).then_inc(n_e, 1)

        @b.tensor
        def _(pe):
            pe.wait_ge(n_w, 48)
            for t in range(NT + 1):
                if t < NT:
                    pe.wait_ge(n_xn, t + 1)
                    if t >= B:
                        pe.wait_ge(n_xt, t - B + 1)
                    for h_ in range(DC):
                        last = nc.tensor.transpose(ps_t[t % B][:, h_ * P:(h_ + 1) * P], xn[:, t % 4, h_ * P:(h_ + 1) * P],
                                                   ident[:, :])
                    last.then_inc(n_tr, 1)
                if t >= 1:
                    u = t - 1
                    pe.wait_ge(n_xt, u + 1)
                    if u >= B:
                        pe.wait_ge(n_hc, u - B + 1)
                    for h_ in range(DC):
                        last = nc.tensor.matmul(ps_h[u % B][:, 0:HE], xt[:, h_, u * P:(u + 1) * P], wg[:, h_, :],
                                                start=(h_ == 0), stop=(h_ == DC - 1))
                    last.then_inc(n_h, 1)


def gat_edges(nc, xt, node, ident, iota, erow_i, edst_hi, edst_lo, node_tab, dest_tab, y_dram, x1_dram,
              b_gat, ln_gamma, ln_beta, ew1, eb1, ew2, eb2, out):
    with ExitStack() as c:
        def sb(name, shape, dt=F32, ctx=c):
            return ctx.enter_context(nc.sbuf_tensor(name, shape, dt))
        def pb(name, ctx=c):
            return ctx.enter_context(nc.psum_tensor(name, [P, 512], F32))
        def sem(name, ctx=c):
            return ctx.enter_context(nc.semaphore(name))
        sums_sb = sb("sums_sb", [P, NC, LO])
        ps_val = [pb(f"ps_val{i}") for i in range(2)]
        rows = HI * CV

        def acc(j):
            return ps_val[j // 2][0:rows, (j % 2) * LO:(j % 2 + 1) * LO]

        with ExitStack() as m:
            w1 = sb("ew1_sb", [P, DC, NE, HID], F32, m)
            w2 = sb("ew2_sb", [P, NE, FC, D], F32, m)
            b1 = sb("eb1_sb", [P, NE * FC], F32, m)
            b2 = sb("eb2_sb", [P, NE, D], F32, m)
            idx = [sb(f"eidx{s}", [P, 2, BT], I32, m) for s in range(SETS)]
            nrow = [sb(f"nrow{s}", [P, BT, VAL], F32, m) for s in range(SETS)]
            drow = [sb(f"drow{s}", [P, BT, 2 * HEADS], F32, m) for s in range(SETS)]
            z = [sb(f"ez{s}", [P, BT, HEADS], F32, m) for s in range(SETS)]
            val = [sb(f"val{s}", [P, BT, VAL], F32, m) for s in range(SETS)]
            oh_lo = [sb(f"elo{s}", [P, BT, LO], F32, m) for s in range(SETS)]
            oh_hi = [sb(f"ehi{s}", [P, BT, HI], F32, m) for s in range(SETS)]
            outer = [sb(f"outer{s}", [P, BT, NC * HI * CV], F32, m) for s in range(2)]
            hid = [sb(f"ehid{s}", [P, FC, P], F32, m) for s in range(2)]
            y_sb = sb("y_sb", [P, NE, D], F32, m)
            zero = sb("zero_e", [P, LO], F32, m)
            ps_h = [pb(f"ps_eh{s}", m) for s in range(2)]
            ps_y = [pb(f"ps_ey{s}", m) for s in range(2)]
            names = ("w", "zero", "idx", "gone", "z", "e", "ch", "outer", "used", "h", "hh", "ymm", "y", "yfree", "yst", "last")
            S = {n: sem("e_" + n, m) for n in names}
            gath = [sem(f"e_gath{s}", m) for s in range(SETS)]
            b = m.enter_context(nc.Block())
            NB = FT // BT
            NI = NB // SETS
            W_LOADS = 16 * (NE + 3)
            assert NT < NI - 2

            @b.sync
            def _(sp):
                sp.sem_inc(S["yfree"], NE)
                for e in range(NE):
                    sp.dma_start(w1[:, :, e, :], ew1[e, :, :].rearrange("(c p) f -> p c f", p=P)).then_inc(S["w"], 16)
                sp.dma_start(w2[:, :, :, :], ew2.rearrange("e (c p) d -> p e c d", p=P)).then_inc(S["w"], 16)
                with nc.allow_non_contiguous_dma(reason="2048 biases, once"):
                    sp.dma_start(b1[:, :], eb1.rearrange("e (c p) -> p (e c)", p=P)).then_inc(S["w"], 16)
                sp.dma_start(b2[:, :, :], eb2.partition_broadcast(P)).then_inc(S["w"], 16)
                with sp.Fori(0, NT) as i:
                    for e in range(NE):
                        n = i * NE + e
                        sp.wait_ge(S["y"], n + 3)
                        sp.dma_start(y_dram[bass.ds(i, 1), :, e * D:(e + 1) * D].rearrange("a p d -> (a p) d"),
                                     y_sb[:, e, :]).then_inc(S["yst"], 16)
                        sp.wait_ge(S["yst"], (n + 1) * 16)
                        sp.sem_inc(S["yfree"], 1)

            @b.gpsimd
            def _(pool):
                def batch(i, s):
                    pool.wait_ge(S["idx"], i * SETS + s + 1)
                    pool.nop(nofuse=True)
                    for t in range(BT):
                        nc.gpsimd.indirect_dma_start(nrow[s][:, t, :], None, node_tab, bass.IndirectOffsetOnAxis(
                            ap=idx[s][:, 0, t:t + 1], axis=0)).then_inc(gath[s], 16)
                        nc.gpsimd.indirect_dma_start(drow[s][:, t, :], None, dest_tab, bass.IndirectOffsetOnAxis(
                            ap=idx[s][:, 1, t:t + 1], axis=0)).then_inc(gath[s], 16)
                with pool.Fori(0, NI) as i:
                    for s in range(SETS):
                        batch(i, s)

            @b.scalar
            def _(act):
                A = nc.scalar
                AHEAD = SETS - 1

                def stage(k, s):
                    A.activation(idx[s][:, :, :], erow_i[:, :, bass.ds(k * BT, BT)], ACT.Copy).then_inc(S["idx"], 1)

                def weights(k, s):
                    act.wait_ge(S["z"], k + 1)
                    A.activation(val[s][:, :, HE:VAL], z[s][:, :, :], ACT.Exp).then_inc(S["e"], 1)

                def gelu(n, e):
                    act.wait_ge(S["h"], n + 1)
                    act.wait_ge(S["ymm"], n + 1)
                    for f in range(FC):
                        last = A.activation(hid[e % 2][:, f, :], ps_h[e % 2][:, f * P:(f + 1) * P], ACT.Gelu,
                                            bias=b1[:, e * FC + f:e * FC + f + 1])
                    last.then_inc(S["hh"], 1)

                def body(i, experts, last=False):
                    for s in range(SETS):
                        k = i * SETS + s
                        if not last or s == 0:
                            act.wait_ge(S["gone"], k + 1)
                            stage(k + AHEAD, (s + AHEAD) % SETS)
                        if not last or s + 1 < SETS:
                            weights(k + 1, (s + 1) % SETS)
                        if experts:
                            gelu(k, s)

                for k in range(AHEAD):
                    stage(k, k)
                act.wait_ge(S["w"], W_LOADS)
                weights(0, 0)
                with act.Fori(0, NT) as i:
                    body(i, True)
                with act.Fori(NT, NI - 1) as i:
                    body(i, False)
                body(NI - 1, False, True)

            @b.vector
            def _(dve):
                v = nc.vector
                v.memset(zero[:, :], 0.0).then_inc(S["zero"], 1)
                dve.wait_ge(S["zero"], 1)
                dve.sem_inc(S["y"], 2)
                dve.sem_inc(S["gone"], 1)

                def first(i, k, s):
                    dve.wait_ge(gath[s], (i + 1) * (32 * BT))
                    dve.wait_ge(S["used"], k + 1)
                    onehot = lambda t: v.tensor_scalar(oh_lo[s][:, t, :], iota[:, :], edst_lo[:, bass.ds(k * BT + t, 1)],
                                                       None, ALU.is_equal)
                    zz = z[s][:, :, :]
                    v.tensor_tensor(zz, nrow[s][:, :, 0:HEADS], drow[s][:, :, 0:HEADS], ALU.add).then_inc(S["ch"], 1)
                    onehot(0)
                    dve.wait_ge(S["ch"], k * 3 + 1)
                    v.scalar_tensor_tensor(zz, zz, 0.2, zz, ALU.mult, ALU.max).then_inc(S["ch"], 1)
                    onehot(1)
                    dve.wait_ge(S["ch"], k * 3 + 2)
                    v.tensor_tensor(zz, zz, drow[s][:, :, HEADS:2 * HEADS], ALU.subtract).then_inc(S["z"], 1)
                    onehot(2)
                    onehot(3)
                    v.tensor_tensor(oh_hi[s][:, :, :], iota[:, 0:HI].unsqueeze(1).to_broadcast([P, BT, HI]),
                                    edst_hi[:, bass.ds(k * BT, BT)].unsqueeze(2).to_broadcast([P, BT, HI]),
                                    ALU.is_equal).then_inc(S["ch"], 1)

                def second(k, s):
                    dve.wait_ge(S["e"], k + 1)
                    v.tensor_tensor(val[s][:, :, 0:HE].rearrange("p t (h e) -> p t h e", h=HEADS),
                                    nrow[s][:, :, HEADS:VAL].rearrange("p t (h e) -> p t h e", h=HEADS),
                                    val[s][:, :, HE:VAL].unsqueeze(3).to_broadcast([P, BT, HEADS, NE]),
                                    ALU.mult).then_inc(S["gone"], 1)
                    dve.wait_ge(S["gone"], k + 2)
                    dve.wait_ge(S["ch"], k * 3 + 3)
                    dve.wait_ge(S["used"], k + 3)
                    for t in range(BT):
                        v.tensor_tensor(outer[s % 2][:, t, :].rearrange("p (j a c) -> p j a c", j=NC, a=HI),
                                        oh_hi[s][:, t, :].unsqueeze(1).unsqueeze(3).to_broadcast([P, NC, HI, CV]),
                                        val[s][:, t, :].rearrange("p (j c) -> p j c", j=NC).unsqueeze(2)
                                        .to_broadcast([P, NC, HI, CV]), ALU.mult).then_inc(S["outer"], 1)

                def evacuate(n, e):
                    dve.wait_ge(S["ymm"], n + 3)
                    dve.wait_ge(S["yfree"], n + 1)
                    v.tensor_tensor(y_sb[:, e, :], ps_y[e % 2][:, 0:D], b2[:, e, :], ALU.add).then_inc(S["y"], 1)

                def body(i, experts, evac0, last=False):
                    for s in range(SETS):
                        k = i * SETS + s
                        if not last or s + 1 < SETS:
                            first(i if s + 1 < SETS else i + 1, k + 1, (s + 1) % SETS)
                        second(k, s)
                        if evac0 if s == 0 else experts:
                            evacuate(k - 1, (s - 1) % NE)

                dve.wait_ge(S["w"], W_LOADS)
                first(0, 0, 0)
                body(0, True, False)
                with dve.Fori(1, NT) as i:
                    body(i, True, True)
                body(NT, False, True)
                with dve.Fori(NT + 1, NI - 1) as i:
                    body(i, False, False)
                body(NI - 1, False, False, True)

            @b.tensor
            def _(pe):
                mm = nc.tensor.matmul
                pe.wait_ge(S["zero"], 1)
                pe.wait_ge(S["w"], W_LOADS)
                for j in range(NC):
                    last = mm(acc(j), zero[:, 0:rows], zero[:, :], start=True, stop=False, skip_group_check=True)
                last.then_inc(S["used"], SETS)
                pe.sem_inc(S["hh"], 2)
                pe.sem_inc(S["ymm"], 2)

                def up(i, n, e):
                    pe.wait_ge(S["hh"], n + 1)
                    for f in range(FC):
                        for h in range(DC):
                            last = mm(ps_h[e % 2][:, f * P:(f + 1) * P], w1[:, h, e, f * P:(f + 1) * P],
                                      xt[:, h, bass.ds(i * P, P)], start=(h == 0), stop=(h == DC - 1), skip_group_check=True)
                    last.then_inc(S["h"], 1)

                def down(n, e):
                    pe.wait_ge(S["hh"], n + 3)
                    pe.wait_ge(S["y"], n + 1)
                    for f in range(FC):
                        last = mm(ps_y[e % 2][:, 0:D], hid[e % 2][:, f, :], w2[:, e, f, :], start=(f == 0),
                                  stop=(f == FC - 1), skip_group_check=True)
                    last.then_inc(S["ymm"], 1)

                def edges(k, s):
                    for t in range(BT):
                        pe.wait_ge(S["outer"], k * BT + t + 1)
                        for j in range(NC):
                            last = mm(acc(j), outer[s % 2][:, t, j * rows:(j + 1) * rows], oh_lo[s][:, t, :],
                                      start=False, stop=False, skip_group_check=True)
                    last.then_inc(S["used"], 1)

                with pe.Fori(0, NT) as i:
                    for s in range(SETS):
                        k = i * SETS + s
                        up(i, k, s)
                        edges(k, s)
                        down(k, s)
                with pe.Fori(NT, NI) as i:
                    for s in range(SETS):
                        edges(i * SETS + s, s)
                pe.sem_inc(S["last"], 1)

        route(nc, c, sb, pb, sem, ps_val, acc, sums_sb, node, ident, y_dram, x1_dram, b_gat, ln_gamma, ln_beta, out)


def route(nc, c, sb, pb, sem, ps_val, acc, sums_sb, node, ident, y_dram, x1_dram, b_gat, ln_gamma, ln_beta, out):
    rows = HI * CV
    NT2 = HI * (LO // P)
    F = 7
    S = sb("S", [P, NT2, VAL])
    tmp = sb("r_tmp", [P, NT, HE])
    par = sb("r_par", [P, 3, HE])
    den = sb("r_den", [P, NT, HEADS])
    mean = sb("r_mean", [P, NT, 3])
    sc = sb("r_sc", [P, NT, NE])
    cnt = sb("r_cnt", [P, NT, NE])
    gt = sb("r_gt", [P, NT, NE])
    gate = sb("r_gate", [P, NT, NE])
    yb = [sb(f"yb{s}", [P, NE * D]) for s in range(F)]
    xb = [sb(f"xb{s}", [P, D]) for s in range(F)]
    ps = [pb(f"ps_r{i}") for i in range(4)]
    r_par, r_ch, r_ev, r_tr, r_cp, r_act, r_actd, r_done = (sem(f"r_{n}") for n in
                                                             ("parl", "ch", "ev", "tr", "cp", "act", "actd", "done"))
    r_in = [sem(f"r_in{s}") for s in range(F)]
    r_out = [sem(f"r_out{s}") for s in range(F)]
    r_free, r_add = sem("r_free"), sem("r_add")
    b = c.enter_context(nc.Block())

    @b.sync
    def _(sp):
        for n, a in enumerate((b_gat, ln_gamma, ln_beta)):
            sp.dma_start(par[:, n, :], a.partition_broadcast(P)).then_inc(r_par, 16)
        sp.sem_inc(r_free, F)

        def body(i):
            for s in range(F):
                t = i * F + s
                sp.wait_ge(r_free, t + 1)
                sp.dma_start(yb[s][:, :], y_dram[bass.ds(t, 1), :, :].rearrange("a p d -> (a p) d")).then_inc(r_in[s], 16)
                sp.dma_start(xb[s][:, :], x1_dram[bass.ds(t, 1), :, :].rearrange("a p d -> (a p) d")).then_inc(r_in[s], 16)
        with sp.Fori(0, NT // F) as i:
            body(i)

    @b.scalar
    def _(act):
        act.wait_ge(r_act, 1)
        nc.scalar.activation(mean[:, :, 2], mean[:, :, 1], ACT.Sqrt).then_inc(r_actd, 1)
        act.wait_ge(r_act, 2)
        nc.scalar.activation(gate[:, :, :], sc[:, :, :], ACT.Exp).then_inc(r_actd, 1)

        def store(i, s, last=False):
            t = i * F + s
            act.wait_ge(r_add, i * (F * NE) + (NE - 1) * F + s + 1)
            n = NREST if last else P
            act.dma_start(out[bass.ds(t * P, n), :], xb[s][0:n, :]).then_inc(r_out[s], 16)
            act.wait_ge(r_out[s], (i + 1) * 16)
            act.sem_inc(r_free, 1)
        with act.Fori(0, NT // F - 1) as i:
            for s in range(F):
                store(i, s)
        for s in range(F):
            store(NT // F - 1, s, s == F - 1)

    @b.tensor
    def _(pe):
        for n in range(NC * 2):
            j, half = n // 2, n % 2
            pe.wait_ge(r_ev, j + 1)
            if n >= 4:
                pe.wait_ge(r_cp, n - 3)
            nc.tensor.transpose(ps[n % 4][:, 0:rows], sums_sb[0:rows, j, half * P:(half + 1) * P],
                                ident[0:rows, 0:rows]).then_inc(r_tr, 1)

    @b.vector
    def _(dve):
        v = nc.vector
        step = Chain(dve, r_ch)
        for j in range(NC):
            v.tensor_copy(sums_sb[0:rows, j, :], acc(j)).then_inc(r_ev, 1)
        for n in range(NC * 2):
            j, half = n // 2, n % 2
            dve.wait_ge(r_tr, n + 1)
            v.tensor_copy(S[:, :, :].rearrange("p (a f) v -> p a f v", f=2)[:, :, half, j * CV:(j + 1) * CV],
                          ps[n % 4][:, 0:rows].rearrange("p (a c) -> p a c", a=HI)).then_inc(r_cp, 1)
        dve.wait_ge(r_cp, NC * 2)
        dve.wait_ge(r_par, 48)
        e_self, h = node["e_self"], node["h"]
        bc = lambda a: a.unsqueeze(3).to_broadcast([P, NT, HEADS, NE])
        four = lambda a: a.rearrange("p t (h e) -> p t h e", h=HEADS)
        step(v.tensor_tensor(four(tmp[:, :, :]), four(h[:, :, :]), bc(e_self[:, :, :]), ALU.mult))
        step(v.tensor_tensor(tmp[:, :, :], tmp[:, :, :], S[:, 0:NT, 0:HE], ALU.add))
        step(v.scalar_tensor_tensor(den[:, :, :], e_self[:, :, :], 1e-16, S[:, 0:NT, HE:VAL], ALU.add, ALU.add))
        step(v.reciprocal(den[:, :, :], den[:, :, :]))
        step(v.tensor_tensor(four(tmp[:, :, :]), four(tmp[:, :, :]), bc(den[:, :, :]), ALU.mult))
        pbc = lambda n: par[:, n, :].unsqueeze(1).to_broadcast([P, NT, HE])
        step(v.tensor_tensor(tmp[:, :, :], tmp[:, :, :], pbc(0), ALU.add))
        mb = lambda n: mean[:, :, n].unsqueeze(2).to_broadcast([P, NT, HE])
        agg = S[:, 0:NT, 0:HE]
        step(v.tensor_reduce(mean[:, :, 0], tmp[:, :, :], AX, ALU.add))
        step(v.tensor_scalar(mean[:, :, 0], mean[:, :, 0], 1.0 / HE, None, ALU.mult))
        step(v.tensor_tensor(tmp[:, :, :], tmp[:, :, :], mb(0), ALU.subtract))
        step(v.tensor_tensor(agg, tmp[:, :, :], tmp[:, :, :], ALU.mult))
        step(v.tensor_reduce(mean[:, :, 1], agg, AX, ALU.add))
        step(v.tensor_scalar(mean[:, :, 1], mean[:, :, 1], 1.0 / HE, EPS, ALU.mult, ALU.add))
        dve.sem_inc(r_act, 1)
        dve.wait_ge(r_actd, 1)
        step(v.reciprocal(mean[:, :, 1], mean[:, :, 2]))
        step(v.tensor_tensor(tmp[:, :, :], tmp[:, :, :], mb(1), ALU.mult))
        step(v.tensor_tensor(tmp[:, :, :], tmp[:, :, :], pbc(1), ALU.mult))
        step(v.tensor_tensor(tmp[:, :, :], tmp[:, :, :], pbc(2), ALU.add))
        step(v.tensor_reduce(sc[:, :, :], tmp[:, :, :].rearrange("p t (h e) -> p t e h", h=HEADS), AX, ALU.add))
        step(v.tensor_scalar(sc[:, :, :], sc[:, :, :], 1.0 / HEADS, None, ALU.mult))
        step(v.memset(cnt[:, :, :], 0.0))
        for e in range(NE):
            for o in range(NE):
                if o == e:
                    continue
                step(v.tensor_tensor(gt[:, :, 0], sc[:, :, o], sc[:, :, e], ALU.is_ge if o < e else ALU.is_gt))
                step(v.tensor_tensor(cnt[:, :, e], cnt[:, :, e], gt[:, :, 0], ALU.add))
        step(v.tensor_scalar(cnt[:, :, :], cnt[:, :, :], 2.0, None, ALU.is_lt))
        step(v.tensor_reduce(mean[:, :, 0], sc[:, :, :], AX, ALU.max))
        step(v.tensor_tensor(sc[:, :, :], sc[:, :, :], mean[:, :, 0].unsqueeze(2).to_broadcast([P, NT, NE]), ALU.subtract))
        dve.sem_inc(r_act, 1)
        dve.wait_ge(r_actd, 2)
        step(v.tensor_tensor(gate[:, :, :], gate[:, :, :], cnt[:, :, :], ALU.mult))
        step(v.tensor_reduce(mean[:, :, 0], gate[:, :, :], AX, ALU.add))
        step(v.reciprocal(mean[:, :, 1], mean[:, :, 0]))
        step(v.tensor_tensor(gate[:, :, :], gate[:, :, :], mean[:, :, 1].unsqueeze(2).to_broadcast([P, NT, NE]), ALU.mult))

        with dve.Fori(0, NT // F) as i:
            for s in range(F):
                dve.wait_ge(r_in[s], (i + 1) * 32)
            for e in range(NE):
                for s in range(F):
                    n = i * (F * NE) + e * F + s
                    if e > 0:
                        dve.wait_ge(r_add, n - F + 1)
                    v.scalar_tensor_tensor(xb[s][:, :], yb[s][:, e * D:(e + 1) * D],
                                           gate[:, bass.ds(i * F + s, 1), e], xb[s][:, :], ALU.mult, ALU.add
                                           ).then_inc(r_add, 1)


_OUTS = [((N, D), "float32")]


def kernel(**inputs):
    import numpy as _np
    import concourse.bacc as _bacc
    from concourse import mybir as _mybir
    from concourse.bass_utils import run_bass_kernel_spmd as _run

    a = {k: _np.asarray(v) for k, v in inputs.items()}
    cut = EFULL * P
    edge = a["L0_ffn_edge_index"]

    def by_tile(e):
        return _np.ascontiguousarray(e[:cut].reshape(EFULL, P).T), e[cut:].reshape(EREST, 1)

    src, src_rest = by_tile(a["src"])
    dst, dst_rest = by_tile(a["dst"])
    arrays = dict(
        x=a["x"], src=src, src_rest=src_rest, dst=dst, dst_rest=dst_rest,
        w1=a["L0_gnn_W1"], b1=a["L0_gnn_b1"], w2=a["L0_gnn_W2"], b2=a["L0_gnn_b2"],
        w_gat=a["L0_ffn_W_gat"], att_src=a["L0_ffn_att_src"], att_dst=a["L0_ffn_att_dst"],
        b_gat=a["L0_ffn_b_gat"], ln_gamma=a["L0_ffn_ln_gamma"], ln_beta=a["L0_ffn_ln_beta"],
        ew1=a["L0_ffn_W1"], eb1=a["L0_ffn_b1"], ew2=a["L0_ffn_W2"], eb2=a["L0_ffn_b2"],
        esrc=edge[0].reshape(P, FT), edst=edge[1].reshape(P, FT),
    )
    nc = _bacc.Bacc("TRN2", target_bir_lowering=False, num_devices=1)
    ins, args = {}, []
    for name, v in arrays.items():
        v = _np.ascontiguousarray(v)
        ins[f"in_{name}"] = v
        args.append(nc.dram_tensor(f"in_{name}", v.shape, _mybir.dt.from_np(v.dtype), kind="ExternalInput").ap())
    for i, (shape, dtype) in enumerate(_OUTS):
        args.append(nc.dram_tensor(f"out_{i}", shape, _mybir.dt.from_np(_np.dtype(dtype)), kind="ExternalOutput").ap())
    program(nc, *args)
    r = _run(nc, [ins], core_ids=[0])
    return r.results[0]["out_0"]
```

```python
import concourse.bass as bass
from concourse import mybir
from contextlib import ExitStack

F32, BF16, I32 = mybir.dt.float32, mybir.dt.bfloat16, mybir.dt.int32
ALU = mybir.AluOpType
ACT = mybir.ActivationFunctionType
AX = mybir.AxisListType.X
RMAX = bass.bass_isa.ReduceOp.max

P = 128
N = 6250
D = 256
DC = D // P
NT = (N + P - 1) // P
NFULL = N // P
NREST = N - NFULL * P

E = 100000
ET = (E + P - 1) // P
EFULL = E // P
EREST = E - EFULL * P
GT = 4
SETS = 4
NG = -(-ET // GT)
NG += -NG % SETS
NGP = NG + 1
HT = 8
WIN = P
AGGC = N + WIN + (-(N + WIN)) % P

EF = 131072
FT = EF // P
HEADS, NE = 4, 4
HE = HEADS * NE
HID = 512
FC = HID // P
VAL = HE + HEADS
BT = 4
FG = FT // BT
FI = NT + 1
FM = FI * SETS
BITS = 13
WORD = 0x40000000
EPS = 1e-5
EPS = 1e-5
NEG = -1.0e30


def program(nc, x, src, src_rest, dst, dst_rest, w1, b1, w2, b2, w_gat, att_src, att_dst, b_gat,
            ln_gamma, ln_beta, ew1, eb1, ew2, eb2, esrc, edst, out):
    table1 = nc.dram_tensor("table1", (NT * P, D), F32).ap()
    table2 = nc.dram_tensor("table2", (NT * P, D), F32).ap()
    node_tab = nc.dram_tensor("node_tab", (NT * P, VAL), F32).ap()
    dest_tab = nc.dram_tensor("dest_tab", (AGGC, 2 * HEADS), F32).ap()
    x1_dram = nc.dram_tensor("x1_dram", (NT, P, D), F32).ap()
    y_dram = nc.dram_tensor("y_dram", (NT, P, NE * D), F32).ap()

    with ExitStack() as top:
        def sb(name, shape, dt=F32, ctx=top):
            return ctx.enter_context(nc.sbuf_tensor(name, shape, dt))

        ident = sb("ident", [P, P])
        iota = sb("iota", [P, P])
        tile_base = sb("tile_base", [P, NT])
        ed = dict(
            src_i=sb("esrc_i", [P, FT], I32), win_i=sb("ewin_i", [1, FG], I32),
            rel=sb("erel", [P, FT]), left=sb("eleft", [P, FT]), left_i=sb("eleft_i", [P, 1], I32))
        agg = sb("agg", [P, DC, AGGC])
        node = dict(as_=sb("as_", [P, NT, HEADS]), ad=sb("ad", [P, NT, 2, HEADS]),
                    h=sb("h", [P, NT, HE]), e_self=sb("e_self", [P, NT, HEADS]))
        with ExitStack() as nodes:
            x_sb = sb("x_sb", [P, NT, D], F32, nodes)
            with ExitStack() as gnn:
                def gb(name, shape, dt=F32):
                    return sb(name, shape, dt, gnn)
                g = dict(
                    nc=nc, x=x, x_sb=x_sb, ident=ident, iota=iota, table1=table1, table2=table2, agg=agg,
                    src_f=gb("src_f", [P, NG * GT]),
                    dst_i=gb("dst_i", [P, NG * GT], I32),
                    dst_left=gb("dst_left", [P, NG * GT]),
                    rel=gb("rel", [P, NGP * GT]),
                    dst_hi=gb("dst_hi", [P, NGP * GT]),
                    dst_lo=gb("dst_lo", [P, NGP * GT]),
                    iota_bf=gb("iota_bf", [P, P], BF16),
                    tile_base=tile_base,
                    left_i=gb("left_i", [P, 1], I32),
                    rs_out=gb("rs_out", [P, NT]),
                    rs_in=gb("rs_in", [P, NT]),
                    w=[gb("w_1", [P, DC, D]), gb("w_2", [P, DC, D])],
                    b=[gb("b_1", [P, D]), gb("b_2", [P, D])],
                    ed=ed,
                )
                key = [gb("key_a", [P, FT]), gb("key_b", [P, FT])]
                odd = gb("odd_row", [P, 2])
                g.update(key=key, odd=odd)
                prologue(g, src, src_rest, dst, dst_rest, (w1, w2), (b1, b2), esrc, edst)
                aggregate(g, 1)
                transform(g, 1)
                aggregate(g, 2)
                transform(g, 2)
            gat_nodes(nc, x_sb, agg, node, ident, node_tab, dest_tab, x1_dram, w_gat, att_src, att_dst)
        gat_edges(nc, agg, node, ident, iota, tile_base, ed, node_tab, dest_tab, y_dram, x1_dram,
                  b_gat, ln_gamma, ln_beta, ew1, eb1, ew2, eb2, out)


class Chain:

    def __init__(self, eng, sem):
        self.eng, self.sem, self.n = eng, sem, 0

    def __call__(self, ins):
        self.n += 1
        ins.then_inc(self.sem, 1)
        self.eng.wait_ge(self.sem, self.n)


def mark_left(v, step, rel, left, tmp, far, far_max, n_main=None):
    step(v.tensor_scalar(tmp, rel, 0.0, None, ALU.is_lt))
    step(v.scalar_tensor_tensor(far, rel, float(WIN - 1), tmp, ALU.is_gt, ALU.max))
    if n_main is not None:
        step(v.memset(far[:, n_main:], 1.0))
    step(v.tensor_scalar(tmp, left, 0.0, None, ALU.is_ge))
    step(v.tensor_tensor(far, far, tmp, ALU.mult))
    step(v.tensor_scalar(tmp, left, float(N), None, ALU.is_lt))
    step(v.tensor_tensor(far, far, tmp, ALU.mult))
    step(v.scalar_tensor_tensor(tmp, left, 1.0, far, ALU.add, ALU.mult))
    step(v.tensor_scalar(left, tmp, -1.0, None, ALU.add))
    step(v.tensor_reduce(far_max, far, AX, ALU.max))


def semaphores(nc, c):
    mine = []

    def sem(name):
        mine.append(nc.alloc_semaphore(name))
        return mine[-1]
    def clear():
        nc.clear_and_free_semaphores(mine)
        nc.all_engine_barrier()
    c.callback(clear)
    return sem


class Sorter:
    COL = FT.bit_length() - 1
    ROW = P.bit_length() - 1
    LEVELS = COL + ROW
    BLK = FT // P
    CHANGES = 2 * ROW + 1

    def __init__(self, nc, key, odd, pb, sem, ident):
        self.nc, self.ident, self.key, self.odd = nc, ident, key, odd
        self.ps = [pb(f"ps_sort{i}") for i in range(2)]
        self.stage_done = sem("sort_stage")
        self.ready = sem("sort_ready")
        self.turned = sem("sort_turned")


    def vector_steps(self, dve):
        v, key = self.nc.vector, self.key
        count, cur, changes = 0, 0, 0

        def wait():
            dve.wait_ge(self.stage_done, count)

        def halves(buf, j):
            a = buf[:, :].rearrange("p (a two b) -> p a two b", two=2, b=1 << j)
            return a[:, :, 0, :], a[:, :, 1, :]

        def exchange(j):
            nonlocal count, cur
            lo, hi = halves(key[cur], j)
            to_lo, to_hi = halves(key[1 - cur], j)
            v.tensor_tensor(to_lo, lo, hi, ALU.min)
            v.tensor_tensor(to_hi, lo, hi, ALU.max).then_inc(self.stage_done, 1)
            count += 1
            cur = 1 - cur
            wait()

        def negate(*parts):
            nonlocal count
            for part, by in parts:
                last = v.tensor_scalar(part, part, by, None, ALU.mult)
            last.then_inc(self.stage_done, 1)
            count += 1
            wait()

        def flips(buf, bit):
            return buf[:, :].rearrange("p (a four b) -> p a four b", four=4, b=1 << bit)[:, :, 1:3, :]

        def change():
            nonlocal changes, cur, count
            dve.sem_inc(self.ready, 1)
            cur = 1 - cur
            for i, half in enumerate(self.ps):
                dve.wait_ge(self.turned, 2 * changes + i + 1)
                last = v.tensor_copy(key[cur][:, i * 512:(i + 1) * 512], half[:, :])
            last.then_inc(self.stage_done, 1)
            count += 1
            changes += 1
            wait()

        negate((halves(key[0], 1)[1], -1.0))
        for level in range(1, self.COL + 1):
            for j in reversed(range(level)):
                exchange(j)
                yield
            if level < self.COL - 1:
                negate((flips(key[cur], level), -1.0))
            elif level == self.COL - 1:
                lo, hi = halves(key[cur], level)
                negate((lo, self.odd[:, 0:1]), (hi, self.odd[:, 1:2]))
        for level in range(self.COL + 1, self.LEVELS + 1):
            change()
            shift = P.bit_length() - 1
            rows = key[cur][:, :].rearrange("q (r p) -> q r p", p=P)

            def row_bits(four, b):
                return key[cur][:, :].rearrange("q (a four b) -> q a four b", four=four, b=b)
            if level < self.LEVELS:
                negate((row_bits(4, 1 << (level - 1 - self.COL))[:, :, 1:3, :], -1.0))
            else:
                negate((row_bits(2, P // 2)[:, :, 1, :], -1.0))
            for j in reversed(range(shift, level)):
                exchange(j - self.COL if j >= self.COL else j - shift + self.ROW)
                yield
            change()
            for j in reversed(range(shift)):
                exchange(j)
                yield
        change()
        self.result = key[cur]


    def transposes(self, pe, n):
        src = self.key[self.source(n)]
        pe.wait_ge(self.ready, n + 1)
        for r in range(self.BLK):
            half = self.BLK // 2
            last = self.nc.tensor.transpose(self.ps[r // half][:, (r % half) * P:(r % half + 1) * P],
                                            src[:, r * P:(r + 1) * P], self.ident[:, :])
            if r % half == half - 1:
                last.then_inc(self.turned, 1)

    def before(self, n):
        exchanges = self.COL * (self.COL + 1) // 2
        for c in range(1, n + 1):
            level = self.COL + 1 + (c - 1) // 2
            exchanges += level - self.ROW if c % 2 else self.ROW
        return exchanges

    def source(self, n):
        return (self.before(n) + n) % 2


def prologue(g, src, src_rest, dst, dst_rest, ws, bs, esrc, edst):
    nc, x_sb, iota, ident = g["nc"], g["x_sb"], g["iota"], g["ident"]
    src_f, dst_i, rel, dst_left = g["src_f"], g["dst_i"], g["rel"], g["dst_left"]
    with ExitStack() as c:
        def sb(name, shape, dt=F32):
            return c.enter_context(nc.sbuf_tensor(name, shape, dt))
        sem = semaphores(nc, c)
        src_i = sb("src_i", [P, NG * GT], I32)
        key_i = sb("key_i", [P, FT], I32)
        src_hi = sb("src_hi", [P, NG * GT])
        src_lo = sb("src_lo", [P, NG * GT])
        tmp = sb("tmp_f", [P, NG * GT])
        far = sb("far", [P, NG * GT])
        far_max = sb("far_max", [P, 2])
        row_no = sb("row_no", [P, 1])
        esrc_i = g["ed"]["src_i"]
        edst_i = g["ed"]["rel"][:, :].bitcast(I32)
        ones = sb("ones", [1, P])
        row_f = sb("row_f", [1, NG])
        oh_lo = sb("oh_lo", [P, 2, HT, P], BF16)
        oh_hi = sb("oh_hi", [P, 2, HT, NT], BF16)
        zero = sb("zero", [P, P], BF16)
        stats = sb("stats", [P, NT, 6])
        mv = sb("mv", [P, NT, 2])
        scale = sb("scale", [P, NT])
        std = sb("std", [P, NT])
        xn = sb("xn", [P, 4, D])
        ps_deg = c.enter_context(nc.psum_tensor("ps_deg", [P, 512], F32))
        ps_win = c.enter_context(nc.psum_tensor("ps_win", [P, 512], F32))
        s_fill = sem("s_fill")
        s_edges = sem("s_edges")
        s_fedges = sem("s_fedges")
        s_x = sem("s_x")
        s_w = sem("s_w")
        s_iota = sem("s_iota")
        s_iota2 = sem("s_iota2")
        s_ch = sem("s_ch")
        s_keys = sem("s_keys")
        s_win = sem("s_win")
        s_oh = sem("s_oh")
        s_used = sem("s_used")
        s_var = sem("s_var")
        s_sd = sem("s_sd")
        s_deg = sem("s_deg")
        s_sdeg = sem("s_sdeg")
        s_xn = sem("s_xn")
        s_xst = [sem(f"s_xst{i}") for i in range(4)]
        s_far = sem("s_far")
        s_farall = sem("s_farall")
        b = c.enter_context(nc.Block())
        NH = NG * GT // HT

        @b.sync
        def _(sp):
            sp.wait_ge(s_fill, 1)
            sp.dma_start(src_i[:, 0:EFULL], src).then_inc(s_edges, 16)
            sp.dma_start(src_i[0:EREST, EFULL:ET], src_rest).then_inc(s_edges, 16)
            sp.dma_start(dst_i[:, 0:EFULL], dst).then_inc(s_edges, 16)
            sp.dma_start(dst_i[0:EREST, EFULL:ET], dst_rest).then_inc(s_edges, 16)
            sp.dma_start(x_sb[0:NREST, NFULL, :], g["x"][NFULL * P:N, :]).then_inc(s_x, 16)
            sp.dma_start(x_sb[:, 0:NFULL, :], g["x"][0:NFULL * P, :].rearrange("(t p) d -> p t d", p=P)).then_inc(s_x, 16)
            sp.dma_start(esrc_i[:, :], esrc).then_inc(s_fedges, 16)
            sp.dma_start(edst_i[:, :], edst).then_inc(s_fedges, 16)
            for w_sb, w, b_sb, bias in zip(g["w"], ws, g["b"], bs):
                sp.dma_start(w_sb[:, :, :], w.rearrange("(c p) n -> p c n", p=P)).then_inc(s_w, 16)
                sp.dma_start(b_sb[:, :], bias.partition_broadcast(P)).then_inc(s_w, 16)
            for t in range(NT):
                sp.wait_ge(s_xn, t + 1)
                sp.dma_start(g["table1"][t * P:(t + 1) * P, :], xn[:, t % 4, :]).then_inc(s_xst[t % 4], 16)
            for q in range(4):
                sp.wait_ge(s_xst[q], 16 * len(range(q, NT, 4)))
            sp.wait_ge(s_w, 64)

        @b.gpsimd
        def _(pool):
            nc.gpsimd.iota(iota[:, :], pattern=[[1, P]], base=0, channel_multiplier=0,
                           allow_small_or_imprecise_dtypes=True).then_inc(s_iota, 1)
            nc.gpsimd.iota(g["tile_base"][:, :], pattern=[[P, NT]], base=0, channel_multiplier=0,
                           allow_small_or_imprecise_dtypes=True).then_inc(s_iota2, 1)
            nc.gpsimd.iota(row_no[:, :], pattern=[[0, 1]], base=0, channel_multiplier=1,
                           allow_small_or_imprecise_dtypes=True).then_inc(s_iota2, 1)
            nc.gpsimd.memset(ident[:, :], 0.0).then_inc(s_iota2, 1)
            pool.wait_ge(s_iota2, 3)
            nc.gpsimd.affine_select(out=ident[:, :], in_=ident[:, :], compare_op=ALU.not_equal, fill=1.0,
                                    base=0, pattern=[[-1, P]], channel_multiplier=1).then_inc(s_iota2, 1)
            pool.wait_ge(s_iota2, 4)
            pool.wait_ge(s_far, 1)
            nc.gpsimd.partition_all_reduce(far_max[:, 1:2], far_max[:, 0:1], P, RMAX).then_inc(s_farall, 1)

        @b.vector
        def _(dve):
            v = nc.vector
            step = Chain(dve, s_ch)
            v.memset(x_sb[:, NFULL, :], 0.0)
            v.memset(src_i[:, EFULL:NG * GT], -1)
            v.memset(dst_i[:, EFULL:NG * GT], -1).then_inc(s_fill, 1)
            v.memset(zero[:, :], 0.0)
            v.memset(ones[:, :], 1.0)
            v.memset(rel[:, NG * GT:NGP * GT], -1.0)
            v.memset(g["dst_hi"][:, NG * GT:NGP * GT], -1.0)
            step(v.memset(g["dst_lo"][:, NG * GT:NGP * GT], -1.0))
            dve.wait_ge(s_iota, 1)
            v.tensor_copy(g["iota_bf"][:, :], iota[:, 0:P])
            dve.wait_ge(s_edges, 64)

            def keys(raw, hi, lo, n):
                step(v.tensor_single_scalar(key_i[:, 0:n], raw[:, 0:n], 7, op=ALU.arith_shift_right))
                step(v.tensor_copy(hi[:, 0:n], key_i[:, 0:n]))
                step(v.tensor_single_scalar(key_i[:, 0:n], raw[:, 0:n], P - 1, op=ALU.bitwise_and))
                step(v.tensor_copy(lo[:, 0:n], key_i[:, 0:n]))

            keys(src_i, src_hi, src_lo, NG * GT)

            def onehots(i, par):
                t0 = i * (2 * HT) + par * HT
                for t in range(HT):
                    v.tensor_scalar(oh_lo[:, par, t, :], g["iota_bf"][:, :], src_lo[:, bass.ds(t0 + t, 1)], None,
                                    ALU.is_equal)
                v.tensor_tensor(oh_hi[:, par, :, :], iota[:, 0:NT].unsqueeze(1).to_broadcast([P, HT, NT]),
                                src_hi[:, bass.ds(t0, HT)].unsqueeze(2).to_broadcast([P, HT, NT]),
                                ALU.is_equal).then_inc(s_oh, 1)

            with dve.Fori(0, NH // 2) as i:
                for par in range(2):
                    dve.wait_ge(s_used, i * 2 + par + 1)
                    onehots(i, par)

            dve.wait_ge(s_x, 32)
            for t in range(NT):
                last = v.bn_stats(stats[:, t, :], x_sb[:, t, :])
            step(last)
            for t in range(NT):
                last = v.bn_aggr(mv[:, t, :], stats[:, t, :])
            step(last)
            step(v.tensor_scalar(scale[:, :], mv[:, :, 1], EPS, None, ALU.add))
            dve.sem_inc(s_var, 1)

            keys(dst_i, g["dst_hi"], g["dst_lo"], NG * GT)
            step(v.tensor_copy(dst_left[:, :], dst_i[:, :]))
            step(v.tensor_copy(row_f[:, :], dst_left[0:1, 0:NG * GT:GT]))
            dve.sem_inc(s_keys, 1)
            dve.wait_ge(s_win, 1)
            step(v.tensor_tensor(rel[:, 0:NG * GT].rearrange("p (g t) -> p g t", t=GT),
                                 dst_left[:, :].rearrange("p (g t) -> p g t", t=GT),
                                 ps_win[:, 0:NG].unsqueeze(2).to_broadcast([P, NG, GT]), ALU.subtract))
            mark_left(v, step, rel[:, 0:NG * GT], dst_left[:, :], tmp[:, :], far[:, :], far_max[:, 0:1])
            dve.sem_inc(s_far, 1)
            dve.wait_ge(s_farall, 1)
            step(v.tensor_copy(g["left_i"][:, :], far_max[:, 1:2]))
            step(v.tensor_copy(src_f[:, :], src_i[:, :]))
            step(v.tensor_scalar(src_f[:, :], src_f[:, :], 0.0, None, ALU.max))

            dve.wait_ge(s_used, NH + 2)
            step(v.tensor_scalar(g["rs_out"][:, :], ps_deg[:, 0:NT], 1.0, None, ALU.max))
            dve.sem_inc(s_deg, 1)
            dve.wait_ge(s_sd, 1)
            step(v.reciprocal(scale[:, :], std[:, :]))
            dve.wait_ge(s_sdeg, 1)
            step(v.reciprocal(g["rs_out"][:, :], src_hi[:, 0:NT]))
            step(v.tensor_tensor(scale[:, :], scale[:, :], g["rs_out"][:, :], ALU.mult))
            for t in range(NT):
                if t >= 4:
                    dve.wait_ge(s_xst[t % 4], 16 * (t // 4))
                v.tensor_scalar(xn[:, t % 4, :], x_sb[:, t, :], mv[:, t, 0:1], scale[:, t:t + 1],
                                ALU.subtract, ALU.mult).then_inc(s_xn, 1)

            dve.wait_ge(s_iota2, 4)
            dve.wait_ge(s_fedges, 32)
            step(v.tensor_scalar(esrc_i[:, :], esrc_i[:, :], float(N - 1), None, ALU.min))
            step(v.tensor_scalar(edst_i[:, :], edst_i[:, :], float((1 << BITS) - 1), None, ALU.min))
            step(v.tensor_scalar(edst_i[:, :], edst_i[:, :], BITS, WORD, ALU.logical_shift_left, ALU.bitwise_or))
            step(v.tensor_tensor(g["key"][0][:, :].bitcast(I32), edst_i[:, :], esrc_i[:, :], ALU.bitwise_or))
            step(v.tensor_copy(key_i[:, 0:1], row_no[:, :]))
            step(v.tensor_single_scalar(key_i[:, 1:2], key_i[:, 0:1], 1, op=ALU.bitwise_and))
            step(v.tensor_copy(far[:, 0:1], key_i[:, 1:2]))
            step(v.tensor_scalar(g["odd"][:, 0:1], far[:, 0:1], -2.0, 1.0, ALU.mult, ALU.add))
            step(v.tensor_scalar(g["odd"][:, 1:2], far[:, 0:1], 2.0, -1.0, ALU.mult, ALU.add))

        @b.scalar
        def _(act):
            act.wait_ge(s_var, 1)
            nc.scalar.activation(std[:, :], scale[:, :], ACT.Sqrt).then_inc(s_sd, 1)
            act.wait_ge(s_deg, 1)
            nc.scalar.activation(src_hi[:, 0:NT], g["rs_out"][:, :], ACT.Sqrt).then_inc(s_sdeg, 1)

        @b.tensor
        def _(pe):
            pe.wait_ge(s_ch, 1)
            nc.tensor.matmul(ps_deg[:, 0:NT], zero[:, :], zero[:, 0:NT], start=True, stop=False,
                             skip_group_check=True).then_inc(s_used, 2)
            with pe.Fori(0, NH // 2) as i:
                for par in range(2):
                    pe.wait_ge(s_oh, i * 2 + par + 1)
                    for t in range(HT):
                        last = nc.tensor.matmul(ps_deg[:, 0:NT], oh_lo[:, par, t, :], oh_hi[:, par, t, :],
                                                start=False, stop=False, skip_group_check=True)
                    last.then_inc(s_used, 1)
            pe.wait_ge(s_keys, 1)
            nc.tensor.matmul(ps_win[:, 0:NG], ones[:, :], row_f[:, :], start=True, stop=True).then_inc(s_win, 1)


def aggregate(g, layer):
    nc, agg, iota = g["nc"], g["agg"], g["iota"]
    table = g["table1"] if layer == 1 else g["table2"]
    rel, src_f, dst_i, dst_left = g["rel"], g["src_f"], g["dst_i"], g["dst_left"]
    hist = layer == 1
    with ExitStack() as c:
        def sb(name, shape, dt=F32):
            return c.enter_context(nc.sbuf_tensor(f"{name}_{layer}", shape, dt))
        sem_of = semaphores(nc, c)
        def sem(name):
            return sem_of(f"{name}_{layer}")
        idx = [sb(f"idx{s}", [P, GT], I32) for s in range(SETS)]
        msg = [sb(f"msg{s}", [P, GT, D]) for s in range(SETS)]
        oh = [sb(f"oh{s}", [P, GT, WIN]) for s in range(SETS)]
        if hist:
            oh_lo = [sb(f"ohlo{s}", [P, GT, P], BF16) for s in range(SETS)]
            oh_hi = [sb(f"ohhi{s}", [P, GT, NT], BF16) for s in range(SETS)]
        zero = sb("zero_a", [P, P], BF16)
        left_rel = sb("left_rel", [P, GT])
        ps = [c.enter_context(nc.psum_tensor(f"ps_agg{s}_{layer}", [P, 512], F32)) for s in range(SETS)]
        ps_deg = c.enter_context(nc.psum_tensor(f"ps_in_{layer}", [P, 512], F32))
        idx_ready = sem("idx_ready")
        gathered = [sem(f"gathered{s}") for s in range(SETS)]
        oh_ready = sem("oh_ready")
        summed = sem("summed")
        added = sem("added")
        zeroed = sem("zeroed")
        chain = sem("chain")
        l_idx, l_gath, l_oh, l_sum, l_add, l_ch = (sem(f"left_{n}") for n in ("idx", "gath", "oh", "sum", "add", "ch"))
        s_deg, s_sdeg = sem("s_deg"), sem("s_sdeg")
        sorting = layer == 2
        if sorting:
            ed = g["ed"]
            sorter = Sorter(nc, g["key"], g["odd"], lambda n: c.enter_context(nc.psum_tensor(n, [P, 512], F32)),
                            sem, g["ident"])
            far_max = sb("far_max_e", [P, 2])
            row_f = sb("row_fe", [1, FG])
            ones = sb("ones_e", [1, P])
            s_row, s_win, s_far, s_all, s_tail = sem("e_row"), sem("e_win"), sem("e_far"), sem("e_all"), sem("e_tail")
            PER_ITER = 4
        b = c.enter_context(nc.Block())

        @b.scalar
        def _(act):
            with act.Fori(0, NG // SETS) as i:
                for s in range(SETS):
                    act.wait_ge(summed, i * SETS + s + 1)
                    nc.scalar.activation(idx[s][:, :], src_f[:, bass.ds(i * (SETS * GT) + s * GT, GT)],
                                         ACT.Copy).then_inc(idx_ready, 1)
            if hist:
                act.wait_ge(s_deg, 1)
                nc.scalar.activation(left_rel[:, 0:GT], zero[:, 0:GT], ACT.Sqrt)
                nc.scalar.activation(g["dst_hi"][:, 0:NT], g["rs_in"][:, :], ACT.Sqrt).then_inc(s_sdeg, 1)
            left = act.value_load(g["left_i"][0:1, 0:1], min_val=0, max_val=1)
            with act.If(left > 0):
                with act.Fori(0, NG) as k:
                    act.wait_ge(l_sum, k * NT + 1)
                    nc.scalar.activation(idx[0][:, :], src_f[:, bass.ds(k * GT, GT)], ACT.Copy).then_inc(l_idx, 1)
            act.sem_inc(l_ch, 1)

        @b.gpsimd
        def _(pool):
            def gathers(s, done):
                for t in range(GT):
                    nc.gpsimd.indirect_dma_start(msg[s][:, t, :], None, table,
                                                 bass.IndirectOffsetOnAxis(ap=idx[s][:, t:t + 1], axis=0)
                                                 ).then_inc(done, 16)
            with pool.Fori(0, NG // SETS) as i:
                for s in range(SETS):
                    pool.wait_ge(idx_ready, i * SETS + s + 1)
                    pool.nop(nofuse=True)
                    gathers(s, gathered[s])
            if sorting:
                pool.wait_ge(s_far, 1)
                nc.gpsimd.partition_all_reduce(far_max[:, 1:2], far_max[:, 0:1], P, RMAX).then_inc(s_all, 1)
            left = pool.value_load(g["left_i"][0:1, 0:1], min_val=0, max_val=1)
            with pool.If(left > 0):
                with pool.Fori(0, NG) as k:
                    pool.wait_ge(l_idx, k + 1)
                    pool.nop(nofuse=True)
                    gathers(0, l_gath)
            pool.sem_inc(l_ch, 1)

        @b.vector
        def _(dve):
            v = nc.vector
            v.memset(zero[:, :], 0.0).then_inc(zeroed, 1)
            v.memset(agg[:, :, :], 0.0).then_inc(chain, 1)

            def unpack(dve, v):
                step = Chain(dve, s_tail)
                word = sorter.result[:, :].bitcast(I32).rearrange("q (r p) -> q p r", p=P)
                spare = g["key"][0] if sorter.result is g["key"][1] else g["key"][1]
                spare_i = spare[:, :].bitcast(I32)
                by_tile = lambda a: a.rearrange("q (p r) -> q p r", p=P)
                step(v.tensor_single_scalar(by_tile(ed["src_i"][:, :]), word, (1 << BITS) - 1, op=ALU.bitwise_and))
                step(v.tensor_scalar(by_tile(spare_i), word, BITS, (1 << BITS) - 1, ALU.arith_shift_right, ALU.bitwise_and))
                step(v.tensor_copy(ed["left"][:, :], spare_i))
                step(v.tensor_scalar(row_f[:, :], ed["left"][0:1, 0:FT:BT], float(N), None, ALU.min))
                step(v.tensor_copy(ed["win_i"][:, :], row_f[:, :]))
                step(v.memset(ones[:, :], 1.0))
                dve.sem_inc(s_row, 1)
                dve.wait_ge(s_win, 1)
                step(v.tensor_tensor(ed["rel"][:, :].rearrange("p (g t) -> p g t", t=BT),
                                     ed["left"][:, :].rearrange("p (g t) -> p g t", t=BT),
                                     ps_deg[:, 0:FG].unsqueeze(2).to_broadcast([P, FG, BT]), ALU.subtract))
                mark_left(v, step, ed["rel"][:, :], ed["left"][:, :], spare[:, :], sorter.result[:, :],
                          far_max[:, 0:1], FM * BT)
                dve.sem_inc(s_far, 1)
                dve.wait_ge(s_all, 1)
                step(v.tensor_copy(ed["left_i"][:, :], far_max[:, 1:2]))

            def onehots(k, s):
                for t in range(GT):
                    last = v.tensor_scalar(oh[s][:, t, :], iota[:, 0:WIN], rel[:, bass.ds(k * GT + t, 1)], None, ALU.is_equal)
                if hist:
                    for t in range(GT):
                        v.tensor_scalar(oh_lo[s][:, t, :], g["iota_bf"][:, :], g["dst_lo"][:, bass.ds(k * GT + t, 1)],
                                        None, ALU.is_equal)
                    last = v.tensor_tensor(oh_hi[s][:, :, :], iota[:, 0:NT].unsqueeze(1).to_broadcast([P, GT, NT]),
                                           g["dst_hi"][:, bass.ds(k * GT, GT)].unsqueeze(2).to_broadcast([P, GT, NT]),
                                           ALU.is_equal)
                last.then_inc(oh_ready, 1)

            def iteration(i):
                for s in range(SETS):
                    k = i * SETS + s
                    dve.wait_ge(summed, k + 2)
                    onehots(k + 1, (s + 1) % SETS)
                    dve.wait_ge(summed, k + SETS + 1)
                    dve.wait_ge(chain, k + 1)
                    w = dve.value_load(dst_i[0:1, bass.ds(k * GT, 1)], min_val=0, max_val=N - 1)
                    win = agg[:, :, bass.ds(w, WIN)]
                    v.tensor_tensor(win, win, ps[s][:, 0:D].rearrange("p (c n) -> p c n", c=DC),
                                    ALU.add).then_inc(chain, 1)

            onehots(0, 0)
            if not sorting:
                with dve.Fori(0, NG // SETS) as i:
                    iteration(i)
            else:
                steps = sorter.vector_steps(dve)
                for i in range(NG // SETS):
                    iteration(i)
                    for _ in range(PER_ITER):
                        next(steps, None)
                unpack(dve, v)
            if hist:
                v.tensor_scalar(g["rs_in"][:, :], ps_deg[:, 0:NT], 1.0, None, ALU.max).then_inc(s_deg, 1)
                dve.wait_ge(s_sdeg, 1)
                v.reciprocal(g["rs_in"][:, :], g["dst_hi"][:, 0:NT]).then_inc(s_deg, 1)
            left = dve.value_load(g["left_i"][0:1, 0:1], min_val=0, max_val=1)
            with dve.If(left > 0):
                dve.wait_ge(chain, NG + 1)
                with dve.Fori(0, NG) as k:
                    with dve.Fori(0, NT) as t:
                        n = k * NT + t
                        dve.wait_ge(l_add, n + 1)
                        v.tensor_scalar(left_rel[:, :], dst_left[:, bass.ds(k * GT, GT)],
                                        g["tile_base"][:, bass.ds(t, 1)], None, ALU.subtract).then_inc(l_oh, 1)
                        dve.wait_ge(l_oh, n * 2 + 1)
                        for j in range(GT):
                            last = v.tensor_scalar(oh[0][:, j, :], iota[:, 0:P],
                                                   left_rel[:, j:j + 1], None, ALU.is_equal)
                        last.then_inc(l_oh, 1)
                        dve.wait_ge(l_sum, n + 2)
                        win = agg[:, :, bass.ds(t * P, P)]
                        v.tensor_tensor(win, win, ps[0][:, 0:D].rearrange("p (c n) -> p c n", c=DC),
                                        ALU.add).then_inc(l_add, 1)
            dve.sem_inc(l_ch, 1)

        @b.tensor
        def _(pe):
            t_ = nc.tensor
            pe.wait_ge(zeroed, 1)
            t_.matmul(ps_deg[:, 0:NT], zero[:, :], zero[:, 0:NT], start=True, stop=False,
                      skip_group_check=True).then_inc(summed, SETS)

            def sums(s):
                for h in range(DC):
                    for t in range(GT):
                        last = t_.matmul(ps[s][:, h * WIN:(h + 1) * WIN], msg[s][:, t, h * P:(h + 1) * P], oh[s][:, t, :],
                                         start=(t == 0), stop=(t == GT - 1), skip_group_check=True)
                return last

            def iteration(i):
                for s in range(SETS):
                    k = i * SETS + s
                    pe.wait_ge(oh_ready, k + 1)
                    if hist:
                        for t in range(GT):
                            t_.matmul(ps_deg[:, 0:NT], oh_lo[s][:, t, :], oh_hi[s][:, t, :], start=False, stop=False,
                                      skip_group_check=True)
                    pe.wait_ge(gathered[s], (i + 1) * (16 * GT))
                    sums(s).then_inc(summed, 1)

            if not sorting:
                with pe.Fori(0, NG // SETS) as i:
                    iteration(i)
            else:
                turn = 0
                for i in range(NG // SETS):
                    iteration(i)
                    while turn < sorter.CHANGES and sorter.before(turn) <= (i + 1) * PER_ITER - 1:
                        sorter.transposes(pe, turn)
                        turn += 1
                assert turn == sorter.CHANGES
                pe.wait_ge(s_row, 1)
                t_.matmul(ps_deg[:, 0:FG], ones[:, :], row_f[:, :], start=True, stop=True,
                          skip_group_check=True).then_inc(s_win, 1)
            left = pe.value_load(g["left_i"][0:1, 0:1], min_val=0, max_val=1)
            pe.sem_inc(l_sum, 1)
            pe.sem_inc(l_add, 1)
            with pe.If(left > 0):
                with pe.Fori(0, NG) as k:
                    pe.wait_ge(l_gath, (k + 1) * (16 * GT))
                    pe.nop(nofuse=True)
                    with pe.Fori(0, NT) as t:
                        pe.wait_ge(l_oh, (k * NT + t) * 2 + 2)
                        sums(0).then_inc(l_sum, 1)
            pe.sem_inc(l_ch, 1)


def transform(g, layer):
    nc, agg, x_sb = g["nc"], g["agg"], g["x_sb"]
    w, bias = g["w"][layer - 1], g["b"][layer - 1]
    B = 4
    with ExitStack() as c:
        sem_of = semaphores(nc, c)
        def sem(name):
            return sem_of(f"{name}_{layer}")
        lin = c.enter_context(nc.sbuf_tensor(f"lin_{layer}", [P, B, D], F32))
        hid = c.enter_context(nc.sbuf_tensor(f"hid_{layer}", [P, B, D], F32))
        ps = [c.enter_context(nc.psum_tensor(f"ps_lin{s}_{layer}", [P, 512], F32)) for s in range(B)]
        t_mm, t_lin, t_hid, t_add = sem("t_mm"), sem("t_lin"), sem("t_hid"), sem("t_add")
        stored = [sem(f"t_st{s}") for s in range(B)]
        b = c.enter_context(nc.Block())

        @b.tensor
        def _(pe):
            for t in range(NT):
                if t >= B:
                    pe.wait_ge(t_lin, t - B + 1)
                for h in range(DC):
                    last = nc.tensor.matmul(ps[t % B][:, 0:D], agg[:, h, t * P:(t + 1) * P], w[:, h, :],
                                            start=(h == 0), stop=(h == DC - 1))
                last.then_inc(t_mm, 1)

        @b.vector
        def _(dve):
            for t in range(NT):
                dve.wait_ge(t_mm, t + 1)
                if layer == 1 and t >= B:
                    dve.wait_ge(t_hid, t - B + 1)
                if layer == 2 and t >= B:
                    dve.wait_ge(t_add, t - B + 1)
                nc.vector.scalar_tensor_tensor(lin[:, t % B, :], ps[t % B][:, 0:D], g["rs_in"][:, t:t + 1],
                                               bias[:, :], ALU.mult, ALU.add).then_inc(t_lin, 1)
                if layer == 2 and t >= 1:
                    dve.wait_ge(t_lin, t)
                    nc.vector.tensor_tensor(x_sb[:, t - 1, :], x_sb[:, t - 1, :], lin[:, (t - 1) % B, :],
                                            ALU.add).then_inc(t_add, 1)
            if layer == 2:
                dve.wait_ge(t_lin, NT)
                nc.vector.tensor_tensor(x_sb[:, NT - 1, :], x_sb[:, NT - 1, :], lin[:, (NT - 1) % B, :],
                                        ALU.add).then_inc(t_add, 1)

        if layer == 1:
            @b.scalar
            def _(act):
                for t in range(NT):
                    act.wait_ge(t_lin, t + 1)
                    if t >= B:
                        act.wait_ge(stored[t % B], 16 * (t // B))
                    nc.scalar.activation(hid[:, t % B, :], lin[:, t % B, :], ACT.Relu,
                                         scale=g["rs_out"][:, t:t + 1]).then_inc(t_hid, 1)

            @b.sync
            def _(sp):
                for t in range(NT):
                    sp.wait_ge(t_hid, t + 1)
                    sp.dma_start(g["table2"][t * P:(t + 1) * P, :], hid[:, t % B, :]).then_inc(stored[t % B], 16)
                for s in range(B):
                    sp.wait_ge(stored[s], 16 * len(range(s, NT, B)))


def gat_nodes(nc, x_sb, xt, node, ident, node_tab, dest_tab, x1_dram, w_gat, att_src, att_dst):
    as_, ad, h = node["as_"], node["ad"], node["h"]
    B = 2
    with ExitStack() as c:
        def sb(name, shape, dt=F32):
            return c.enter_context(nc.sbuf_tensor(name, shape, dt))
        sem = semaphores(nc, c)
        wg = sb("wg", [P, DC, HE])
        att = sb("att", [P, 2, HE])
        stats = sb("stats_g", [P, NT, 6])
        mv = sb("mv_g", [P, NT, 2])
        dev = sb("dev_g", [P, NT])
        xn = sb("xn_g", [P, 4, D])
        prod = sb("prod_g", [P, NT, HE])
        row = sb("row_g", [P, NT, VAL])
        real = sb("real", [P, 2])
        top = sb("top_g", [P, 2, HEADS])
        z = sb("z_g", [P, NT, HEADS])
        ps_t = [c.enter_context(nc.psum_tensor(f"ps_t{s}", [P, 512], F32)) for s in range(B)]
        ps_h = [c.enter_context(nc.psum_tensor(f"ps_h{s}", [P, 512], F32)) for s in range(B)]
        n_w, n_x1, n_ch, n_var, n_dev = sem("n_w"), sem("n_x1"), sem("n_ch"), sem("n_var"), sem("n_dev")
        n_xn, n_tr, n_xt, n_h, n_hc = sem("n_xn"), sem("n_tr"), sem("n_xt"), sem("n_h"), sem("n_hc")
        spare = sb("spare_g", [P, 2 * HEADS])
        n_top, n_all, n_z, n_e, n_tab, n_st, n_real = (sem(k) for k in ("n_top", "n_all", "n_z", "n_e", "n_tab", "n_st", "n_real"))
        b = c.enter_context(nc.Block())

        @b.sync
        def _(sp):
            sp.dma_start(wg[:, :, :], w_gat.rearrange("(c p) n -> p c n", p=P)).then_inc(n_w, 16)
            sp.dma_start(att[:, 0, :], att_src.rearrange("h e -> (h e)").partition_broadcast(P)).then_inc(n_w, 16)
            sp.dma_start(att[:, 1, :], att_dst.rearrange("h e -> (h e)").partition_broadcast(P)).then_inc(n_w, 16)
            sp.dma_start(x1_dram.rearrange("t p d -> p t d"), x_sb[:, :, :]).then_inc(n_x1, 16)
            sp.wait_ge(n_tab, 1)
            sp.dma_start(node_tab.rearrange("(t p) v -> p t v", p=P), row[:, :, :]).then_inc(n_st, 16)
            sp.dma_start(dest_tab[NT * P:AGGC, :], spare[:, :]).then_inc(n_st, 16)
            sp.wait_ge(n_tab, 2)
            sp.dma_start(dest_tab[0:NT * P, :].rearrange("(t p) v -> p t v", p=P),
                         ad[:, :, :, :].rearrange("p t a h -> p t (a h)")).then_inc(n_st, 16)
            sp.wait_ge(n_x1, 16)
            sp.wait_ge(n_st, 48)

        @b.gpsimd
        def _(pool):
            nc.gpsimd.memset(real[:, 0:1], 1.0).then_inc(n_real, 1)
            pool.wait_ge(n_real, 1)
            nc.gpsimd.affine_select(out=real[:, 0:1], in_=real[:, 0:1], compare_op=ALU.is_ge, fill=0.0,
                                    base=NREST - 1, pattern=[[0, 1]], channel_multiplier=-1).then_inc(n_real, 1)
            pool.wait_ge(n_top, 1)
            nc.gpsimd.partition_all_reduce(top[:, 1, :], top[:, 0, :], P, RMAX).then_inc(n_all, 1)

        @b.vector
        def _(dve):
            v = nc.vector
            step = Chain(dve, n_ch)
            v.memset(spare[:, :], 0.0)
            for t in range(NT):
                last = v.bn_stats(stats[:, t, :], x_sb[:, t, :])
            step(last)
            for t in range(NT):
                last = v.bn_aggr(mv[:, t, :], stats[:, t, :])
            step(last)
            step(v.tensor_scalar(dev[:, :], mv[:, :, 1], EPS, None, ALU.add))
            dve.sem_inc(n_var, 1)
            dve.wait_ge(n_dev, 1)
            step(v.reciprocal(dev[:, :], z[:, :, 0]))
            for t in range(NT + 1):
                if t < NT:
                    if t >= 4:
                        dve.wait_ge(n_tr, t - 3)
                    v.tensor_scalar(xn[:, t % 4, :], x_sb[:, t, :], mv[:, t, 0:1], dev[:, t:t + 1],
                                    ALU.subtract, ALU.mult).then_inc(n_xn, 1)
                if t >= 1:
                    dve.wait_ge(n_h, t)
                    v.tensor_copy(h[:, t - 1, :], ps_h[(t - 1) % B][:, 0:HE]).then_inc(n_hc, 1)
            dve.wait_ge(n_w, 48)
            dve.wait_ge(n_hc, NT)
            for a, o in ((0, as_[:, :, :]), (1, ad[:, :, 0, :])):
                step(v.tensor_tensor(prod[:, :, :], h[:, :, :], att[:, a, :].unsqueeze(1).to_broadcast([P, NT, HE]), ALU.mult))
                step(v.tensor_reduce(o, prod[:, :, :].rearrange("p t (h e) -> p t h e", h=HEADS), AX, ALU.add))
            v.tensor_copy(row[:, :, 0:HEADS], as_[:, :, :])
            v.tensor_copy(row[:, :, HEADS:VAL], h[:, :, :]).then_inc(n_tab, 1)
            dve.wait_ge(n_real, 2)
            v.tensor_copy(z[:, :, :], as_[:, :, :])
            step(v.tensor_scalar(real[:, 1:2], real[:, 0:1], 1.0, -NEG, ALU.subtract, ALU.mult))
            step(v.tensor_scalar(z[:, NT - 1, :], as_[:, NT - 1, :], real[:, 0:1], real[:, 1:2], ALU.mult, ALU.add))
            step(v.tensor_reduce(top[:, 0, :], z[:, :, :].rearrange("p t h -> p h t"), AX, ALU.max))
            dve.sem_inc(n_top, 1)
            dve.wait_ge(n_all, 1)
            guard = ad[:, :, 1, :]
            step(v.tensor_tensor(guard, ad[:, :, 0, :], top[:, 1, :].unsqueeze(1).to_broadcast([P, NT, HEADS]), ALU.add))
            step(v.scalar_tensor_tensor(guard, guard, 0.2, guard, ALU.mult, ALU.max))
            dve.sem_inc(n_tab, 1)
            step(v.tensor_tensor(z[:, :, :], as_[:, :, :], ad[:, :, 0, :], ALU.add))
            step(v.scalar_tensor_tensor(z[:, :, :], z[:, :, :], 0.2, z[:, :, :], ALU.mult, ALU.max))
            step(v.tensor_tensor(z[:, :, :], z[:, :, :], guard, ALU.subtract))
            dve.sem_inc(n_z, 1)

        @b.scalar
        def _(act):
            act.wait_ge(n_var, 1)
            nc.scalar.activation(z[:, :, 0], dev[:, :], ACT.Sqrt).then_inc(n_dev, 1)
            for t in range(NT):
                act.wait_ge(n_tr, t + 1)
                nc.scalar.activation(xt[:, :, t * P:(t + 1) * P],
                                     ps_t[t % B][:, 0:D].rearrange("p (c n) -> p c n", c=DC), ACT.Copy).then_inc(n_xt, 1)
            act.wait_ge(n_z, 1)
            nc.scalar.activation(node["e_self"][:, :, :], z[:, :, :], ACT.Exp).then_inc(n_e, 1)

        @b.tensor
        def _(pe):
            pe.wait_ge(n_w, 48)
            for t in range(NT + 1):
                if t < NT:
                    pe.wait_ge(n_xn, t + 1)
                    if t >= B:
                        pe.wait_ge(n_xt, t - B + 1)
                    for h_ in range(DC):
                        last = nc.tensor.transpose(ps_t[t % B][:, h_ * P:(h_ + 1) * P], xn[:, t % 4, h_ * P:(h_ + 1) * P],
                                                   ident[:, :])
                    last.then_inc(n_tr, 1)
                if t >= 1:
                    u = t - 1
                    pe.wait_ge(n_xt, u + 1)
                    if u >= B:
                        pe.wait_ge(n_hc, u - B + 1)
                    for h_ in range(DC):
                        last = nc.tensor.matmul(ps_h[u % B][:, 0:HE], xt[:, h_, u * P:(u + 1) * P], wg[:, h_, :],
                                                start=(h_ == 0), stop=(h_ == DC - 1))
                    last.then_inc(n_h, 1)


def gat_edges(nc, xt, node, ident, iota, tile_base, ed, node_tab, dest_tab, y_dram, x1_dram,
              b_gat, ln_gamma, ln_beta, ew1, eb1, ew2, eb2, out):
    with ExitStack() as c:
        def sb(name, shape, dt=F32, ctx=c):
            return ctx.enter_context(nc.sbuf_tensor(name, shape, dt))
        def pb(name, ctx=c):
            return ctx.enter_context(nc.psum_tensor(name, [P, 512], F32))
        def sem(name, ctx=c):
            return ctx.enter_context(nc.semaphore(name))
        sums = sb("sums", [VAL, AGGC])

        with ExitStack() as m:
            w1 = sb("ew1_sb", [P, DC, NE, HID], F32, m)
            w2 = sb("ew2_sb", [P, NE, FC, D], F32, m)
            b1 = sb("eb1_sb", [P, NE * FC], F32, m)
            b2 = sb("eb2_sb", [P, NE, D], F32, m)
            idx = [sb(f"eidx{s}", [P, BT], I32, m) for s in range(SETS)]
            nrow = [sb(f"nrow{s}", [P, BT, VAL], F32, m) for s in range(SETS)]
            win = [sb(f"ewin{s}", [P, 2 * HEADS], F32, m) for s in range(SETS)]
            oh = [sb(f"eoh{s}", [P, BT, WIN], F32, m) for s in range(SETS)]
            oh_t = [sb(f"eoht{s}", [P, BT, P], F32, m) for s in range(2)]
            z = [sb(f"ez{s}", [P, BT, HEADS], F32, m) for s in range(SETS)]
            val = [sb(f"val{s}", [P, BT, VAL], F32, m) for s in range(SETS)]
            left_rel = sb("eleft_rel", [P, BT], F32, m)
            hid = [sb(f"ehid{s}", [P, FC, P], F32, m) for s in range(2)]
            y_sb = sb("y_sb", [P, NE, D], F32, m)
            ps_t = pb("ps_et", m)
            ps_ad = pb("ps_ead", m)
            ps_sum = [pb(f"ps_es{s}", m) for s in range(2)]
            ps_h = [pb(f"ps_eh{s}", m) for s in range(2)]
            ps_y = [pb(f"ps_ey{s}", m) for s in range(2)]
            S = {n: sem("e_" + n, m) for n in
                 ("w",
                  "idx",
                  "oh",
                  "t",
                  "tcopy",
                  "ad",
                  "z",
                  "e",
                  "val",
                  "used",
                  "ev",
                  "ch",
                  "end",
                  "h",
                  "hh",
                  "ymm",
                  "y",
                  "yst",
                  "yfree")}
            gath = [sem(f"e_gath{s}", m) for s in range(SETS)]
            winl = [sem(f"e_winl{s}", m) for s in range(SETS)]
            L = {n: sem("l_" + n, m) for n in
                 ("idx", "gath", "win", "oh", "t", "tcopy", "ad", "z", "e", "val", "sum", "ev", "zc")}
            b = m.enter_context(nc.Block())
            W_LOADS = 16 * (NE + 3)

            @b.sync
            def _(sp):
                sp.sem_inc(S["yfree"], NE)
                for e in range(NE):
                    sp.dma_start(w1[:, :, e, :], ew1[e, :, :].rearrange("(c p) f -> p c f", p=P)).then_inc(S["w"], 16)
                sp.dma_start(w2[:, :, :, :], ew2.rearrange("e (c p) d -> p e c d", p=P)).then_inc(S["w"], 16)
                with nc.allow_non_contiguous_dma(reason="2048 biases, once"):
                    sp.dma_start(b1[:, :], eb1.rearrange("e (c p) -> p (e c)", p=P)).then_inc(S["w"], 16)
                sp.dma_start(b2[:, :, :], eb2.partition_broadcast(P)).then_inc(S["w"], 16)
                with sp.Fori(0, NT) as i:
                    for e in range(NE):
                        n = i * NE + e
                        sp.wait_ge(S["y"], n + 3)
                        sp.dma_start(y_dram[bass.ds(i, 1), :, e * D:(e + 1) * D].rearrange("a p d -> (a p) d"),
                                     y_sb[:, e, :]).then_inc(S["yst"], 16)
                        sp.wait_ge(S["yst"], (n + 1) * 16)
                        sp.sem_inc(S["yfree"], 1)
                left = sp.value_load(ed["left_i"][0:1, 0:1], min_val=0, max_val=1)
                with sp.If(left > 0):
                    with sp.Fori(0, FG) as k:
                        with sp.Fori(0, NT) as t:
                            sp.wait_ge(L["ev"], k * NT + t + 1)
                            sp.dma_start(win[0][:, :], dest_tab[bass.ds(t * P, P), :]).then_inc(L["win"], 16)
                sp.sem_inc(S["end"], 1)

            def gathers(s, done):
                for t in range(BT):
                    nc.gpsimd.indirect_dma_start(nrow[s][:, t, :], None, node_tab, bass.IndirectOffsetOnAxis(
                        ap=idx[s][:, t:t + 1], axis=0)).then_inc(done, 16)

            @b.gpsimd
            def _(pool):
                with pool.Fori(0, FI) as i:
                    for s in range(SETS):
                        pool.wait_ge(S["idx"], i * SETS + s + 1)
                        pool.nop(nofuse=True)
                        gathers(s, gath[s])
                left = pool.value_load(ed["left_i"][0:1, 0:1], min_val=0, max_val=1)
                with pool.If(left > 0):
                    with pool.Fori(0, FG) as k:
                        pool.wait_ge(L["idx"], k + 1)
                        pool.nop(nofuse=True)
                        gathers(0, L["gath"])
                pool.sem_inc(S["end"], 1)

            @b.scalar
            def _(act):
                A = nc.scalar

                def stage(k, s, done):
                    A.activation(idx[s][:, :], ed["src_i"][:, bass.ds(k * BT, BT)], ACT.Copy).then_inc(done, 1)

                def window(k, s):
                    w = act.value_load(ed["win_i"][0:1, bass.ds(k, 1)], min_val=0, max_val=N)
                    act.dma_start(win[s][:, :], dest_tab[bass.ds(w, WIN), :]).then_inc(winl[s], 16)

                def turned(k, s):
                    act.wait_ge(S["t"], k + 1)
                    act.wait_ge(S["ad"], k + SETS - 1)
                    A.activation(oh_t[s % 2][:, :, :].rearrange("p t e -> p (t e)"), ps_t[:, :],
                                 ACT.Copy).then_inc(S["tcopy"], 1)

                def weights(k, s):
                    act.wait_ge(S["z"], k + 2)
                    A.activation(val[s][:, :, HE:VAL], z[s][:, :, :], ACT.Exp).then_inc(S["e"], 1)

                def gelu(n, e):
                    act.wait_ge(S["h"], n + 1)
                    act.wait_ge(S["ymm"], n + 1)
                    for f in range(FC):
                        last = A.activation(hid[e % 2][:, f, :], ps_h[e % 2][:, f * P:(f + 1) * P], ACT.Gelu,
                                            bias=b1[:, e * FC + f:e * FC + f + 1])
                    last.then_inc(S["hh"], 1)

                def body(i, experts, last=False):
                    for s in range(SETS):
                        k = i * SETS + s
                        if not last or s + 3 < SETS:
                            act.wait_ge(S["val"], k + 1)
                            act.wait_ge(S["ad"], k + SETS)
                            stage(k + 3, (s + 3) % SETS, S["idx"])
                            window(k + 3, (s + 3) % SETS)
                        if experts:
                            gelu(k, s)
                        if not last or s + 2 < SETS:
                            turned(k + 2, (s + 2) % SETS)
                        if not last or s + 1 < SETS:
                            weights(k + 1, (s + 1) % SETS)

                for k in range(3):
                    stage(k, k, S["idx"])
                    window(k, k)
                act.wait_ge(S["w"], W_LOADS)
                turned(0, 0)
                turned(1, 1)
                weights(0, 0)
                with act.Fori(0, NT) as i:
                    body(i, True)
                body(FI - 1, False, True)

                left = act.value_load(ed["left_i"][0:1, 0:1], min_val=0, max_val=1)
                with act.If(left > 0):
                    with act.Fori(0, FG) as k:
                        act.wait_ge(L["ev"], k * NT + 1)
                        stage(k, 0, L["idx"])
                        with act.Fori(0, NT) as t:
                            act.wait_ge(L["t"], k * NT + t + 1)
                            A.activation(oh_t[0][:, :, :].rearrange("p t e -> p (t e)"), ps_t[:, :],
                                         ACT.Copy).then_inc(L["tcopy"], 1)
                            act.wait_ge(L["z"], k * NT + t + 1)
                            A.activation(val[0][:, :, HE:VAL], z[0][:, :, :], ACT.Exp).then_inc(L["e"], 1)
                act.sem_inc(S["end"], 1)

            @b.vector
            def _(dve):
                v = nc.vector
                dve.sem_inc(S["y"], 2)
                dve.sem_inc(S["val"], 1)
                dve.sem_inc(S["z"], 1)
                v.memset(sums[:, :], 0.0).then_inc(S["ev"], 2)

                def onehots(k, s):
                    dve.wait_ge(S["used"], k + 1)
                    for t in range(BT):
                        last = v.tensor_scalar(oh[s][:, t, :], iota[:, :], ed["rel"][:, bass.ds(k * BT + t, 1)], None,
                                               ALU.is_equal)
                    last.then_inc(S["oh"], 1)

                def exponents(s, chain, n, done):
                    zz = z[s][:, :, :]
                    dest = ps_ad[:, 0:BT * 2 * HEADS].rearrange("p (t h) -> p t h", t=BT)
                    v.tensor_tensor(zz, nrow[s][:, :, 0:HEADS], dest[:, :, 0:HEADS], ALU.add).then_inc(chain, 1)
                    dve.wait_ge(chain, n * 3 + 1)
                    v.scalar_tensor_tensor(zz, zz, 0.2, zz, ALU.mult, ALU.max).then_inc(chain, 1)
                    dve.wait_ge(chain, n * 3 + 2)
                    v.tensor_tensor(zz, zz, dest[:, :, HEADS:2 * HEADS], ALU.subtract).then_inc(chain, 1)
                    dve.wait_ge(chain, n * 3 + 3)
                    v.tensor_scalar(zz, zz, 0.0, None, ALU.min).then_inc(done, 1)

                def weighted(s, done):
                    v.tensor_tensor(val[s][:, :, 0:HE].rearrange("p t (h e) -> p t h e", h=HEADS),
                                    nrow[s][:, :, HEADS:VAL].rearrange("p t (h e) -> p t h e", h=HEADS),
                                    val[s][:, :, HE:VAL].unsqueeze(3).to_broadcast([P, BT, HEADS, NE]),
                                    ALU.mult).then_inc(done, 1)

                def evacuate(k, s):
                    dve.wait_ge(S["used"], k + SETS + 1)
                    dve.wait_ge(S["ev"], k + 2)
                    w = dve.value_load(ed["win_i"][0:1, bass.ds(k, 1)], min_val=0, max_val=N)
                    to = sums[:, bass.ds(w, WIN)]
                    v.tensor_tensor(to, to, ps_sum[s % 2][0:VAL, 0:WIN], ALU.add).then_inc(S["ev"], 1)

                def output(n, e):
                    dve.wait_ge(S["ymm"], n + 3)
                    dve.wait_ge(S["yfree"], n + 1)
                    v.tensor_tensor(y_sb[:, e, :], ps_y[e % 2][:, 0:D], b2[:, e, :], ALU.add).then_inc(S["y"], 1)

                def group_exponents(i, k, s):
                    dve.wait_ge(gath[s], (i + 1) * (16 * BT))
                    dve.wait_ge(S["ad"], k + SETS + 1)
                    exponents(s, S["ch"], k, S["z"])

                def body(i, experts, first=False, last=False):
                    for s in range(SETS):
                        k = i * SETS + s
                        dve.wait_ge(S["e"], k + 1)
                        weighted(s, S["val"])
                        if not last or s + 3 < SETS:
                            onehots(k + 3, (s + 3) % SETS)
                        if not first or s > 0:
                            evacuate(k - 1, (s - 1) % SETS)
                            if experts or s == 0:
                                output(k - 1, (s - 1) % NE)
                        if not last or s + 1 < SETS:
                            group_exponents(i if s + 1 < SETS else i + 1, k + 1, (s + 1) % SETS)

                for k in range(3):
                    onehots(k, k)
                dve.wait_ge(S["w"], W_LOADS)
                group_exponents(0, 0, 0)
                body(0, True, first=True)
                with dve.Fori(1, NT) as i:
                    body(i, True)
                body(FI - 1, False, last=True)
                evacuate(FM - 1, SETS - 1)

                left = dve.value_load(ed["left_i"][0:1, 0:1], min_val=0, max_val=1)
                with dve.If(left > 0):
                    dve.wait_ge(S["ev"], FM + 2)
                    dve.sem_inc(L["ev"], 1)
                    with dve.Fori(0, FG) as k:
                        with dve.Fori(0, NT) as t:
                            n = k * NT + t
                            dve.wait_ge(L["ev"], n + 1)
                            v.tensor_scalar(left_rel[:, :], ed["left"][:, bass.ds(k * BT, BT)],
                                            tile_base[:, bass.ds(t, 1)], None, ALU.subtract).then_inc(L["oh"], 1)
                            dve.wait_ge(L["oh"], n * 2 + 1)
                            for j in range(BT):
                                last = v.tensor_scalar(oh[0][:, j, :], iota[:, :], left_rel[:, j:j + 1], None, ALU.is_equal)
                            last.then_inc(L["oh"], 1)
                            dve.wait_ge(L["gath"], (k + 1) * (16 * BT))
                            dve.wait_ge(L["ad"], n + 1)
                            exponents(0, L["zc"], n, L["z"])
                            dve.wait_ge(L["e"], n + 1)
                            weighted(0, L["val"])
                            dve.wait_ge(L["sum"], n + 1)
                            to = sums[:, bass.ds(t * P, P)]
                            v.tensor_tensor(to, to, ps_sum[0][0:VAL, 0:WIN], ALU.add).then_inc(L["ev"], 1)
                dve.sem_inc(S["end"], 1)

            @b.tensor
            def _(pe):
                mm = nc.tensor.matmul
                pe.sem_inc(S["used"], SETS)
                pe.sem_inc(S["ad"], SETS)
                pe.sem_inc(S["tcopy"], 1)
                pe.sem_inc(S["hh"], 2)
                pe.sem_inc(S["ymm"], 2)

                def turn(s, done):
                    for t in range(BT):
                        last = nc.tensor.transpose(ps_t[:, t * P:(t + 1) * P], oh[s][:, t, :], ident[:, :])
                    last.then_inc(done, 1)

                def destinations(s, half, done):
                    W = 2 * HEADS
                    for t in range(BT):
                        last = mm(ps_ad[:, t * W:(t + 1) * W], oh_t[half][:, t, :], win[s][:, :], start=True, stop=True,
                                  skip_group_check=True)
                    last.then_inc(done, 1)

                def add_up(s, half, done):
                    for t in range(BT):
                        last = mm(ps_sum[half][0:VAL, 0:WIN], val[s][:, t, :], oh[s][:, t, :], start=(t == 0),
                                  stop=(t == BT - 1), skip_group_check=True)
                    last.then_inc(done, 1)

                def group_turn(k, s):
                    pe.wait_ge(S["oh"], k + 1)
                    pe.wait_ge(S["tcopy"], k + 1)
                    turn(s, S["t"])

                def group_destinations(i, k, s):
                    pe.wait_ge(S["tcopy"], k + 2)
                    pe.wait_ge(winl[s], (i + 1) * 16)
                    pe.wait_ge(S["z"], k + 1)
                    destinations(s, s % 2, S["ad"])

                def group_sums(k, s):
                    pe.wait_ge(S["val"], k + 2)
                    pe.wait_ge(S["ev"], k + 1)
                    add_up(s, s % 2, S["used"])

                def up(i, n, e):
                    pe.wait_ge(S["hh"], n + 1)
                    for f in range(FC):
                        for h in range(DC):
                            last = mm(ps_h[e % 2][:, f * P:(f + 1) * P], w1[:, h, e, f * P:(f + 1) * P],
                                      xt[:, h, bass.ds(i * P, P)], start=(h == 0), stop=(h == DC - 1), skip_group_check=True)
                    last.then_inc(S["h"], 1)

                def down(n, e):
                    pe.wait_ge(S["hh"], n + 3)
                    pe.wait_ge(S["y"], n + 1)
                    for f in range(FC):
                        last = mm(ps_y[e % 2][:, 0:D], hid[e % 2][:, f, :], w2[:, e, f, :], start=(f == 0),
                                  stop=(f == FC - 1), skip_group_check=True)
                    last.then_inc(S["ymm"], 1)

                def body(i, experts, first=False, last=False):
                    for s in range(SETS):
                        k = i * SETS + s
                        if experts:
                            up(i, k, s)
                        if (experts or s == 0) and not (first and s == 0):
                            down(k - 1, (s - 1) % NE)
                        if not last or s + 2 < SETS:
                            group_turn(k + 2, (s + 2) % SETS)
                        if not last or s + 1 < SETS:
                            group_destinations(i if s + 1 < SETS else i + 1, k + 1, (s + 1) % SETS)
                        group_sums(k, s)

                pe.wait_ge(S["w"], W_LOADS)
                group_turn(0, 0)
                group_turn(1, 1)
                group_destinations(0, 0, 0)
                body(0, True, first=True)
                with pe.Fori(1, NT) as i:
                    body(i, True)
                body(FI - 1, False, last=True)

                left = pe.value_load(ed["left_i"][0:1, 0:1], min_val=0, max_val=1)
                with pe.If(left > 0):
                    with pe.Fori(0, FG) as k:
                        with pe.Fori(0, NT) as t:
                            n = k * NT + t
                            pe.wait_ge(L["oh"], n * 2 + 2)
                            turn(0, L["t"])
                            pe.wait_ge(L["tcopy"], n + 1)
                            pe.wait_ge(L["win"], (n + 1) * 16)
                            destinations(0, 0, L["ad"])
                            pe.wait_ge(L["val"], n + 1)
                            add_up(0, 0, L["sum"])
                pe.sem_inc(S["end"], 1)

        route(nc, c, sb, pb, sem, sums, node, ident, y_dram, x1_dram, b_gat, ln_gamma, ln_beta, out)


def route(nc, c, sb, pb, sem, sums, node, ident, y_dram, x1_dram, b_gat, ln_gamma, ln_beta, out):
    F = 7
    S = sb("S", [P, NT, VAL])
    tmp = sb("r_tmp", [P, NT, HE])
    par = sb("r_par", [P, 3, HE])
    den = sb("r_den", [P, NT, HEADS])
    mean = sb("r_mean", [P, NT, 3])
    sc = sb("r_sc", [P, NT, NE])
    cnt = sb("r_cnt", [P, NT, NE])
    gt = sb("r_gt", [P, NT, NE])
    gate = sb("r_gate", [P, NT, NE])
    yb = [sb(f"yb{s}", [P, NE * D]) for s in range(F)]
    xb = [sb(f"xb{s}", [P, D]) for s in range(F)]
    PB = 512 // VAL
    ps = [pb(f"ps_r{i}") for i in range(-(-NT // PB))]
    r_par, r_ch, r_tr, r_act, r_actd = (sem(f"r_{n}") for n in ("parl", "ch", "tr", "act", "actd"))
    r_in = [sem(f"r_in{s}") for s in range(F)]
    r_out = [sem(f"r_out{s}") for s in range(F)]
    r_free, r_add = sem("r_free"), sem("r_add")
    b = c.enter_context(nc.Block())

    @b.sync
    def _(sp):
        for n, a in enumerate((b_gat, ln_gamma, ln_beta)):
            sp.dma_start(par[:, n, :], a.partition_broadcast(P)).then_inc(r_par, 16)
        sp.sem_inc(r_free, F)

        def body(i):
            for s in range(F):
                t = i * F + s
                sp.wait_ge(r_free, t + 1)
                sp.dma_start(yb[s][:, :], y_dram[bass.ds(t, 1), :, :].rearrange("a p d -> (a p) d")).then_inc(r_in[s], 16)
                sp.dma_start(xb[s][:, :], x1_dram[bass.ds(t, 1), :, :].rearrange("a p d -> (a p) d")).then_inc(r_in[s], 16)
        with sp.Fori(0, NT // F) as i:
            body(i)

    @b.scalar
    def _(act):
        act.wait_ge(r_act, 1)
        nc.scalar.activation(mean[:, :, 2], mean[:, :, 1], ACT.Sqrt).then_inc(r_actd, 1)
        act.wait_ge(r_act, 2)
        nc.scalar.activation(gate[:, :, :], sc[:, :, :], ACT.Exp).then_inc(r_actd, 1)

        def store(i, s, last=False):
            t = i * F + s
            act.wait_ge(r_add, i * (F * NE) + (NE - 1) * F + s + 1)
            n = NREST if last else P
            act.dma_start(out[bass.ds(t * P, n), :], xb[s][0:n, :]).then_inc(r_out[s], 16)
            act.wait_ge(r_out[s], (i + 1) * 16)
            act.sem_inc(r_free, 1)
        with act.Fori(0, NT // F - 1) as i:
            for s in range(F):
                store(i, s)
        for s in range(F):
            store(NT // F - 1, s, s == F - 1)

    @b.tensor
    def _(pe):
        for t in range(NT):
            last = nc.tensor.transpose(ps[t // PB][:, (t % PB) * VAL:(t % PB + 1) * VAL], sums[:, t * P:(t + 1) * P],
                                       ident[0:VAL, 0:VAL])
            if t % PB == PB - 1 or t == NT - 1:
                last.then_inc(r_tr, 1)

    @b.vector
    def _(dve):
        v = nc.vector
        step = Chain(dve, r_ch)
        for i, bank in enumerate(ps):
            n = min(PB, NT - i * PB)
            dve.wait_ge(r_tr, i + 1)
            step(v.tensor_copy(S[:, i * PB:i * PB + n, :], bank[:, 0:n * VAL].rearrange("p (t v) -> p t v", v=VAL)))
        dve.wait_ge(r_par, 48)
        e_self, h = node["e_self"], node["h"]
        bc = lambda a: a.unsqueeze(3).to_broadcast([P, NT, HEADS, NE])
        four = lambda a: a.rearrange("p t (h e) -> p t h e", h=HEADS)
        step(v.tensor_tensor(four(tmp[:, :, :]), four(h[:, :, :]), bc(e_self[:, :, :]), ALU.mult))
        step(v.tensor_tensor(tmp[:, :, :], tmp[:, :, :], S[:, 0:NT, 0:HE], ALU.add))
        step(v.scalar_tensor_tensor(den[:, :, :], e_self[:, :, :], 1e-16, S[:, 0:NT, HE:VAL], ALU.add, ALU.add))
        step(v.reciprocal(den[:, :, :], den[:, :, :]))
        step(v.tensor_tensor(four(tmp[:, :, :]), four(tmp[:, :, :]), bc(den[:, :, :]), ALU.mult))
        pbc = lambda n: par[:, n, :].unsqueeze(1).to_broadcast([P, NT, HE])
        step(v.tensor_tensor(tmp[:, :, :], tmp[:, :, :], pbc(0), ALU.add))
        mb = lambda n: mean[:, :, n].unsqueeze(2).to_broadcast([P, NT, HE])
        agg = S[:, 0:NT, 0:HE]
        step(v.tensor_reduce(mean[:, :, 0], tmp[:, :, :], AX, ALU.add))
        step(v.tensor_scalar(mean[:, :, 0], mean[:, :, 0], 1.0 / HE, None, ALU.mult))
        step(v.tensor_tensor(tmp[:, :, :], tmp[:, :, :], mb(0), ALU.subtract))
        step(v.tensor_tensor(agg, tmp[:, :, :], tmp[:, :, :], ALU.mult))
        step(v.tensor_reduce(mean[:, :, 1], agg, AX, ALU.add))
        step(v.tensor_scalar(mean[:, :, 1], mean[:, :, 1], 1.0 / HE, EPS, ALU.mult, ALU.add))
        dve.sem_inc(r_act, 1)
        dve.wait_ge(r_actd, 1)
        step(v.reciprocal(mean[:, :, 1], mean[:, :, 2]))
        step(v.tensor_tensor(tmp[:, :, :], tmp[:, :, :], mb(1), ALU.mult))
        step(v.tensor_tensor(tmp[:, :, :], tmp[:, :, :], pbc(1), ALU.mult))
        step(v.tensor_tensor(tmp[:, :, :], tmp[:, :, :], pbc(2), ALU.add))
        step(v.tensor_reduce(sc[:, :, :], tmp[:, :, :].rearrange("p t (h e) -> p t e h", h=HEADS), AX, ALU.add))
        step(v.tensor_scalar(sc[:, :, :], sc[:, :, :], 1.0 / HEADS, None, ALU.mult))
        step(v.memset(cnt[:, :, :], 0.0))
        for e in range(NE):
            for o in range(NE):
                if o == e:
                    continue
                step(v.tensor_tensor(gt[:, :, 0], sc[:, :, o], sc[:, :, e], ALU.is_ge if o < e else ALU.is_gt))
                step(v.tensor_tensor(cnt[:, :, e], cnt[:, :, e], gt[:, :, 0], ALU.add))
        step(v.tensor_scalar(cnt[:, :, :], cnt[:, :, :], 2.0, None, ALU.is_lt))
        step(v.tensor_reduce(mean[:, :, 0], sc[:, :, :], AX, ALU.max))
        step(v.tensor_tensor(sc[:, :, :], sc[:, :, :], mean[:, :, 0].unsqueeze(2).to_broadcast([P, NT, NE]), ALU.subtract))
        dve.sem_inc(r_act, 1)
        dve.wait_ge(r_actd, 2)
        step(v.tensor_tensor(gate[:, :, :], gate[:, :, :], cnt[:, :, :], ALU.mult))
        step(v.tensor_reduce(mean[:, :, 0], gate[:, :, :], AX, ALU.add))
        step(v.reciprocal(mean[:, :, 1], mean[:, :, 0]))
        step(v.tensor_tensor(gate[:, :, :], gate[:, :, :], mean[:, :, 1].unsqueeze(2).to_broadcast([P, NT, NE]), ALU.mult))

        with dve.Fori(0, NT // F) as i:
            for s in range(F):
                dve.wait_ge(r_in[s], (i + 1) * 32)
            for e in range(NE):
                for s in range(F):
                    n = i * (F * NE) + e * F + s
                    if e > 0:
                        dve.wait_ge(r_add, n - F + 1)
                    v.scalar_tensor_tensor(xb[s][:, :], yb[s][:, e * D:(e + 1) * D],
                                           gate[:, bass.ds(i * F + s, 1), e], xb[s][:, :], ALU.mult, ALU.add
                                           ).then_inc(r_add, 1)


_OUTS = [((N, D), "float32")]


def kernel(**inputs):
    import numpy as _np
    import concourse.bacc as _bacc
    from concourse import mybir as _mybir
    from concourse.bass_utils import run_bass_kernel_spmd as _run

    a = {k: _np.asarray(v) for k, v in inputs.items()}
    cut = EFULL * P
    edge = a["L0_ffn_edge_index"]

    def by_tile(e):
        return _np.ascontiguousarray(e[:cut].reshape(EFULL, P).T), e[cut:].reshape(EREST, 1)

    src, src_rest = by_tile(a["src"])
    dst, dst_rest = by_tile(a["dst"])
    arrays = dict(
        x=a["x"], src=src, src_rest=src_rest, dst=dst, dst_rest=dst_rest,
        w1=a["L0_gnn_W1"], b1=a["L0_gnn_b1"], w2=a["L0_gnn_W2"], b2=a["L0_gnn_b2"],
        w_gat=a["L0_ffn_W_gat"], att_src=a["L0_ffn_att_src"], att_dst=a["L0_ffn_att_dst"],
        b_gat=a["L0_ffn_b_gat"], ln_gamma=a["L0_ffn_ln_gamma"], ln_beta=a["L0_ffn_ln_beta"],
        ew1=a["L0_ffn_W1"], eb1=a["L0_ffn_b1"], ew2=a["L0_ffn_W2"], eb2=a["L0_ffn_b2"],
        esrc=edge[0].reshape(P, FT), edst=edge[1].reshape(P, FT),
    )
    nc = _bacc.Bacc("TRN2", target_bir_lowering=False, num_devices=1)
    ins, args = {}, []
    for name, v in arrays.items():
        v = _np.ascontiguousarray(v)
        ins[f"in_{name}"] = v
        args.append(nc.dram_tensor(f"in_{name}", v.shape, _mybir.dt.from_np(v.dtype), kind="ExternalInput").ap())
    for i, (shape, dtype) in enumerate(_OUTS):
        args.append(nc.dram_tensor(f"out_{i}", shape, _mybir.dt.from_np(_np.dtype(dtype)), kind="ExternalOutput").ap())
    program(nc, *args)
    r = _run(nc, [ins], core_ids=[0])
    return r.results[0]["out_0"]
```

```python
import concourse.bass as bass
from concourse import mybir
from contextlib import ExitStack

F32, BF16, I32 = mybir.dt.float32, mybir.dt.bfloat16, mybir.dt.int32
ALU = mybir.AluOpType
ACT = mybir.ActivationFunctionType
AX = mybir.AxisListType.X
RMAX = bass.bass_isa.ReduceOp.max

P = 128
N = 6250
D = 256
DC = D // P
NT = (N + P - 1) // P
NFULL = N // P
NREST = N - NFULL * P

E = 100000
ET = (E + P - 1) // P
EFULL = E // P
EREST = E - EFULL * P
GT = 4
SETS = 4
NG = -(-ET // GT)
NG += -NG % SETS
NGP = NG + 1
HT = 16
WIN = P
AGGC = N + WIN + (-(N + WIN)) % P

EF = 131072
FT = EF // P
HEADS, NE = 4, 4
HE = HEADS * NE
HID = 512
FC = HID // P
PIECES = 3
VAL = HE + HEADS
BT = 4
FG = FT // BT
ST = 2
TT = ST * BT
FSTEPS = FT // TT
STEPS = 2 * NT + 1
FI = STEPS // SETS
TAIL = STEPS - FI * SETS
FM = STEPS * ST
KEEP = NT - NT // 4 * 3
NOUT = NT - KEEP
BITS = 13
WORD = 0x40000000
EPS = 1e-5
WIDE = 16.0
NEG = -1.0e30
CAP = 32.0


def program(nc, x, src, src_rest, dst, dst_rest, w1, b1, w2, b2, w_gat, att_src, att_dst, b_gat,
            ln_gamma, ln_beta, ew1, eb1, ew2, eb2, esrc, edst, out):
    table1 = nc.dram_tensor("table1", (NT * P, D), F32).ap()
    table2 = nc.dram_tensor("table2", (NT * P, D), F32).ap()
    node_tab = nc.dram_tensor("node_tab", (NT * P, VAL), F32).ap()
    dest_tab = nc.dram_tensor("dest_tab", (AGGC, PIECES * 2 * HEADS), BF16).ap()
    yx_dram = nc.dram_tensor("yx_dram", (NT, P, (NE + 1) * D), F32).ap()

    with ExitStack() as top:
        def sb(name, shape, dt=F32, ctx=top):
            return ctx.enter_context(nc.sbuf_tensor(name, shape, dt))

        ident = sb("ident", [P, P])
        iota = sb("iota", [P, P])
        tile_base = sb("tile_base", [P, NT])
        iota_bf = sb("iota_bf", [P, P], BF16)
        expert = dict(w1=sb("ew1_sb", [P, DC, NE, HID]), w2=sb("ew2_sb", [P, NE, FC, D]),
                      b1=sb("eb1_sb", [P, NE * FC]), b2=sb("eb2_sb", [P, NE, D]))
        ed = dict(
            src_i=sb("esrc_i", [P, FT], I32), win_i=sb("ewin_i", [1, FG], I32),
            rel=sb("erel", [P, FT]), left=sb("eleft", [P, FT]), left_i=sb("eleft_i", [P, 1], I32))
        agg = sb("agg", [P, DC, AGGC])
        node = dict(as_=sb("as_", [P, NT, HEADS]), ad=sb("ad", [P, NT, 2, HEADS]),
                    h=sb("h", [P, NT, HE]), e_self=sb("e_self", [P, NT, HEADS]),
                    top=sb("top", [P, 2, 2, HEADS]), wide_i=sb("wide_i", [P, 1], I32))
        with ExitStack() as nodes:
            x_sb = sb("x_sb", [P, NT, D], F32, nodes)
            with ExitStack() as gnn:
                def gb(name, shape, dt=F32):
                    return sb(name, shape, dt, gnn)
                room = [expert["w1"][:, :, :, :].rearrange("p c e f -> p (c e f)"),
                        expert["w2"][:, :, :, :].rearrange("p e c d -> p (e c d)")]
                used = [0, 0]

                def at(i, n):
                    used[i] += n
                    return room[i][:, used[i] - n:used[i]]
                g = dict(
                    nc=nc, x=x, x_sb=x_sb, ident=ident, iota=iota, table1=table1, table2=table2, agg=agg,
                    src_f=at(0, NG * GT),
                    dst_i=gb("dst_i", [P, NG * GT], I32),
                    dst_left=at(1, NG * GT),
                    rel=at(0, NGP * GT),
                    dst_hi=at(1, NGP * GT),
                    dst_lo=at(1, NGP * GT),
                    iota_bf=iota_bf,
                    tile_base=tile_base,
                    left_i=gb("left_i", [P, 1], I32),
                    rs_out=gb("rs_out", [P, NT]),
                    rs_in=gb("rs_in", [P, NT]),
                    w=[at(1, DC * D).rearrange("p (c n) -> p c n", c=DC) for _ in range(2)],
                    b=[gb("b_1", [P, D]), gb("b_2", [P, D])],
                    ed=ed,
                )
                key = [at(0, FT), at(0, FT)]
                odd = gb("odd_row", [P, 2])
                g.update(key=key, odd=odd)
                prologue(g, src, src_rest, dst, dst_rest, (w1, w2), (b1, b2), esrc, edst)
                aggregate(g, 1)
                transform(g)
                aggregate(g, 2)
                finish_nodes(g, node, node_tab, dest_tab, yx_dram, w_gat, att_src, att_dst,
                             expert, (ew1, eb1, ew2, eb2))
        own_guards(nc, node, ident, iota, tile_base, ed, node_tab, dest_tab)
        gat_edges(nc, agg, node, ident, iota_bf, tile_base, ed, node_tab, dest_tab, yx_dram,
                  b_gat, ln_gamma, ln_beta, expert, out)


class Chain:

    def __init__(self, eng, sem):
        self.eng, self.sem, self.n = eng, sem, 0

    def __call__(self, ins):
        self.n += 1
        ins.then_inc(self.sem, 1)
        self.eng.wait_ge(self.sem, self.n)


def split(v, step, value, pieces, rest):
    step(v.tensor_copy(pieces(0), value))
    step(v.tensor_tensor(rest, value, pieces(0), ALU.subtract))
    step(v.tensor_copy(pieces(1), rest))
    step(v.tensor_tensor(pieces(2), rest, pieces(1), ALU.subtract))


def mark_left(v, step, rel, left, tmp, far, far_max, n_main=None):
    step(v.tensor_scalar(tmp, rel, 0.0, None, ALU.is_lt))
    step(v.scalar_tensor_tensor(far, rel, float(WIN - 1), tmp, ALU.is_gt, ALU.max))
    if n_main is not None:
        step(v.memset(far[:, n_main:], 1.0))
    step(v.tensor_scalar(tmp, left, 0.0, None, ALU.is_ge))
    step(v.tensor_tensor(far, far, tmp, ALU.mult))
    step(v.tensor_scalar(tmp, left, float(N), None, ALU.is_lt))
    step(v.tensor_tensor(far, far, tmp, ALU.mult))
    step(v.scalar_tensor_tensor(tmp, left, 1.0, far, ALU.add, ALU.mult))
    step(v.tensor_scalar(left, tmp, -1.0, None, ALU.add))
    step(v.tensor_reduce(far_max, far, AX, ALU.max))


def semaphores(nc, c):
    mine = []

    def sem(name):
        mine.append(nc.alloc_semaphore(name))
        return mine[-1]
    def clear():
        nc.clear_and_free_semaphores(mine)
        nc.all_engine_barrier()
    c.callback(clear)
    return sem


class Sorter:
    COL = FT.bit_length() - 1
    ROW = P.bit_length() - 1
    LEVELS = COL + ROW
    BLK = FT // P
    CHANGES = 2 * ROW + 1

    def __init__(self, nc, key, odd, pb, sem, ident):
        self.nc, self.ident, self.key, self.odd = nc, ident, key, odd
        self.ps = [pb(f"ps_sort{i}") for i in range(2)]
        self.stage_done = sem("sort_stage")
        self.ready = sem("sort_ready")
        self.turned = sem("sort_turned")


    def vector_steps(self, dve):
        v, key = self.nc.vector, self.key
        count, cur, changes = 0, 0, 0

        def wait():
            dve.wait_ge(self.stage_done, count)

        def halves(buf, j):
            a = buf[:, :].rearrange("p (a two b) -> p a two b", two=2, b=1 << j)
            return a[:, :, 0, :], a[:, :, 1, :]

        def exchange(j):
            nonlocal count, cur
            lo, hi = halves(key[cur], j)
            to_lo, to_hi = halves(key[1 - cur], j)
            v.tensor_tensor(to_lo, lo, hi, ALU.min)
            v.tensor_tensor(to_hi, lo, hi, ALU.max).then_inc(self.stage_done, 1)
            count += 1
            cur = 1 - cur
            wait()

        def negate(*parts):
            nonlocal count
            for part, by in parts:
                last = v.tensor_scalar(part, part, by, None, ALU.mult)
            last.then_inc(self.stage_done, 1)
            count += 1
            wait()

        def flips(buf, bit):
            return buf[:, :].rearrange("p (a four b) -> p a four b", four=4, b=1 << bit)[:, :, 1:3, :]

        def change():
            nonlocal changes, cur, count
            dve.sem_inc(self.ready, 1)
            cur = 1 - cur
            for i, half in enumerate(self.ps):
                dve.wait_ge(self.turned, 2 * changes + i + 1)
                last = v.tensor_copy(key[cur][:, i * 512:(i + 1) * 512], half[:, :])
            last.then_inc(self.stage_done, 1)
            count += 1
            changes += 1
            wait()

        negate((halves(key[0], 1)[1], -1.0))
        for level in range(1, self.COL + 1):
            for j in reversed(range(level)):
                exchange(j)
                yield
            if level < self.COL - 1:
                negate((flips(key[cur], level), -1.0))
            elif level == self.COL - 1:
                lo, hi = halves(key[cur], level)
                negate((lo, self.odd[:, 0:1]), (hi, self.odd[:, 1:2]))
        for level in range(self.COL + 1, self.LEVELS + 1):
            change()
            shift = P.bit_length() - 1
            rows = key[cur][:, :].rearrange("q (r p) -> q r p", p=P)

            def row_bits(four, b):
                return key[cur][:, :].rearrange("q (a four b) -> q a four b", four=four, b=b)
            if level < self.LEVELS:
                negate((row_bits(4, 1 << (level - 1 - self.COL))[:, :, 1:3, :], -1.0))
            else:
                negate((row_bits(2, P // 2)[:, :, 1, :], -1.0))
            for j in reversed(range(shift, level)):
                exchange(j - self.COL if j >= self.COL else j - shift + self.ROW)
                yield
            change()
            for j in reversed(range(shift)):
                exchange(j)
                yield
        change()
        self.result = key[cur]


    def transposes(self, pe, n):
        src = self.key[self.source(n)]
        pe.wait_ge(self.ready, n + 1)
        for r in range(self.BLK):
            half = self.BLK // 2
            last = self.nc.tensor.transpose(self.ps[r // half][:, (r % half) * P:(r % half + 1) * P],
                                            src[:, r * P:(r + 1) * P], self.ident[:, :])
            if r % half == half - 1:
                last.then_inc(self.turned, 1)

    def before(self, n):
        exchanges = self.COL * (self.COL + 1) // 2
        for c in range(1, n + 1):
            level = self.COL + 1 + (c - 1) // 2
            exchanges += level - self.ROW if c % 2 else self.ROW
        return exchanges

    def source(self, n):
        return (self.before(n) + n) % 2


def prologue(g, src, src_rest, dst, dst_rest, ws, bs, esrc, edst):
    nc, x_sb, iota, ident = g["nc"], g["x_sb"], g["iota"], g["ident"]
    src_f, dst_i, rel, dst_left = g["src_f"], g["dst_i"], g["rel"], g["dst_left"]
    with ExitStack() as c:
        def sb(name, shape, dt=F32):
            return c.enter_context(nc.sbuf_tensor(name, shape, dt))
        sem = semaphores(nc, c)
        EC = NG * GT
        src_i = sb("src_i", [P, EC], I32)
        key_i = sb("key_i", [P, EC], I32)
        src_hi = sb("src_hi", [P, EC], BF16)
        src_lo = sb("src_lo", [P, EC], BF16)
        tmp = sb("tmp_f", [P, EC])
        far = sb("far", [P, EC])
        far_max = sb("far_max", [P, 2])
        row_no = sb("row_no", [P, 1])
        esrc_i = g["ed"]["src_i"]
        edst_i = g["ed"]["rel"][:, :].bitcast(I32)
        ones = sb("ones", [1, P])
        row_f = sb("row_f", [1, NG])
        iota_t = sb("iota_t", [P, P, HT], BF16)
        oh_lo = [sb(f"oh_lo{s}", [P, P, HT], BF16) for s in range(2)]
        oh_hi = [sb(f"oh_hi{s}", [P, NT, HT], BF16) for s in range(2)]
        zero = sb("zero", [P, P], BF16)
        scrap = sb("scrap", [P, 2, D])
        mean = sb("mean", [P, NT])
        var = sb("var", [P, NT])
        scale = sb("scale", [P, NT])
        shift = sb("shift", [P, NT])
        root = sb("root", [P, NT])
        table = g["agg"][:, :, :].rearrange("p c n -> p (c n)")[:, 0:NT * D].rearrange("p (t d) -> p t d", d=D)
        ps_deg = c.enter_context(nc.psum_tensor("ps_deg", [P, 512], F32))
        ps_win = c.enter_context(nc.psum_tensor("ps_win", [P, 512], F32))
        names = ("fill", "src", "dst", "fedges", "x", "w", "iota", "iota2", "ch", "keys", "win", "oh", "used",
                 "sum", "mean", "var", "sd", "deg", "sdeg", "ab", "ta", "tv", "tst", "far", "farall")
        S = {n: sem("s_" + n) for n in names}
        b = c.enter_context(nc.Block())
        NH = EC // HT
        TS = 7
        assert NH * HT == EC and NH % 2 == 1 and NT % TS == 0

        @b.sync
        def _(sp):
            sp.wait_ge(S["fill"], 1)
            sp.dma_start(src_i[:, 0:EFULL], src).then_inc(S["src"], 16)
            sp.dma_start(src_i[0:EREST, EFULL:ET], src_rest).then_inc(S["src"], 16)
            sp.dma_start(dst_i[:, 0:EFULL], dst).then_inc(S["dst"], 16)
            sp.dma_start(dst_i[0:EREST, EFULL:ET], dst_rest).then_inc(S["dst"], 16)
            for w_sb, w, b_sb, bias in zip(g["w"], ws, g["b"], bs):
                sp.dma_start(w_sb[:, :, :], w.rearrange("(c p) n -> p c n", p=P)).then_inc(S["w"], 16)
                sp.dma_start(b_sb[:, :], bias.partition_broadcast(P)).then_inc(S["w"], 16)
            sp.dma_start(esrc_i[:, :], esrc).then_inc(S["fedges"], 16)
            sp.dma_start(edst_i[:, :], edst).then_inc(S["fedges"], 16)
            for k in range(NT // TS):
                t = (k + 1) * TS
                sp.wait_ge(S["ta"], t - t // 3)
                sp.wait_ge(S["tv"], t // 3)
                sp.dma_start(g["table1"][k * TS * P:(k + 1) * TS * P, :].rearrange("(t p) d -> p t d", p=P),
                             table[:, k * TS:(k + 1) * TS, :]).then_inc(S["tst"], 16)
            sp.wait_ge(S["tst"], 16 * (NT // TS))
            sp.wait_ge(S["w"], 64)
            sp.wait_ge(S["fedges"], 32)

        @b.gpsimd
        def _(pool):
            nc.gpsimd.iota(iota[:, :], pattern=[[1, P]], base=0, channel_multiplier=0,
                           allow_small_or_imprecise_dtypes=True).then_inc(S["iota"], 1)
            nc.gpsimd.iota(g["tile_base"][:, :], pattern=[[P, NT]], base=0, channel_multiplier=0,
                           allow_small_or_imprecise_dtypes=True).then_inc(S["iota2"], 1)
            nc.gpsimd.iota(row_no[:, :], pattern=[[0, 1]], base=0, channel_multiplier=1,
                           allow_small_or_imprecise_dtypes=True).then_inc(S["iota2"], 1)
            nc.gpsimd.memset(ident[:, :], 0.0).then_inc(S["iota2"], 1)
            pool.wait_ge(S["iota2"], 3)
            nc.gpsimd.affine_select(out=ident[:, :], in_=ident[:, :], compare_op=ALU.not_equal, fill=1.0,
                                    base=0, pattern=[[-1, P]], channel_multiplier=1).then_inc(S["iota2"], 1)
            pool.wait_ge(S["iota2"], 4)
            pool.wait_ge(S["far"], 1)
            nc.gpsimd.partition_all_reduce(far_max[:, 1:2], far_max[:, 0:1], P, RMAX).then_inc(S["farall"], 1)

        @b.vector
        def _(dve):
            v = nc.vector
            step = Chain(dve, S["ch"])
            v.memset(x_sb[:, NFULL, :], 0.0)
            v.memset(src_i[:, EFULL:EC], -1)
            v.memset(dst_i[:, EFULL:EC], -1).then_inc(S["fill"], 1)
            v.memset(zero[:, :], 0.0)
            v.memset(ones[:, :], 1.0)
            v.memset(rel[:, EC:NGP * GT], -1.0)
            v.memset(g["dst_hi"][:, EC:NGP * GT], -1.0)
            step(v.memset(g["dst_lo"][:, EC:NGP * GT], -1.0))
            dve.wait_ge(S["iota"], 1)
            v.tensor_copy(g["iota_bf"][:, :], iota[:, 0:P])
            v.tensor_copy(iota_t[:, :, :], iota[:, :].unsqueeze(2).to_broadcast([P, P, HT]))
            dve.wait_ge(S["src"], 32)

            def keys(raw, hi, lo):
                step(v.tensor_single_scalar(key_i[:, :], raw[:, :], 7, op=ALU.arith_shift_right))
                step(v.tensor_copy(hi, key_i[:, :]))
                step(v.tensor_single_scalar(key_i[:, :], raw[:, :], P - 1, op=ALU.bitwise_and))
                step(v.tensor_copy(lo, key_i[:, :]))

            keys(src_i, src_hi[:, :], src_lo[:, :])

            def onehots(n, s):
                dve.wait_ge(S["used"], n + 1)
                for o, k, size in ((oh_lo[s], src_lo, P), (oh_hi[s], src_hi, NT)):
                    last = v.tensor_tensor(o[:, :, :], iota_t[:, 0:size, :],
                                           k[:, bass.ds(n * HT, HT)].unsqueeze(1).to_broadcast([P, size, HT]), ALU.is_equal)
                last.then_inc(S["oh"], 1)

            with dve.Fori(0, NH // 2) as i:
                for s in range(2):
                    onehots(i * 2 + s, s)
            onehots(NH - 1, 0)
            dve.wait_ge(S["sd"], 1)
            step(v.reciprocal(scale[:, :], root[:, :]))

            dve.wait_ge(S["used"], NH + 2)
            step(v.tensor_scalar(g["rs_out"][:, :], ps_deg[:, 0:NT], 1.0, None, ALU.max))
            dve.sem_inc(S["deg"], 1)
            dve.wait_ge(S["sdeg"], 1)
            step(v.reciprocal(g["rs_out"][:, :], root[:, :]))
            step(v.tensor_tensor(scale[:, :], scale[:, :], g["rs_out"][:, :], ALU.mult))
            step(v.tensor_tensor(shift[:, :], mean[:, :], scale[:, :], ALU.mult))
            dve.sem_inc(S["ab"], 1)
            for t in range(2, NT, 3):
                v.tensor_scalar(table[:, t, :], x_sb[:, t, :], scale[:, t:t + 1], shift[:, t:t + 1],
                                ALU.mult, ALU.add).then_inc(S["tv"], 1)

            dve.wait_ge(S["dst"], 32)
            keys(dst_i, g["dst_hi"][:, 0:EC], g["dst_lo"][:, 0:EC])
            step(v.tensor_copy(dst_left[:, :], dst_i[:, :]))
            step(v.tensor_copy(row_f[:, :], dst_left[0:1, 0:EC:GT]))
            dve.sem_inc(S["keys"], 1)
            dve.wait_ge(S["win"], 1)
            step(v.tensor_tensor(rel[:, 0:EC].rearrange("p (g t) -> p g t", t=GT),
                                 dst_left[:, :].rearrange("p (g t) -> p g t", t=GT),
                                 ps_win[:, 0:NG].unsqueeze(2).to_broadcast([P, NG, GT]), ALU.subtract))
            mark_left(v, step, rel[:, 0:EC], dst_left[:, :], tmp[:, :], far[:, :], far_max[:, 0:1])
            dve.sem_inc(S["far"], 1)
            step(v.tensor_copy(src_f[:, :], src_i[:, :]))
            step(v.tensor_scalar(src_f[:, :], src_f[:, :], 0.0, None, ALU.max))
            dve.wait_ge(S["farall"], 1)
            step(v.tensor_copy(g["left_i"][:, :], far_max[:, 1:2]))

            dve.wait_ge(S["iota2"], 4)
            step(v.tensor_copy(key_i[:, 0:1], row_no[:, :]))
            step(v.tensor_single_scalar(key_i[:, 1:2], key_i[:, 0:1], 1, op=ALU.bitwise_and))
            step(v.tensor_copy(far[:, 0:1], key_i[:, 1:2]))
            step(v.tensor_scalar(g["odd"][:, 0:1], far[:, 0:1], -2.0, 1.0, ALU.mult, ALU.add))
            step(v.tensor_scalar(g["odd"][:, 1:2], far[:, 0:1], 2.0, -1.0, ALU.mult, ALU.add))

        @b.scalar
        def _(act):
            A = nc.scalar
            act.wait_ge(S["fill"], 1)
            half = NFULL // 2
            act.dma_start(x_sb[0:NREST, NFULL, :], g["x"][NFULL * P:N, :]).then_inc(S["x"], 16)
            act.dma_start(x_sb[:, 0:half, :], g["x"][0:half * P, :].rearrange("(t p) d -> p t d", p=P)).then_inc(S["x"], 16)
            act.dma_start(x_sb[:, half:NFULL, :],
                          g["x"][half * P:NFULL * P, :].rearrange("(t p) d -> p t d", p=P)).then_inc(S["x"], 16)
            act.wait_ge(S["x"], 48)
            for t in range(NT):
                if t >= 2:
                    act.wait_ge(S["sum"], t - 1)
                A.activation(scrap[:, t % 2, :], x_sb[:, t, :], ACT.Copy, accum_out=mean[:, t:t + 1]).then_inc(S["sum"], 1)
            act.wait_ge(S["sum"], NT)
            A.mul(mean[:, :], mean[:, :], -1.0 / D).then_inc(S["mean"], 1)
            act.wait_ge(S["mean"], 1)
            for t in range(NT):
                if t >= 2:
                    act.wait_ge(S["var"], t - 1)
                A.activation(scrap[:, t % 2, :], x_sb[:, t, :], ACT.Square, bias=mean[:, t:t + 1],
                             accum_out=var[:, t:t + 1]).then_inc(S["var"], 1)
            act.wait_ge(S["var"], NT)
            A.activation(var[:, :], var[:, :], ACT.Copy, bias=EPS, scale=1.0 / D).then_inc(S["mean"], 1)
            act.wait_ge(S["mean"], 2)
            A.activation(root[:, :], var[:, :], ACT.Sqrt).then_inc(S["sd"], 1)
            act.wait_ge(S["deg"], 1)
            A.activation(root[:, :], g["rs_out"][:, :], ACT.Sqrt).then_inc(S["sdeg"], 1)
            act.wait_ge(S["ab"], 1)
            for t in range(NT):
                if t % 3 == 2:
                    continue
                A.activation(table[:, t, :], x_sb[:, t, :], ACT.Identity, bias=shift[:, t:t + 1],
                             scale=scale[:, t:t + 1]).then_inc(S["ta"], 1)

        @b.tensor
        def _(pe):
            pe.wait_ge(S["ch"], 1)
            nc.tensor.matmul(ps_deg[:, 0:NT], zero[:, :], zero[:, 0:NT], start=True, stop=False,
                             skip_group_check=True).then_inc(S["used"], 2)

            def count(n, s):
                pe.wait_ge(S["oh"], n + 1)
                for t in range(HT):
                    last = nc.tensor.matmul(ps_deg[:, 0:NT], oh_lo[s][:, :, t], oh_hi[s][:, :, t],
                                            start=False, stop=False, skip_group_check=True)
                last.then_inc(S["used"], 1)
            with pe.Fori(0, NH // 2) as i:
                for s in range(2):
                    count(i * 2 + s, s)
            count(NH - 1, 0)
            pe.wait_ge(S["keys"], 1)
            nc.tensor.matmul(ps_win[:, 0:NG], ones[:, :], row_f[:, :], start=True, stop=True).then_inc(S["win"], 1)


def aggregate(g, layer):
    nc, agg, iota = g["nc"], g["agg"], g["iota"]
    table = g["table1"] if layer == 1 else g["table2"]
    rel, src_f, dst_i, dst_left = g["rel"], g["src_f"], g["dst_i"], g["dst_left"]
    hist = layer == 1
    with ExitStack() as c:
        def sb(name, shape, dt=F32):
            return c.enter_context(nc.sbuf_tensor(f"{name}_{layer}", shape, dt))
        sem_of = semaphores(nc, c)
        def sem(name):
            return sem_of(f"{name}_{layer}")
        idx = [sb(f"idx{s}", [P, GT], I32) for s in range(SETS)]
        msg = [sb(f"msg{s}", [P, GT, D]) for s in range(SETS)]
        oh = [sb(f"oh{s}", [P, GT, WIN]) for s in range(SETS)]
        if hist:
            oh_lo = [sb(f"ohlo{s}", [P, GT, P], BF16) for s in range(SETS)]
            oh_hi = [sb(f"ohhi{s}", [P, GT, NT], BF16) for s in range(SETS)]
        zero = sb("zero_a", [P, P], BF16)
        left_rel = sb("left_rel", [P, GT])
        ps = [c.enter_context(nc.psum_tensor(f"ps_agg{s}_{layer}", [P, 512], F32)) for s in range(SETS)]
        ps_deg = c.enter_context(nc.psum_tensor(f"ps_in_{layer}", [P, 512], F32))
        idx_ready = sem("idx_ready")
        gathered = [sem(f"gathered{s}") for s in range(SETS)]
        oh_ready = sem("oh_ready")
        summed = sem("summed")
        added = sem("added")
        zeroed = sem("zeroed")
        chain = sem("chain")
        l_idx, l_gath, l_oh, l_sum, l_add, l_ch = (sem(f"left_{n}") for n in ("idx", "gath", "oh", "sum", "add", "ch"))
        s_deg, s_sdeg = sem("s_deg"), sem("s_sdeg")
        sorting = layer == 2
        if sorting:
            ed = g["ed"]
            sorter = Sorter(nc, g["key"], g["odd"], lambda n: c.enter_context(nc.psum_tensor(n, [P, 512], F32)),
                            sem, g["ident"])
            far_max = sb("far_max_e", [P, 2])
            row_f = sb("row_fe", [1, FG])
            ones = sb("ones_e", [1, P])
            s_row, s_win, s_far, s_all, s_tail = sem("e_row"), sem("e_win"), sem("e_far"), sem("e_all"), sem("e_tail")
            PER_ITER = 4
            UNPACK = -(-(sorter.before(sorter.CHANGES - 1) + 1) // PER_ITER)
            assert UNPACK + 2 < NG // SETS
        b = c.enter_context(nc.Block())

        @b.scalar
        def _(act):
            with act.Fori(0, NG // SETS) as i:
                for s in range(SETS):
                    act.wait_ge(summed, i * SETS + s + 1)
                    nc.scalar.activation(idx[s][:, :], src_f[:, bass.ds(i * (SETS * GT) + s * GT, GT)],
                                         ACT.Copy).then_inc(idx_ready, 1)
            if hist:
                act.wait_ge(s_deg, 1)
                nc.scalar.activation(left_rel[:, 0:GT], zero[:, 0:GT], ACT.Sqrt)
                nc.scalar.activation(g["dst_hi"][:, 0:NT], g["rs_in"][:, :], ACT.Sqrt).then_inc(s_sdeg, 1)
            left = act.value_load(g["left_i"][0:1, 0:1], min_val=0, max_val=1)
            with act.If(left > 0):
                with act.Fori(0, NG) as k:
                    act.wait_ge(l_sum, k * NT + 1)
                    nc.scalar.activation(idx[0][:, :], src_f[:, bass.ds(k * GT, GT)], ACT.Copy).then_inc(l_idx, 1)
            act.sem_inc(l_ch, 1)

        @b.gpsimd
        def _(pool):
            def gathers(s, done):
                for t in range(GT):
                    nc.gpsimd.indirect_dma_start(msg[s][:, t, :], None, table,
                                                 bass.IndirectOffsetOnAxis(ap=idx[s][:, t:t + 1], axis=0)
                                                 ).then_inc(done, 16)
            with pool.Fori(0, NG // SETS) as i:
                for s in range(SETS):
                    pool.wait_ge(idx_ready, i * SETS + s + 1)
                    pool.nop(nofuse=True)
                    gathers(s, gathered[s])
            if sorting:
                pool.wait_ge(s_far, 1)
                nc.gpsimd.partition_all_reduce(far_max[:, 1:2], far_max[:, 0:1], P, RMAX).then_inc(s_all, 1)
            left = pool.value_load(g["left_i"][0:1, 0:1], min_val=0, max_val=1)
            with pool.If(left > 0):
                with pool.Fori(0, NG) as k:
                    pool.wait_ge(l_idx, k + 1)
                    pool.nop(nofuse=True)
                    gathers(0, l_gath)
            pool.sem_inc(l_ch, 1)

        @b.vector
        def _(dve):
            v = nc.vector
            v.memset(zero[:, :], 0.0).then_inc(zeroed, 1)
            v.memset(agg[:, :, :], 0.0).then_inc(chain, 1)

            def unpack(step):
                word = sorter.result[:, :].bitcast(I32).rearrange("q (r p) -> q p r", p=P)
                spare = g["key"][0] if sorter.result is g["key"][1] else g["key"][1]
                spare_i = spare[:, :].bitcast(I32)
                by_tile = lambda a: a.rearrange("q (p r) -> q p r", p=P)
                step(v.tensor_single_scalar(by_tile(ed["src_i"][:, :]), word, (1 << BITS) - 1, op=ALU.bitwise_and))
                step(v.tensor_scalar(by_tile(spare_i), word, BITS, (1 << BITS) - 1, ALU.arith_shift_right, ALU.bitwise_and))
                step(v.tensor_copy(ed["left"][:, :], spare_i))
                step(v.tensor_scalar(row_f[:, :], ed["left"][0:1, 0:FT:BT], float(N), None, ALU.min))
                step(v.tensor_copy(ed["win_i"][:, :], row_f[:, :]))
                step(v.memset(ones[:, :], 1.0))
                dve.sem_inc(s_row, 1)
                yield
                dve.wait_ge(s_win, 1)
                step(v.tensor_tensor(ed["rel"][:, :].rearrange("p (g t) -> p g t", t=BT),
                                     ed["left"][:, :].rearrange("p (g t) -> p g t", t=BT),
                                     ps_deg[:, 0:FG].unsqueeze(2).to_broadcast([P, FG, BT]), ALU.subtract))
                mark_left(v, step, ed["rel"][:, :], ed["left"][:, :], spare[:, :], sorter.result[:, :],
                          far_max[:, 0:1], FM * BT)
                dve.sem_inc(s_far, 1)
                yield
                dve.wait_ge(s_all, 1)
                step(v.tensor_copy(ed["left_i"][:, :], far_max[:, 1:2]))

            def onehots(k, s):
                for t in range(GT):
                    last = v.tensor_scalar(oh[s][:, t, :], iota[:, 0:WIN], rel[:, bass.ds(k * GT + t, 1)], None, ALU.is_equal)
                if hist:
                    for t in range(GT):
                        v.tensor_scalar(oh_lo[s][:, t, :], g["iota_bf"][:, :], g["dst_lo"][:, bass.ds(k * GT + t, 1)],
                                        None, ALU.is_equal)
                    last = v.tensor_tensor(oh_hi[s][:, :, :], iota[:, 0:NT].unsqueeze(1).to_broadcast([P, GT, NT]),
                                           g["dst_hi"][:, bass.ds(k * GT, GT)].unsqueeze(2).to_broadcast([P, GT, NT]),
                                           ALU.is_equal)
                last.then_inc(oh_ready, 1)

            def iteration(i):
                for s in range(SETS):
                    k = i * SETS + s
                    dve.wait_ge(summed, k + 2)
                    onehots(k + 1, (s + 1) % SETS)
                    dve.wait_ge(summed, k + SETS + 1)
                    dve.wait_ge(chain, k + 1)
                    w = dve.value_load(dst_i[0:1, bass.ds(k * GT, 1)], min_val=0, max_val=N - 1)
                    win = agg[:, :, bass.ds(w, WIN)]
                    v.tensor_tensor(win, win, ps[s][:, 0:D].rearrange("p (c n) -> p c n", c=DC),
                                    ALU.add).then_inc(chain, 1)

            onehots(0, 0)
            if not sorting:
                with dve.Fori(0, NG // SETS) as i:
                    iteration(i)
            else:
                steps = sorter.vector_steps(dve)
                for i in range(NG // SETS):
                    iteration(i)
                    if i < UNPACK:
                        for _ in range(PER_ITER):
                            next(steps, None)
                    elif i == UNPACK:
                        parts = unpack(Chain(dve, s_tail))
                        next(parts)
                    elif i == UNPACK + 2:
                        next(parts)
                next(parts, None)
            if hist:
                v.tensor_scalar(g["rs_in"][:, :], ps_deg[:, 0:NT], 1.0, None, ALU.max).then_inc(s_deg, 1)
                dve.wait_ge(s_sdeg, 1)
                v.reciprocal(g["rs_in"][:, :], g["dst_hi"][:, 0:NT]).then_inc(s_deg, 1)
            left = dve.value_load(g["left_i"][0:1, 0:1], min_val=0, max_val=1)
            with dve.If(left > 0):
                dve.wait_ge(chain, NG + 1)
                with dve.Fori(0, NG) as k:
                    with dve.Fori(0, NT) as t:
                        n = k * NT + t
                        dve.wait_ge(l_add, n + 1)
                        v.tensor_scalar(left_rel[:, :], dst_left[:, bass.ds(k * GT, GT)],
                                        g["tile_base"][:, bass.ds(t, 1)], None, ALU.subtract).then_inc(l_oh, 1)
                        dve.wait_ge(l_oh, n * 2 + 1)
                        for j in range(GT):
                            last = v.tensor_scalar(oh[0][:, j, :], iota[:, 0:P],
                                                   left_rel[:, j:j + 1], None, ALU.is_equal)
                        last.then_inc(l_oh, 1)
                        dve.wait_ge(l_sum, n + 2)
                        win = agg[:, :, bass.ds(t * P, P)]
                        v.tensor_tensor(win, win, ps[0][:, 0:D].rearrange("p (c n) -> p c n", c=DC),
                                        ALU.add).then_inc(l_add, 1)
            dve.sem_inc(l_ch, 1)

        @b.tensor
        def _(pe):
            t_ = nc.tensor
            pe.wait_ge(zeroed, 1)
            t_.matmul(ps_deg[:, 0:NT], zero[:, :], zero[:, 0:NT], start=True, stop=False,
                      skip_group_check=True).then_inc(summed, SETS)

            def sums(s):
                for h in range(DC):
                    for t in range(GT):
                        last = t_.matmul(ps[s][:, h * WIN:(h + 1) * WIN], msg[s][:, t, h * P:(h + 1) * P], oh[s][:, t, :],
                                         start=(t == 0), stop=(t == GT - 1), skip_group_check=True)
                return last

            def iteration(i):
                for s in range(SETS):
                    k = i * SETS + s
                    pe.wait_ge(oh_ready, k + 1)
                    if hist:
                        for t in range(GT):
                            t_.matmul(ps_deg[:, 0:NT], oh_lo[s][:, t, :], oh_hi[s][:, t, :], start=False, stop=False,
                                      skip_group_check=True)
                    pe.wait_ge(gathered[s], (i + 1) * (16 * GT))
                    sums(s).then_inc(summed, 1)

            if not sorting:
                with pe.Fori(0, NG // SETS) as i:
                    iteration(i)
            else:
                turn = 0
                for i in range(NG // SETS):
                    iteration(i)
                    while turn < sorter.CHANGES and sorter.before(turn) <= (i + 1) * PER_ITER - 1:
                        sorter.transposes(pe, turn)
                        turn += 1
                    if i == UNPACK + 1:
                        pe.wait_ge(s_row, 1)
                        t_.matmul(ps_deg[:, 0:FG], ones[:, :], row_f[:, :], start=True, stop=True,
                                  skip_group_check=True).then_inc(s_win, 1)
                assert turn == sorter.CHANGES
            left = pe.value_load(g["left_i"][0:1, 0:1], min_val=0, max_val=1)
            pe.sem_inc(l_sum, 1)
            pe.sem_inc(l_add, 1)
            with pe.If(left > 0):
                with pe.Fori(0, NG) as k:
                    pe.wait_ge(l_gath, (k + 1) * (16 * GT))
                    pe.nop(nofuse=True)
                    with pe.Fori(0, NT) as t:
                        pe.wait_ge(l_oh, (k * NT + t) * 2 + 2)
                        sums(0).then_inc(l_sum, 1)
            pe.sem_inc(l_ch, 1)


def transform(g):
    nc, agg, x_sb = g["nc"], g["agg"], g["x_sb"]
    w, bias = g["w"][0], g["b"][0]
    B = 4
    R = 14
    TS = 7
    assert NT % TS == 0 and R % TS == 0
    with ExitStack() as c:
        sem = semaphores(nc, c)
        lin = c.enter_context(nc.sbuf_tensor("lin", [P, B, D], F32))
        hid = c.enter_context(nc.sbuf_tensor("hid", [P, R, D], F32))
        ps = [c.enter_context(nc.psum_tensor(f"ps_lin{s}", [P, 512], F32)) for s in range(B)]
        t_mm, t_lin, t_hid, t_words = sem("t_mm"), sem("t_lin"), sem("t_hid"), sem("t_words")
        stored = [sem(f"t_st{s}") for s in range(R // TS)]
        b = c.enter_context(nc.Block())

        @b.tensor
        def _(pe):
            for t in range(NT):
                if t >= B:
                    pe.wait_ge(t_lin, t - B + 1)
                for h in range(DC):
                    last = nc.tensor.matmul(ps[t % B][:, 0:D], agg[:, h, t * P:(t + 1) * P], w[:, h, :],
                                            start=(h == 0), stop=(h == DC - 1))
                last.then_inc(t_mm, 1)

        def words(step):
            v = nc.vector
            esrc_i, edst_i = g["ed"]["src_i"][:, :], g["ed"]["rel"][:, :].bitcast(I32)
            step(v.tensor_scalar(esrc_i, esrc_i, float(N - 1), None, ALU.min))
            step(v.tensor_scalar(edst_i, edst_i, float((1 << BITS) - 1), None, ALU.min))
            step(v.tensor_scalar(edst_i, edst_i, BITS, WORD, ALU.logical_shift_left, ALU.bitwise_or))
            step(v.tensor_tensor(g["key"][0][:, :].bitcast(I32), edst_i, esrc_i, ALU.bitwise_or))

        @b.vector
        def _(dve):
            for t in range(NT):
                dve.wait_ge(t_mm, t + 1)
                if t >= B:
                    dve.wait_ge(t_hid, t - B + 1)
                nc.vector.scalar_tensor_tensor(lin[:, t % B, :], ps[t % B][:, 0:D], g["rs_in"][:, t:t + 1],
                                               bias[:, :], ALU.mult, ALU.add).then_inc(t_lin, 1)
                nc.vector.tensor_tensor(x_sb[:, t, :], x_sb[:, t, :], g["b"][1][:, :], ALU.add)
                if t == NT // 2:
                    words(Chain(dve, t_words))

        @b.scalar
        def _(act):
            for t in range(NT):
                act.wait_ge(t_lin, t + 1)
                if t >= R:
                    act.wait_ge(stored[t % R // TS], 16 * (t // R))
                nc.scalar.activation(hid[:, t % R, :], lin[:, t % B, :], ACT.Relu,
                                     scale=g["rs_out"][:, t:t + 1]).then_inc(t_hid, 1)

        @b.sync
        def _(sp):
            for k in range(NT // TS):
                s = k % (R // TS)
                sp.wait_ge(t_hid, (k + 1) * TS)
                sp.dma_start(g["table2"][k * TS * P:(k + 1) * TS * P, :].rearrange("(t p) d -> p t d", p=P),
                             hid[:, s * TS:(s + 1) * TS, :]).then_inc(stored[s], 16)
            for s in range(R // TS):
                sp.wait_ge(stored[s], 16 * len(range(s, NT // TS, R // TS)))


def finish_nodes(g, node, node_tab, dest_tab, yx_dram, w_gat, att_src, att_dst, expert, expert_in):
    nc, x_sb, xt, ident = g["nc"], g["x_sb"], g["agg"], g["ident"]
    w = g["w"][1]
    as_, ad, h = node["as_"], node["ad"], node["h"]
    B = 4
    TB = 7
    NB = NT // TB
    assert NB * TB == NT
    with ExitStack() as c:
        def sb(name, shape, dt=F32):
            return c.enter_context(nc.sbuf_tensor(name, shape, dt))
        sem = semaphores(nc, c)
        wg = sb("wg", [P, DC, HE])
        att = sb("att", [P, 2, HE])
        stats = sb("stats_g", [P, NT, 6])
        mv = sb("mv_g", [P, NT, 2])
        dev = sb("dev_g", [P, NT])
        root = sb("root_g", [P, NT])
        shift = sb("shift_g", [P, NT])
        xn = sb("xn_g", [P, 2 * TB, D])
        prod = sb("prod_g", [P, 2, TB, HE])
        row = sb("row_g", [P, NT, VAL])
        real = sb("real", [P, 2])
        top = node["top"]
        z = sb("z_g", [P, NT, HEADS])
        spare = sb("spare_g", [P, PIECES * 2 * HEADS], BF16)
        dest = sb("dest_g", [P, NT, PIECES, 2 * HEADS], BF16)
        rest = sb("rest_g", [P, NT, 2 * HEADS])
        spread = sb("spread_g", [P, HEADS + 1])
        ps_x = [c.enter_context(nc.psum_tensor(f"ps_x{s}", [P, 512], F32)) for s in range(B)]
        ps_t = [c.enter_context(nc.psum_tensor(f"ps_t{s}", [P, 512], F32)) for s in range(2)]
        ps_h = [c.enter_context(nc.psum_tensor(f"ps_h{s}", [P, 512], F32)) for s in range(2)]
        S = {n: sem("n_" + n) for n in
             ("w",
              "small",
              "ex",
              "mm",
              "x1",
              "x1st",
              "stats",
              "ch",
              "var",
              "root",
              "ab",
              "xn",
              "tr",
              "xt",
              "h",
              "hc",
              "row",
              "top", "all", "z", "e", "tab", "st", "real")}
        b = c.enter_context(nc.Block())

        @b.sync
        def _(sp):
            ew1, eb1, ew2, eb2 = expert_in
            sp.dma_start(wg[:, :, :], w_gat.rearrange("(c p) n -> p c n", p=P)).then_inc(S["w"], 16)
            sp.dma_start(att[:, 0, :], att_src.rearrange("h e -> (h e)").partition_broadcast(P)).then_inc(S["w"], 16)
            sp.dma_start(att[:, 1, :], att_dst.rearrange("h e -> (h e)").partition_broadcast(P)).then_inc(S["w"], 16)
            with nc.allow_non_contiguous_dma(reason="2048 biases, once"):
                sp.dma_start(expert["b1"][:, :], eb1.rearrange("e (c p) -> p (e c)", p=P)).then_inc(S["small"], 16)
            sp.dma_start(expert["b2"][:, :, :], eb2.partition_broadcast(P)).then_inc(S["small"], 16)
            for k in range(NB):
                t = (k + 1) * TB
                sp.wait_ge(S["x1"], t)
                sp.dma_start(yx_dram[k * TB:t, :, NE * D:(NE + 1) * D].rearrange("t p d -> p t d"),
                             x_sb[:, k * TB:t, :]).then_inc(S["x1st"], 16)
            sp.wait_ge(S["row"], 2 * NB)
            sp.dma_start(node_tab.rearrange("(t p) v -> p t v", p=P), row[:, :, :]).then_inc(S["st"], 16)
            sp.dma_start(dest_tab[NT * P:AGGC, :], spare[:, :]).then_inc(S["st"], 16)
            sp.wait_ge(S["tab"], 1)
            sp.dma_start(dest_tab[0:NT * P, :].rearrange("(t p) v -> p t v", p=P),
                         dest[:, :, :, :].rearrange("p t c h -> p t (c h)")).then_inc(S["st"], 16)
            sp.wait_ge(S["small"], 32)
            sp.wait_ge(S["x1st"], 16 * NB)
            sp.wait_ge(S["ex"], 16 * (NE + 1))
            sp.wait_ge(S["st"], 48)

        @b.gpsimd
        def _(pool):
            nc.gpsimd.memset(real[:, 0:1], 1.0).then_inc(S["real"], 1)
            pool.wait_ge(S["real"], 1)
            nc.gpsimd.affine_select(out=real[:, 0:1], in_=real[:, 0:1], compare_op=ALU.is_ge, fill=0.0,
                                    base=NREST - 1, pattern=[[0, 1]], channel_multiplier=-1).then_inc(S["real"], 1)
            ew1, _, ew2, _ = expert_in
            pool.wait_ge(S["mm"], NT)
            for e in range(NE):
                pool.dma_start(expert["w1"][:, :, e, :], ew1[e, :, :].rearrange("(c p) f -> p c f", p=P)).then_inc(S["ex"], 16)
            pool.dma_start(expert["w2"][:, :, :, :], ew2.rearrange("e (c p) d -> p e c d", p=P)).then_inc(S["ex"], 16)
            pool.wait_ge(S["top"], 1)
            nc.gpsimd.partition_all_reduce(top[:, 1, :, :].rearrange("p a h -> p (a h)"),
                                           top[:, 0, :, :].rearrange("p a h -> p (a h)"), P, RMAX).then_inc(S["all"], 1)

        @b.vector
        def _(dve):
            v = nc.vector
            step = Chain(dve, S["ch"])
            v.memset(spare[:, :], 0.0)

            def features(k):
                at = slice(k * TB, (k + 1) * TB)
                dve.wait_ge(S["h"], k + 1)
                step(v.tensor_copy(h[:, at, :], ps_h[k % 2][:, 0:TB * HE].rearrange("p (t v) -> p t v", t=TB)))
                dve.sem_inc(S["hc"], 1)
                for a in range(2):
                    last = v.tensor_tensor(prod[:, a, :, :], h[:, at, :], att[:, a, :].unsqueeze(1).to_broadcast([P, TB, HE]),
                                           ALU.mult)
                step(last)
                for a, o in ((0, as_[:, at, :]), (1, ad[:, at, 0, :])):
                    last = v.tensor_reduce(o, prod[:, a, :, :].rearrange("p t (h e) -> p t h e", h=HEADS), AX, ALU.add)
                step(last)
                v.tensor_copy(row[:, at, 0:HEADS], as_[:, at, :]).then_inc(S["row"], 1)
                v.tensor_copy(row[:, at, HEADS:VAL], h[:, at, :]).then_inc(S["row"], 1)

            dve.wait_ge(S["w"], 48)
            for k in range(NB):
                for t in range(k * TB, (k + 1) * TB + 2):
                    if t < (k + 1) * TB:
                        dve.wait_ge(S["mm"], t + 1)
                        v.scalar_tensor_tensor(x_sb[:, t, :], ps_x[t % B][:, 0:D], g["rs_in"][:, t:t + 1], x_sb[:, t, :],
                                               ALU.mult, ALU.add).then_inc(S["x1"], 1)
                    u = t - 1
                    if k * TB <= u < (k + 1) * TB:
                        dve.wait_ge(S["x1"], u + 1)
                        v.bn_stats(stats[:, u, :], x_sb[:, u, :]).then_inc(S["stats"], 1)
                    u = t - 2
                    if k * TB <= u:
                        dve.wait_ge(S["stats"], u + 1)
                        last = v.bn_aggr(mv[:, u, :], stats[:, u, :])
                step(last)
                at = slice(k * TB, (k + 1) * TB)
                step(v.tensor_scalar(dev[:, at], mv[:, at, 1], EPS, None, ALU.add))
                dve.sem_inc(S["var"], 1)
                if k >= 2:
                    features(k - 2)
                dve.wait_ge(S["root"], k + 1)
                step(v.reciprocal(dev[:, at], root[:, at]))
                step(v.scalar_tensor_tensor(shift[:, at], mv[:, at, 0], -1.0, dev[:, at], ALU.mult, ALU.mult))
                dve.sem_inc(S["ab"], 1)
            features(NB - 2)
            features(NB - 1)
            dve.wait_ge(S["real"], 2)
            v.tensor_copy(z[:, :, :], as_[:, :, :])
            step(v.tensor_scalar(real[:, 1:2], real[:, 0:1], 1.0, -NEG, ALU.subtract, ALU.mult))
            step(v.tensor_scalar(z[:, NT - 1, :], as_[:, NT - 1, :], real[:, 0:1], real[:, 1:2], ALU.mult, ALU.add))
            step(v.tensor_reduce(top[:, 0, 0, :], z[:, :, :].rearrange("p t h -> p h t"), AX, ALU.max))
            step(v.tensor_scalar(z[:, :, :], as_[:, :, :], -1.0, None, ALU.mult))
            step(v.tensor_scalar(z[:, NT - 1, :], z[:, NT - 1, :], real[:, 0:1], real[:, 1:2], ALU.mult, ALU.add))
            step(v.tensor_reduce(top[:, 0, 1, :], z[:, :, :].rearrange("p t h -> p h t"), AX, ALU.max))
            dve.sem_inc(S["top"], 1)
            dve.wait_ge(S["all"], 1)
            guard = ad[:, :, 1, :]
            step(v.tensor_tensor(guard, ad[:, :, 0, :], top[:, 1, 0, :].unsqueeze(1).to_broadcast([P, NT, HEADS]), ALU.add))
            step(v.scalar_tensor_tensor(guard, guard, 0.2, guard, ALU.mult, ALU.max))
            split(v, step, ad[:, :, :, :].rearrange("p t a h -> p t (a h)"), lambda i: dest[:, :, i, :], rest[:, :, :])
            dve.sem_inc(S["tab"], 1)
            step(v.tensor_tensor(z[:, :, :], as_[:, :, :], ad[:, :, 0, :], ALU.add))
            step(v.scalar_tensor_tensor(z[:, :, :], z[:, :, :], 0.2, z[:, :, :], ALU.mult, ALU.max))
            step(v.tensor_tensor(z[:, :, :], z[:, :, :], guard, ALU.subtract))
            dve.sem_inc(S["z"], 1)
            step(v.tensor_tensor(spread[:, 0:HEADS], top[:, 1, 0, :], top[:, 1, 1, :], ALU.add))
            step(v.tensor_reduce(spread[:, HEADS:HEADS + 1], spread[:, 0:HEADS], AX, ALU.max))
            step(v.tensor_scalar(spread[:, HEADS:HEADS + 1], spread[:, HEADS:HEADS + 1], WIDE, None, ALU.is_gt))
            step(v.tensor_copy(node["wide_i"][:, :], spread[:, HEADS:HEADS + 1]))

        @b.scalar
        def _(act):
            A = nc.scalar
            for k in range(NB + 1):
                if k >= 1:
                    for t in range((k - 1) * TB, k * TB):
                        act.wait_ge(S["tr"], t + 1)
                        A.activation(xt[:, :, t * P:(t + 1) * P],
                                     ps_t[t % 2][:, 0:D].rearrange("p (c n) -> p c n", c=DC), ACT.Copy).then_inc(S["xt"], 1)
                if k < NB:
                    at = slice(k * TB, (k + 1) * TB)
                    act.wait_ge(S["var"], k + 1)
                    A.activation(root[:, at], dev[:, at], ACT.Sqrt).then_inc(S["root"], 1)
                    act.wait_ge(S["ab"], k + 1)
                    for t in range(k * TB, (k + 1) * TB):
                        A.activation(xn[:, t % (2 * TB), :], x_sb[:, t, :], ACT.Identity, bias=shift[:, t:t + 1],
                                     scale=dev[:, t:t + 1]).then_inc(S["xn"], 1)
            act.wait_ge(S["z"], 1)
            A.activation(node["e_self"][:, :, :], z[:, :, :], ACT.Exp).then_inc(S["e"], 1)

        @b.tensor
        def _(pe):
            mm = nc.tensor.matmul

            def project(u):
                pe.wait_ge(S["xt"], u + 1)
                k, i = divmod(u, TB)
                if i == 0 and k >= 2:
                    pe.wait_ge(S["hc"], k - 1)
                for c_ in range(DC):
                    last = mm(ps_h[k % 2][:, i * HE:(i + 1) * HE], xt[:, c_, u * P:(u + 1) * P], wg[:, c_, :],
                              start=(c_ == 0), stop=(c_ == DC - 1), skip_group_check=True)
                if i == TB - 1:
                    last.then_inc(S["h"], 1)

            for k in range(NB + 1):
                if k < NB:
                    for t in range(k * TB, (k + 1) * TB):
                        if t >= B:
                            pe.wait_ge(S["x1"], t - B + 1)
                        for c_ in range(DC):
                            last = mm(ps_x[t % B][:, 0:D], g["agg"][:, c_, t * P:(t + 1) * P], w[:, c_, :],
                                      start=(c_ == 0), stop=(c_ == DC - 1))
                        last.then_inc(S["mm"], 1)
                if k == 1:
                    pe.wait_ge(S["w"], 48)
                if k >= 1:
                    for t in range((k - 1) * TB, k * TB):
                        pe.wait_ge(S["xn"], t + 1)
                        if t >= 2:
                            pe.wait_ge(S["xt"], t - 1)
                        for c_ in range(DC):
                            last = nc.tensor.transpose(ps_t[t % 2][:, c_ * P:(c_ + 1) * P],
                                                       xn[:, t % (2 * TB), c_ * P:(c_ + 1) * P], ident[:, :])
                        last.then_inc(S["tr"], 1)
                        if t > (k - 1) * TB:
                            project(t - 1)
                    project(k * TB - 1)


def own_guards(nc, node, ident, iota, tile_base, ed, node_tab, dest_tab):
    as_, ad, top = node["as_"], node["ad"], node["top"]
    with ExitStack() as c:
        def sb(name, shape, dt=F32):
            return c.enter_context(nc.sbuf_tensor(name, shape, dt))
        sem = semaphores(nc, c)
        idx = sb("g_idx", [P, BT], I32)
        rows = sb("g_rows", [P, BT, VAL])
        shift = sb("g_shift", [P, HEADS])
        term = sb("g_term", [P, BT, HEADS])
        rel = sb("g_rel", [P, BT])
        spot = sb("g_spot", [P, HEADS, BT, P])
        most = sb("g_most", [P, HEADS])
        maxima = sb("g_maxima", [HEADS, AGGC])
        z = sb("g_z", [P, NT, HEADS])
        dest = sb("g_dest", [P, NT, PIECES, 2 * HEADS], BF16)
        rest = sb("g_rest", [P, NT, 2 * HEADS])
        ps = [c.enter_context(nc.psum_tensor(f"ps_g{h}", [P, 512], F32)) for h in range(HEADS)]
        ps_m = c.enter_context(nc.psum_tensor("ps_gm", [P, 512], F32))
        g_ch, g_fin, g_z, g_e, g_st = (sem(n) for n in ("g_ch", "g_fin", "g_z", "g_e", "g_st"))
        loops = [{n: sem(f"g{i}_{n}") for n in
                  ("idx",
                   "gath",
                   "term",
                   "rel",
                   "spot",
                   "turn",
                   "most",
                   "back",
                   "max")}
                 for i in range(2)]
        b = c.enter_context(nc.Block())

        def cond(eng):
            return eng.If(eng.value_load(node["wide_i"][0:1, 0:1], min_val=0, max_val=1) > 0)

        def left(eng):
            return eng.If(eng.value_load(ed["left_i"][0:1, 0:1], min_val=0, max_val=1) > 0)

        @b.gpsimd
        def _(pool):
            def gather(k, L):
                pool.wait_ge(L["idx"], k + 1)
                pool.nop(nofuse=True)
                for t in range(BT):
                    nc.gpsimd.indirect_dma_start(rows[:, t, :], None, node_tab, bass.IndirectOffsetOnAxis(
                        ap=idx[:, t:t + 1], axis=0)).then_inc(L["gath"], 16)
            with cond(pool):
                with pool.Fori(0, FG) as k:
                    gather(k, loops[0])
                with left(pool):
                    with pool.Fori(0, FG) as k:
                        gather(k, loops[1])

        @b.scalar
        def _(act):
            def stage(k, L, n):
                act.wait_ge(L["max"], n + 1)
                nc.scalar.activation(idx[:, :], ed["src_i"][:, bass.ds(k * BT, BT)], ACT.Copy).then_inc(L["idx"], 1)
            with cond(act):
                with act.Fori(0, FG) as k:
                    stage(k, loops[0], k)
                with left(act):
                    with act.Fori(0, FG) as k:
                        stage(k, loops[1], k * NT)
                act.wait_ge(g_z, 1)
                nc.scalar.activation(node["e_self"][:, :, :], z[:, :, :], ACT.Exp).then_inc(g_e, 1)

        @b.vector
        def _(dve):
            v = nc.vector
            step = Chain(dve, g_ch)

            def terms(k, L):
                dve.wait_ge(L["gath"], (k + 1) * (16 * BT))
                v.tensor_tensor(term[:, :, :], rows[:, :, 0:HEADS], shift[:, :].unsqueeze(1).to_broadcast([P, BT, HEADS]),
                                ALU.add).then_inc(L["term"], 1)
                dve.wait_ge(L["term"], k + 1)

            def maximum(n, L, k, w):
                dve.wait_ge(L["rel"], n + 1)
                for h in range(HEADS):
                    for t in range(BT):
                        last = v.tensor_scalar(spot[:, h, t, :], iota[:, :], rel[:, t:t + 1], term[:, t, h:h + 1],
                                               ALU.is_equal, ALU.mult)
                last.then_inc(L["spot"], 1)
                dve.wait_ge(L["turn"], n + 1)
                for h in range(HEADS):
                    last = v.tensor_reduce(most[:, h:h + 1], ps[h][:, :], AX, ALU.max)
                last.then_inc(L["most"], 1)
                dve.wait_ge(L["back"], n + 1)
                to = maxima[:, bass.ds(w, WIN)]
                v.tensor_tensor(to, to, ps_m[0:HEADS, 0:P], ALU.max).then_inc(L["max"], 1)
                dve.wait_ge(L["max"], n + 2)

            with cond(dve):
                step(v.memset(maxima[:, :], 0.0))
                step(v.tensor_scalar(shift[:, :], top[:, 1, 1, :], 1.0, None, ALU.add))
                for L in loops:
                    dve.sem_inc(L["max"], 1)
                L = loops[0]
                with dve.Fori(0, FG) as k:
                    terms(k, L)
                    v.tensor_copy(rel[:, :], ed["rel"][:, bass.ds(k * BT, BT)]).then_inc(L["rel"], 1)
                    w = dve.value_load(ed["win_i"][0:1, bass.ds(k, 1)], min_val=0, max_val=N)
                    maximum(k, L, k, w)
                with left(dve):
                    L = loops[1]
                    with dve.Fori(0, FG) as k:
                        terms(k, L)
                        dve.nop(nofuse=True)
                        with dve.Fori(0, NT) as t:
                            v.tensor_scalar(rel[:, :], ed["left"][:, bass.ds(k * BT, BT)], tile_base[:, bass.ds(t, 1)],
                                            None, ALU.subtract).then_inc(L["rel"], 1)
                            maximum(k * NT + t, L, k, t * P)
                dve.sem_inc(g_fin, 1)
                dve.wait_ge(g_fin, 2)
                guard = ad[:, :, 1, :]
                step(v.tensor_tensor(guard, ps[0][:, 0:NT * HEADS].rearrange("p (t h) -> p t h", h=HEADS),
                                     shift[:, :].unsqueeze(1).to_broadcast([P, NT, HEADS]), ALU.subtract))
                step(v.tensor_tensor(guard, guard, as_[:, :, :], ALU.max))
                step(v.tensor_tensor(guard, guard, ad[:, :, 0, :], ALU.add))
                step(v.scalar_tensor_tensor(guard, guard, 0.2, guard, ALU.mult, ALU.max))
                step(v.tensor_tensor(z[:, :, :], as_[:, :, :], ad[:, :, 0, :], ALU.add))
                step(v.scalar_tensor_tensor(z[:, :, :], z[:, :, :], 0.2, z[:, :, :], ALU.mult, ALU.max))
                step(v.tensor_tensor(z[:, :, :], z[:, :, :], guard, ALU.subtract))
                split(v, step, ad[:, :, :, :].rearrange("p t a h -> p t (a h)"), lambda i: dest[:, :, i, :], rest[:, :, :])
                dve.sem_inc(g_z, 1)

        @b.tensor
        def _(pe):
            def maximum(n, L):
                pe.wait_ge(L["spot"], n + 1)
                for h in range(HEADS):
                    for t in range(BT):
                        last = nc.tensor.transpose(ps[h][:, t * P:(t + 1) * P], spot[:, h, t, :], ident[:, :])
                last.then_inc(L["turn"], 1)
                pe.wait_ge(L["most"], n + 1)
                nc.tensor.transpose(ps_m[0:HEADS, 0:P], most[:, :], ident[:, :]).then_inc(L["back"], 1)
            with cond(pe):
                with pe.Fori(0, FG) as k:
                    maximum(k, loops[0])
                with left(pe):
                    with pe.Fori(0, FG) as k:
                        with pe.Fori(0, NT) as t:
                            maximum(k * NT + t, loops[1])
                pe.wait_ge(g_fin, 1)
                for t in range(NT):
                    last = nc.tensor.transpose(ps[0][:, t * HEADS:(t + 1) * HEADS], maxima[:, t * P:(t + 1) * P],
                                               ident[0:HEADS, 0:HEADS])
                last.then_inc(g_fin, 1)

        @b.sync
        def _(sp):
            with cond(sp):
                sp.wait_ge(g_z, 1)
                sp.dma_start(dest_tab[0:NT * P, :].rearrange("(t p) v -> p t v", p=P),
                             dest[:, :, :, :].rearrange("p t c h -> p t (c h)")).then_inc(g_st, 16)
                sp.wait_ge(g_st, 16)


def gat_edges(nc, xt, node, ident, iota_bf, tile_base, ed, node_tab, dest_tab, yx_dram,
              b_gat, ln_gamma, ln_beta, expert, out):
    with ExitStack() as c:
        def sb(name, shape, dt=F32, ctx=c):
            return ctx.enter_context(nc.sbuf_tensor(name, shape, dt))
        def pb(name, ctx=c):
            return ctx.enter_context(nc.psum_tensor(name, [P, 512], F32))
        def sem(name, ctx=c):
            return ctx.enter_context(nc.semaphore(name))
        sums = sb("sums", [PIECES * VAL, AGGC])
        y_keep = sb("y_keep", [P, KEEP, NE * D])

        with ExitStack() as m:
            w1, w2, b1, b2 = (expert[n] for n in ("w1", "w2", "b1", "b2"))
            EP = 2
            W = PIECES * 2 * HEADS
            ident_bf = sb("ident_bf", [P, P], BF16, m)
            idx = [sb(f"eidx{s}", [P, TT], I32, m) for s in range(SETS)]
            nrow = [sb(f"nrow{s}", [P, TT, VAL], F32, m) for s in range(SETS)]
            win = [sb(f"ewin{s}", [P, ST, W], BF16, m) for s in range(SETS)]
            dest = sb("edest", [P, TT, 2 * HEADS], F32, m)
            oh = [sb(f"eoh{s}", [P, TT, WIN], BF16, m) for s in range(SETS)]
            oh_t = [sb(f"eoht{s}", [P, TT, P], BF16, m) for s in range(2)]
            z = [sb(f"ez{s}", [P, TT, HEADS], F32, m) for s in range(2)]
            val = [sb(f"val{s}", [P, TT, VAL], F32, m) for s in range(2)]
            rest = sb("erest", [P, TT, VAL], F32, m)
            piece = [sb(f"epiece{s}", [P, TT, PIECES, VAL], BF16, m) for s in range(2)]
            left_rel = sb("eleft_rel", [P, TT], F32, m)
            hid = [sb(f"ehid{s}", [P, FC, P], F32, m) for s in range(2)]
            y_sb = y_keep[:, KEEP - 1, :].rearrange("p (e d) -> p e d", e=NE)
            ps_t = m.enter_context(nc.psum_tensor("ps_et", [P, TT * P], BF16))
            ps_ad = pb("ps_ead", m)
            ps_sum = [pb(f"ps_es{s}", m) for s in range(2)]
            ps_h = [pb(f"ps_eh{s}", m) for s in range(2)]
            ps_y = [pb(f"ps_ey{s}", m) for s in range(2)]
            S = {n: sem("e_" + n, m) for n in
                 ("id",
                  "idx",
                  "oh",
                  "t",
                  "tcopy",
                  "ad",
                  "z",
                  "e",
                  "row",
                  "val",
                  "used",
                  "ev",
                  "zch", "vch",
                  "h",
                  "hh",
                  "ymm",
                  "y",
                  "yst",
                  "yfree")}
            gath = [sem(f"e_gath{s}", m) for s in range(SETS)]
            winl = [sem(f"e_winl{s}", m) for s in range(SETS)]
            L = {n: sem("l_" + n, m) for n in
                 ("idx", "gath", "win", "oh", "t", "tcopy", "ad", "z", "e", "row", "val", "sum", "ev", "zc", "vc", "half")}
            b = m.enter_context(nc.Block())

            @b.sync
            def _(sp):
                sp.sem_inc(S["yfree"], NE)
                with sp.Fori(0, NOUT) as i:
                    for e in range(NE):
                        n = i * NE + e
                        sp.wait_ge(S["y"], n + 3)
                        sp.dma_start(yx_dram[bass.ds(i, 1), :, e * D:(e + 1) * D].rearrange("a p d -> (a p) d"),
                                     y_sb[:, e, :]).then_inc(S["yst"], 16)
                        sp.wait_ge(S["yst"], (n + 1) * 16)
                        sp.sem_inc(S["yfree"], 1)
                left = sp.value_load(ed["left_i"][0:1, 0:1], min_val=0, max_val=1)
                with sp.If(left > 0):
                    with sp.Fori(0, FSTEPS) as k:
                        with sp.Fori(0, NT) as t:
                            sp.wait_ge(L["ev"], k * NT + t + 1)
                            for g in range(ST):
                                sp.dma_start(win[0][:, g, :], dest_tab[bass.ds(t * P, P), :]).then_inc(L["win"], 16)

            def gathers(s, done):
                for t in range(TT):
                    nc.gpsimd.indirect_dma_start(nrow[s][:, t, :], None, node_tab, bass.IndirectOffsetOnAxis(
                        ap=idx[s][:, t:t + 1], axis=0)).then_inc(done, 16)

            @b.gpsimd
            def _(pool):
                def body(i, steps):
                    for s in range(steps):
                        pool.wait_ge(S["idx"], i * SETS + s + 1)
                        pool.nop(nofuse=True)
                        gathers(s, gath[s])
                with pool.Fori(0, FI) as i:
                    body(i, SETS)
                body(FI, TAIL)
                left = pool.value_load(ed["left_i"][0:1, 0:1], min_val=0, max_val=1)
                with pool.If(left > 0):
                    with pool.Fori(0, FSTEPS) as k:
                        pool.wait_ge(L["idx"], k + 1)
                        pool.nop(nofuse=True)
                        gathers(0, L["gath"])

            @b.scalar
            def _(act):
                A = nc.scalar

                def stage(j, s, done):
                    A.activation(idx[s][:, :], ed["src_i"][:, bass.ds(j * TT, TT)], ACT.Copy).then_inc(done, 1)

                def windows(j, s):
                    for g in range(ST):
                        w = act.value_load(ed["win_i"][0:1, bass.ds(j * ST + g, 1)], min_val=0, max_val=N)
                        act.dma_start(win[s][:, g, :], dest_tab[bass.ds(w, WIN), :]).then_inc(winl[s], 16)

                def turned(j, s):
                    act.wait_ge(S["t"], j + 1)
                    act.wait_ge(S["ad"], j + SETS - 1)
                    A.activation(oh_t[s % 2][:, :, :].rearrange("p t e -> p (t e)"), ps_t[:, :],
                                 ACT.Copy).then_inc(S["tcopy"], 1)

                def weights(j, s):
                    act.wait_ge(S["z"], j + 2)
                    A.activation(val[s % 2][:, :, HE:VAL], z[s % 2][:, :, :], ACT.Exp).then_inc(S["e"], 1)

                def gelu(n, e):
                    act.wait_ge(S["h"], n + 1)
                    act.wait_ge(S["ymm"], n + 1)
                    for f in range(FC):
                        last = A.activation(hid[e % 2][:, f, :], ps_h[e % 2][:, f * P:(f + 1) * P], ACT.Gelu,
                                            bias=b1[:, e * FC + f:e * FC + f + 1])
                    last.then_inc(S["hh"], 1)

                def body(i, last=False):
                    for s in range(TAIL if last else SETS):
                        j = i * SETS + s
                        if not last or s + 3 < TAIL:
                            act.wait_ge(S["row"], j + 1)
                            act.wait_ge(S["ad"], j + SETS)
                            stage(j + 3, (s + 3) % SETS, S["idx"])
                            windows(j + 3, (s + 3) % SETS)
                        if not last or s < TAIL - 1:
                            for p in range(EP):
                                gelu(j * EP + p, (s * EP + p) % NE)
                        if not last or s + 2 < TAIL:
                            turned(j + 2, (s + 2) % SETS)
                        if not last or s + 1 < TAIL:
                            weights(j + 1, (s + 1) % SETS)

                for j in range(3):
                    stage(j, j, S["idx"])
                    windows(j, j)
                turned(0, 0)
                turned(1, 1)
                weights(0, 0)
                with act.Fori(0, FI) as i:
                    body(i)
                body(FI, last=True)

                left = act.value_load(ed["left_i"][0:1, 0:1], min_val=0, max_val=1)
                with act.If(left > 0):
                    with act.Fori(0, FSTEPS) as k:
                        act.wait_ge(L["ev"], k * NT + 1)
                        stage(k, 0, L["idx"])
                        with act.Fori(0, NT) as t:
                            act.wait_ge(L["t"], k * NT + t + 1)
                            A.activation(oh_t[0][:, :, :].rearrange("p t e -> p (t e)"), ps_t[:, :],
                                         ACT.Copy).then_inc(L["tcopy"], 1)
                            act.wait_ge(L["z"], k * NT + t + 1)
                            A.activation(val[0][:, :, HE:VAL], z[0][:, :, :], ACT.Exp).then_inc(L["e"], 1)

            @b.vector
            def _(dve):
                v = nc.vector
                dve.sem_inc(S["y"], 2)
                dve.sem_inc(S["row"], 1)
                dve.sem_inc(S["z"], 1)
                v.tensor_copy(ident_bf[:, :], ident[:, :]).then_inc(S["id"], 1)
                v.memset(sums[:, :], 0.0).then_inc(S["ev"], 2 * ST)

                def onehots(j, s):
                    dve.wait_ge(S["used"], j + 1)
                    for t in range(TT):
                        last = v.tensor_scalar(oh[s][:, t, :], iota_bf[:, :], ed["rel"][:, bass.ds(j * TT + t, 1)], None,
                                               ALU.is_equal)
                    last.then_inc(S["oh"], 1)

                def exponents(s, chain, n, done):
                    zz = z[s % 2][:, :, :]
                    c0 = n * 4
                    v.tensor_reduce(dest[:, :, :], ps_ad[:, 0:TT * W].rearrange("p (t c h) -> p t h c", t=TT, c=PIECES),
                                    AX, ALU.add).then_inc(chain, 1)
                    dve.wait_ge(chain, c0 + 1)
                    v.tensor_tensor(zz, nrow[s][:, :, 0:HEADS], dest[:, :, 0:HEADS], ALU.add).then_inc(chain, 1)
                    dve.wait_ge(chain, c0 + 2)
                    v.scalar_tensor_tensor(zz, zz, 0.2, zz, ALU.mult, ALU.max).then_inc(chain, 1)
                    dve.wait_ge(chain, c0 + 3)
                    v.tensor_tensor(zz, zz, dest[:, :, HEADS:2 * HEADS], ALU.subtract).then_inc(chain, 1)
                    dve.wait_ge(chain, c0 + 4)
                    v.tensor_scalar(zz, zz, CAP, None, ALU.min).then_inc(done, 1)

                def weighted(s, chain, n, row, done):
                    h = s % 2
                    v.tensor_tensor(val[h][:, :, 0:HE].rearrange("p t (h e) -> p t h e", h=HEADS),
                                    nrow[s][:, :, HEADS:VAL].rearrange("p t (h e) -> p t h e", h=HEADS),
                                    val[h][:, :, HE:VAL].unsqueeze(3).to_broadcast([P, TT, HEADS, NE]),
                                    ALU.mult).then_inc(row, 1)
                    dve.wait_ge(row, n + row0[row])
                    c0 = n * 3
                    v.tensor_copy(piece[h][:, :, 0, :], val[h][:, :, :]).then_inc(chain, 1)
                    dve.wait_ge(chain, c0 + 1)
                    v.tensor_tensor(rest[:, :, :], val[h][:, :, :], piece[h][:, :, 0, :], ALU.subtract).then_inc(chain, 1)
                    dve.wait_ge(chain, c0 + 2)
                    v.tensor_copy(piece[h][:, :, 1, :], rest[:, :, :]).then_inc(chain, 1)
                    dve.wait_ge(chain, c0 + 3)
                    v.tensor_tensor(piece[h][:, :, 2, :], rest[:, :, :], piece[h][:, :, 1, :], ALU.subtract).then_inc(done, 1)
                row0 = {S["row"]: 2, L["row"]: 1}

                def evacuate(j, s):
                    dve.wait_ge(S["used"], j + SETS + 1)
                    for g in range(ST):
                        k = j * ST + g
                        dve.wait_ge(S["ev"], k + 2 * ST)
                        w = dve.value_load(ed["win_i"][0:1, bass.ds(k, 1)], min_val=0, max_val=N)
                        to = sums[:, bass.ds(w, WIN)]
                        v.tensor_tensor(to, to, ps_sum[s % 2][0:PIECES * VAL, g * WIN:(g + 1) * WIN],
                                        ALU.add).then_inc(S["ev"], 1)

                def output(n, e, tile=None):
                    dve.wait_ge(S["ymm"], n + 3)
                    if tile is None:
                        dve.wait_ge(S["yfree"], n + 1)
                        to = y_sb[:, e, :]
                    else:
                        to = y_keep[:, bass.ds(tile - NOUT, 1), e * D:(e + 1) * D].rearrange("p a d -> p (a d)")
                    v.tensor_tensor(to, ps_y[e % 2][:, 0:D], b2[:, e, :], ALU.add).then_inc(S["y"], 1)

                def step_exponents(i, j, s):
                    dve.wait_ge(gath[s], (i + 1) * (16 * TT))
                    dve.wait_ge(S["ad"], j + SETS + 1)
                    exponents(s, S["zch"], j, S["z"])

                def body(i, first=False, last=False, keep=False):
                    for s in range(TAIL if last else SETS):
                        j = i * SETS + s
                        dve.wait_ge(S["e"], j + 1)
                        dve.wait_ge(S["used"], j + SETS - 1)
                        weighted(s, S["vch"], j, S["row"], S["val"])
                        if not last or s + 3 < TAIL:
                            onehots(j + 3, (s + 3) % SETS)
                        if not first or s > 0:
                            evacuate(j - 1, (s - 1) % SETS)
                        if not last or s + 1 < TAIL:
                            step_exponents(i if s + 1 < SETS else i + 1, j + 1, (s + 1) % SETS)
                        if (not first or s > 0) and (not last or s - 1 < TAIL - 1):
                            tile = i * (SETS * EP // NE) + (s - 1) * EP // NE
                            for p in range(EP):
                                output((j - 1) * EP + p, ((s - 1) * EP + p) % NE,
                                       tile if keep and s > 0 or keep == 2 else None)

                for j in range(3):
                    onehots(j, j)
                step_exponents(0, 0, 0)
                body(0, first=True)
                KI = NOUT // (SETS * EP // NE)
                with dve.Fori(1, KI) as i:
                    body(i)
                body(KI, keep=1)
                with dve.Fori(KI + 1, FI) as i:
                    body(i, keep=2)
                dve.wait_ge(S["yfree"], NOUT * NE + NE)
                body(FI, last=True, keep=2)
                evacuate(STEPS - 1, TAIL - 1)

                left = dve.value_load(ed["left_i"][0:1, 0:1], min_val=0, max_val=1)
                with dve.If(left > 0):
                    dve.wait_ge(S["ev"], FM + 2 * ST)
                    dve.sem_inc(L["ev"], 1)
                    with dve.Fori(0, FSTEPS) as k:
                        with dve.Fori(0, NT) as t:
                            n = k * NT + t
                            dve.wait_ge(L["ev"], n + 1)
                            v.tensor_scalar(left_rel[:, :], ed["left"][:, bass.ds(k * TT, TT)],
                                            tile_base[:, bass.ds(t, 1)], None, ALU.subtract).then_inc(L["oh"], 1)
                            dve.wait_ge(L["oh"], n * 2 + 1)
                            for x in range(TT):
                                last = v.tensor_scalar(oh[0][:, x, :], iota_bf[:, :], left_rel[:, x:x + 1], None, ALU.is_equal)
                            last.then_inc(L["oh"], 1)
                            dve.wait_ge(L["gath"], (k + 1) * (16 * TT))
                            dve.wait_ge(L["ad"], n + 1)
                            exponents(0, L["zc"], n, L["z"])
                            dve.wait_ge(L["e"], n + 1)
                            weighted(0, L["vc"], n, L["row"], L["val"])
                            dve.wait_ge(L["sum"], n + 1)
                            to = sums[:, bass.ds(t * P, P)]
                            for g in range(ST):
                                last = v.tensor_tensor(to, to, ps_sum[0][0:PIECES * VAL, g * WIN:(g + 1) * WIN], ALU.add)
                                if g < ST - 1:
                                    last.then_inc(L["half"], 1)
                                    dve.wait_ge(L["half"], n + 1)
                            last.then_inc(L["ev"], 1)

            @b.tensor
            def _(pe):
                mm = nc.tensor.matmul
                pe.sem_inc(S["used"], SETS)
                pe.sem_inc(S["ad"], SETS)
                pe.sem_inc(S["tcopy"], 1)
                pe.sem_inc(S["hh"], 2)
                pe.sem_inc(S["ymm"], 2)

                def turn(s, done):
                    for t in range(TT):
                        last = nc.tensor.transpose(ps_t[:, t * P:(t + 1) * P], oh[s][:, t, :], ident_bf[:, :])
                    last.then_inc(done, 1)

                def destinations(s, half, done):
                    for t in range(TT):
                        last = mm(ps_ad[:, t * W:(t + 1) * W], oh_t[half][:, t, :], win[s][:, t // BT, :],
                                  start=True, stop=True, skip_group_check=True)
                    last.then_inc(done, 1)

                def add_up(s, half, done):
                    for t in range(TT):
                        g = t // BT
                        last = mm(ps_sum[half][0:PIECES * VAL, g * WIN:(g + 1) * WIN],
                                  piece[half][:, t, :, :].rearrange("p c v -> p (c v)"), oh[s][:, t, :],
                                  start=(t % BT == 0), stop=(t % BT == BT - 1), skip_group_check=True)
                    last.then_inc(done, 1)

                def step_turn(j, s):
                    pe.wait_ge(S["oh"], j + 1)
                    pe.wait_ge(S["tcopy"], j + 1)
                    turn(s, S["t"])

                def step_destinations(i, j, s):
                    pe.wait_ge(S["tcopy"], j + 2)
                    pe.wait_ge(winl[s], (i + 1) * (16 * ST))
                    pe.wait_ge(S["z"], j + 1)
                    destinations(s, s % 2, S["ad"])

                def step_sums(j, s):
                    pe.wait_ge(S["val"], j + 1)
                    pe.wait_ge(S["ev"], j * ST + ST)
                    add_up(s, s % 2, S["used"])

                def up(tile, n, e):
                    pe.wait_ge(S["hh"], n + 1)
                    for f in range(FC):
                        for h in range(DC):
                            last = mm(ps_h[e % 2][:, f * P:(f + 1) * P], w1[:, h, e, f * P:(f + 1) * P],
                                      xt[:, h, bass.ds(tile * P, P)], start=(h == 0), stop=(h == DC - 1), skip_group_check=True)
                    last.then_inc(S["h"], 1)

                def down(n, e):
                    pe.wait_ge(S["hh"], n + 3)
                    pe.wait_ge(S["y"], n + 1)
                    for f in range(FC):
                        last = mm(ps_y[e % 2][:, 0:D], hid[e % 2][:, f, :], w2[:, e, f, :], start=(f == 0),
                                  stop=(f == FC - 1), skip_group_check=True)
                    last.then_inc(S["ymm"], 1)

                def body(i, first=False, last=False):
                    for s in range(TAIL if last else SETS):
                        j = i * SETS + s
                        for p in range(EP):
                            if not last or s < TAIL - 1:
                                up(i * (SETS * EP // NE) + s * EP // NE, j * EP + p, (s * EP + p) % NE)
                            if (not first or s > 0) and (not last or s - 1 < TAIL - 1):
                                down((j - 1) * EP + p, ((s - 1) * EP + p) % NE)
                        if not last or s + 2 < TAIL:
                            step_turn(j + 2, (s + 2) % SETS)
                        if not last or s + 1 < TAIL:
                            step_destinations(i if s + 1 < SETS else i + 1, j + 1, (s + 1) % SETS)
                        step_sums(j, s)

                pe.wait_ge(S["id"], 1)
                step_turn(0, 0)
                step_turn(1, 1)
                step_destinations(0, 0, 0)
                body(0, first=True)
                with pe.Fori(1, FI) as i:
                    body(i)
                body(FI, last=True)

                left = pe.value_load(ed["left_i"][0:1, 0:1], min_val=0, max_val=1)
                with pe.If(left > 0):
                    with pe.Fori(0, FSTEPS) as k:
                        with pe.Fori(0, NT) as t:
                            n = k * NT + t
                            pe.wait_ge(L["oh"], n * 2 + 2)
                            turn(0, L["t"])
                            pe.wait_ge(L["tcopy"], n + 1)
                            pe.wait_ge(L["win"], (n + 1) * (16 * ST))
                            destinations(0, 0, L["ad"])
                            pe.wait_ge(L["val"], n + 1)
                            add_up(0, 0, L["sum"])

        route(nc, c, sb, pb, sem, sums, xt, y_keep, expert["w1"], expert["w2"], node, ident, yx_dram, b_gat, ln_gamma, ln_beta, out)


def route(nc, c, sb, pb, sem, sums, xt, y_keep, w1, w2, node, ident, yx_dram, b_gat, ln_gamma, ln_beta, out):
    TG = 3
    F = 4
    Q = NOUT // TG
    NX = (NE + 1) * D
    S = sb("S", [P, NT, VAL])
    tmp = sb("r_tmp", [P, NT, HE])
    par = sb("r_par", [P, 3, HE])
    den = sb("r_den", [P, NT, HEADS])
    mean = sb("r_mean", [P, NT, 3])
    sc = sb("r_sc", [P, NT, NE])
    cnt = sb("r_cnt", [P, NT, NE])
    gt = sb("r_gt", [P, NT, NE, NE])
    gate = sb("r_gate", [P, NT, NE])
    x_keep = w1[:, :, :, :].rearrange("p c e f -> p (c e f)")[:, 0:KEEP * D].rearrange("p (a d) -> p a d", d=D)
    room = DC * AGGC // (TG * NX)
    assert room == F - 1 and Q * TG == NOUT and Q % F == 0 and KEEP == Q + 1
    xt_flat = xt[:, :, :].rearrange("p c n -> p (c n)")
    yx = [xt_flat[:, s * TG * NX:(s + 1) * TG * NX].rearrange("p (a d) -> p a d", d=NX) for s in range(room)]
    yx.append(w2[:, :, :, :].rearrange("p e c d -> p (e c d)")[:, 0:TG * NX].rearrange("p (a d) -> p a d", d=NX))
    PV = PIECES * VAL
    PB = 512 // PV
    ps = [pb(f"ps_r{i}") for i in range(-(-NT // PB))]
    r_par, r_ch, r_tr, r_act, r_actd = (sem(f"r_{n}") for n in ("parl", "ch", "tr", "act", "actd"))
    r_in = [sem(f"r_in{s}") for s in range(F)]
    r_out = [sem(f"r_out{s}") for s in range(F)]
    r_add = sem("r_add")
    r_xk, r_kmul, r_kadd, r_kout = sem("r_xk"), sem("r_kmul"), sem("r_kadd"), sem("r_kout")
    b = c.enter_context(nc.Block())

    def load(eng, i, s, first=False):
        q = i * F + s
        if not first:
            eng.wait_ge(r_out[s], i * 16)
        eng.dma_start(yx[s], yx_dram[bass.ds(q * TG, TG), :, :].rearrange("a p d -> p a d")).then_inc(r_in[s], 16)

    @b.sync
    def _(sp):
        for n, a in enumerate((b_gat, ln_gamma, ln_beta)):
            sp.dma_start(par[:, n, :], a.partition_broadcast(P)).then_inc(r_par, 16)
        sp.dma_start(x_keep[:, :, :], yx_dram[NOUT:NT, :, NE * D:(NE + 1) * D].rearrange("a p d -> p a d")).then_inc(r_xk, 16)
        for s in range(0, F, 2):
            load(sp, 0, s, first=True)
        with sp.Fori(1, Q // F) as i:
            for s in range(0, F, 2):
                load(sp, i, s)
        CUT = 9
        sp.wait_ge(r_kadd, (1 + CUT) * 3)
        sp.dma_start(out[NFULL * P:N, :], x_keep[0:NREST, KEEP - 1, :]).then_inc(r_kout, 16)
        sp.dma_start(out[NOUT * P:(NOUT + CUT) * P, :].rearrange("(a p) d -> p a d", p=P),
                     x_keep[:, 0:CUT, :]).then_inc(r_kout, 16)
        sp.wait_ge(r_kadd, KEEP * 3)
        sp.dma_start(out[(NOUT + CUT) * P:NFULL * P, :].rearrange("(a p) d -> p a d", p=P),
                     x_keep[:, CUT:NFULL - NOUT, :]).then_inc(r_kout, 16)
        sp.wait_ge(r_kout, 48)

    @b.gpsimd
    def _(pool):
        def add_kept(k, n):
            x = x_keep[:, bass.ds(k, 1), :].rearrange("p a d -> p (a d)")
            half = [y_keep[:, bass.ds(k, 1), h * 2 * D:(h + 1) * 2 * D].rearrange("p a d -> p (a d)") for h in range(2)]
            pool.wait_ge(r_kmul, (n + 1) * NE)
            nc.gpsimd.tensor_tensor(half[0], half[0], half[1], ALU.add).then_inc(r_kadd, 1)
            for e in range(2):
                pool.wait_ge(r_kadd, n * 3 + e + 1)
                y = y_keep[:, bass.ds(k, 1), e * D:(e + 1) * D].rearrange("p a d -> p (a d)")
                nc.gpsimd.tensor_tensor(x, x, y, ALU.add).then_inc(r_kadd, 1)

        def body(i, last=False):
            for s in range(F):
                add_kept(i * F + s, i * F + s + 1)
                if s % 2 and not last:
                    load(pool, i + 1, s)

        for s in range(1, F, 2):
            load(pool, 0, s, first=True)
        pool.wait_ge(r_xk, 16)
        add_kept(KEEP - 1, 0)
        with pool.Fori(0, Q // F - 1) as i:
            body(i)
        body(Q // F - 1, last=True)

    @b.scalar
    def _(act):
        act.wait_ge(r_act, 1)
        nc.scalar.activation(mean[:, :, 2], mean[:, :, 1], ACT.Sqrt).then_inc(r_actd, 1)
        act.wait_ge(r_act, 2)
        nc.scalar.activation(gate[:, :, :], sc[:, :, :], ACT.Exp).then_inc(r_actd, 1)


        def weigh_kept(k):
            for e in range(NE):
                y = y_keep[:, bass.ds(k, 1), e * D:(e + 1) * D].rearrange("p a d -> p (a d)")
                nc.scalar.activation(y, y, ACT.Copy, scale=gate[:, bass.ds(k + NOUT, 1), e]).then_inc(r_kmul, 1)

        act.wait_ge(r_act, 3)
        weigh_kept(KEEP - 1)
        with act.Fori(0, Q // F) as i:
            for s in range(F):
                q = i * F + s
                weigh_kept(q)
                act.wait_ge(r_add, (q + 1) * (NE * TG))
                act.dma_start(out[bass.ds(q * (TG * P), TG * P), :].rearrange("(a p) d -> p a d", p=P),
                              yx[s][:, :, NE * D:NX]).then_inc(r_out[s], 16)
        for s in range(F):
            act.wait_ge(r_out[s], Q // F * 16)

    @b.tensor
    def _(pe):
        for t in range(NT):
            last = nc.tensor.transpose(ps[t // PB][:, (t % PB) * PV:(t % PB + 1) * PV], sums[:, t * P:(t + 1) * P],
                                       ident[0:PV, 0:PV])
            if t % PB == PB - 1 or t == NT - 1:
                last.then_inc(r_tr, 1)

    @b.vector
    def _(dve):
        v = nc.vector
        step = Chain(dve, r_ch)
        step(v.memset(gt[:, :, :, :], 0.0))
        for i, bank in enumerate(ps):
            n = min(PB, NT - i * PB)
            dve.wait_ge(r_tr, i + 1)
            step(v.tensor_reduce(S[:, i * PB:i * PB + n, :],
                                 bank[:, 0:n * PV].rearrange("p (t c v) -> p t v c", c=PIECES, v=VAL), AX, ALU.add))
        dve.wait_ge(r_par, 48)
        e_self, h = node["e_self"], node["h"]
        bc = lambda a: a.unsqueeze(3).to_broadcast([P, NT, HEADS, NE])
        four = lambda a: a.rearrange("p t (h e) -> p t h e", h=HEADS)
        step(v.tensor_tensor(four(tmp[:, :, :]), four(h[:, :, :]), bc(e_self[:, :, :]), ALU.mult))
        step(v.tensor_tensor(tmp[:, :, :], tmp[:, :, :], S[:, 0:NT, 0:HE], ALU.add))
        step(v.scalar_tensor_tensor(den[:, :, :], e_self[:, :, :], 1e-16, S[:, 0:NT, HE:VAL], ALU.add, ALU.add))
        step(v.reciprocal(den[:, :, :], den[:, :, :]))
        step(v.tensor_tensor(four(tmp[:, :, :]), four(tmp[:, :, :]), bc(den[:, :, :]), ALU.mult))
        pbc = lambda n: par[:, n, :].unsqueeze(1).to_broadcast([P, NT, HE])
        step(v.tensor_tensor(tmp[:, :, :], tmp[:, :, :], pbc(0), ALU.add))
        mb = lambda n: mean[:, :, n].unsqueeze(2).to_broadcast([P, NT, HE])
        agg = S[:, 0:NT, 0:HE]
        step(v.tensor_reduce(mean[:, :, 0], tmp[:, :, :], AX, ALU.add))
        step(v.tensor_scalar(mean[:, :, 0], mean[:, :, 0], 1.0 / HE, None, ALU.mult))
        step(v.tensor_tensor(tmp[:, :, :], tmp[:, :, :], mb(0), ALU.subtract))
        step(v.tensor_tensor(agg, tmp[:, :, :], tmp[:, :, :], ALU.mult))
        step(v.tensor_reduce(mean[:, :, 1], agg, AX, ALU.add))
        step(v.tensor_scalar(mean[:, :, 1], mean[:, :, 1], 1.0 / HE, EPS, ALU.mult, ALU.add))
        dve.sem_inc(r_act, 1)
        dve.wait_ge(r_actd, 1)
        step(v.reciprocal(mean[:, :, 1], mean[:, :, 2]))
        step(v.tensor_tensor(tmp[:, :, :], tmp[:, :, :], mb(1), ALU.mult))
        step(v.tensor_tensor(tmp[:, :, :], tmp[:, :, :], pbc(1), ALU.mult))
        step(v.tensor_tensor(tmp[:, :, :], tmp[:, :, :], pbc(2), ALU.add))
        step(v.tensor_reduce(sc[:, :, :], tmp[:, :, :].rearrange("p t (h e) -> p t e h", h=HEADS), AX, ALU.add))
        step(v.tensor_scalar(sc[:, :, :], sc[:, :, :], 1.0 / HEADS, None, ALU.mult))
        for e in range(NE):
            for a, z, op in ((0, e, ALU.is_ge), (e + 1, NE, ALU.is_gt)):
                if a < z:
                    last = v.tensor_tensor(gt[:, :, e, a:z], sc[:, :, a:z],
                                           sc[:, :, e].unsqueeze(2).to_broadcast([P, NT, z - a]), op)
        step(last)
        step(v.tensor_reduce(cnt[:, :, :], gt[:, :, :, :], AX, ALU.add))
        step(v.tensor_scalar(cnt[:, :, :], cnt[:, :, :], 2.0, None, ALU.is_lt))
        step(v.tensor_reduce(mean[:, :, 0], sc[:, :, :], AX, ALU.max))
        step(v.tensor_tensor(sc[:, :, :], sc[:, :, :], mean[:, :, 0].unsqueeze(2).to_broadcast([P, NT, NE]), ALU.subtract))
        dve.sem_inc(r_act, 1)
        dve.wait_ge(r_actd, 2)
        step(v.tensor_tensor(gate[:, :, :], gate[:, :, :], cnt[:, :, :], ALU.mult))
        step(v.tensor_reduce(mean[:, :, 0], gate[:, :, :], AX, ALU.add))
        step(v.reciprocal(mean[:, :, 1], mean[:, :, 0]))
        step(v.tensor_tensor(gate[:, :, :], gate[:, :, :], mean[:, :, 1].unsqueeze(2).to_broadcast([P, NT, NE]), ALU.mult))

        dve.sem_inc(r_act, 1)

        with dve.Fori(0, Q // F) as i:
            for s in range(F):
                q = i * F + s
                dve.wait_ge(r_in[s], (i + 1) * 16)
                for e in range(NE):
                    for a in range(TG):
                        if e > 0:
                            dve.wait_ge(r_add, q * (NE * TG) + (e - 1) * TG + a + 1)
                        x = yx[s][:, a, NE * D:NX]
                        v.scalar_tensor_tensor(x, yx[s][:, a, e * D:(e + 1) * D], gate[:, bass.ds(q * TG + a, 1), e], x,
                                               ALU.mult, ALU.add).then_inc(r_add, 1)


_OUTS = [((N, D), "float32")]


def kernel(**inputs):
    import numpy as _np
    import concourse.bacc as _bacc
    from concourse import mybir as _mybir
    from concourse.bass_utils import run_bass_kernel_spmd as _run

    a = {k: _np.asarray(v) for k, v in inputs.items()}
    cut = EFULL * P
    edge = a["L0_ffn_edge_index"]

    def by_tile(e):
        return _np.ascontiguousarray(e[:cut].reshape(EFULL, P).T), e[cut:].reshape(EREST, 1)

    src, src_rest = by_tile(a["src"])
    dst, dst_rest = by_tile(a["dst"])
    arrays = dict(
        x=a["x"], src=src, src_rest=src_rest, dst=dst, dst_rest=dst_rest,
        w1=a["L0_gnn_W1"], b1=a["L0_gnn_b1"], w2=a["L0_gnn_W2"], b2=a["L0_gnn_b2"],
        w_gat=a["L0_ffn_W_gat"], att_src=a["L0_ffn_att_src"], att_dst=a["L0_ffn_att_dst"],
        b_gat=a["L0_ffn_b_gat"], ln_gamma=a["L0_ffn_ln_gamma"], ln_beta=a["L0_ffn_ln_beta"],
        ew1=a["L0_ffn_W1"], eb1=a["L0_ffn_b1"], ew2=a["L0_ffn_W2"], eb2=a["L0_ffn_b2"],
        esrc=edge[0].reshape(P, FT), edst=edge[1].reshape(P, FT),
    )
    nc = _bacc.Bacc("TRN2", target_bir_lowering=False, num_devices=1)
    ins, args = {}, []
    for name, v in arrays.items():
        v = _np.ascontiguousarray(v)
        ins[f"in_{name}"] = v
        args.append(nc.dram_tensor(f"in_{name}", v.shape, _mybir.dt.from_np(v.dtype), kind="ExternalInput").ap())
    for i, (shape, dtype) in enumerate(_OUTS):
        args.append(nc.dram_tensor(f"out_{i}", shape, _mybir.dt.from_np(_np.dtype(dtype)), kind="ExternalOutput").ap())
    program(nc, *args)
    r = _run(nc, [ins], core_ids=[0])
    return r.results[0]["out_0"]
```
